# Optimizing a Trainium2 kernel written in Bass

```python
import numpy as np
import jax
import jax.numpy as jnp

def _softmax(x, axis=-1):
    return jax.nn.softmax(x, axis=axis)

def _gelu(x):
    return jax.nn.gelu(x, approximate=True)

def _silu(x):
    return jax.nn.silu(x)

def _sigmoid(x):
    return jax.nn.sigmoid(x)

def _layernorm(x, axis=-1, eps=1e-05):
    m = jnp.mean(x, axis=axis, keepdims=True)
    v = jnp.var(x, axis=axis, keepdims=True)
    return (x - m) / jnp.sqrt(v + eps)

def _scatter_add(tgt, idx, src, axis=0):
    return tgt.at[idx].add(src)

def _segment_sum(src, seg, n):
    return jax.ops.segment_sum(src, seg, n)
kernel_name = 'mk_hybrid_d1_jaxref_r8_3fdbf3'

def setup_inputs(seed: int=0):
    np.random.seed(seed)
    _w = jnp.asarray

    def _L0_attn_a_setup():
        import jax, jax.numpy as jnp
        import numpy as np
        D_MODEL = 256
        NHEAD = 16
        DH = D_MODEL // NHEAD
        HID = int(D_MODEL * 4.0 * (2.0 / 3.0))
        EPS = 1e-05

        def _layernorm(x, w, b):
            mu = jnp.mean(x, axis=-1, keepdims=True)
            var = jnp.var(x, axis=-1, keepdims=True)
            return (x - mu) * jax.lax.rsqrt(var + EPS) * w + b

        def _decay_mask(seq_len, nhead, dtype):
            gamma = 1.0 - jnp.exp2(-5.0 - jnp.arange(nhead, dtype=jnp.float32))
            n = jnp.arange(seq_len)
            diff = n[:, None] - n[None, :]
            mask = diff >= 0
            D = jnp.where(mask[None], gamma[:, None, None] ** jnp.maximum(diff, 0)[None].astype(jnp.float32), 0.0)
            return D.astype(dtype)
        key = jax.random.key(seed)
        ks = jax.random.split(key, 13)
        s = lambda k, sh, fan: jax.random.normal(k, sh, jnp.float32) * fan ** (-0.5)
        return {'x': jax.random.normal(ks[0], (2, 256, D_MODEL), jnp.float32), 'norm1_w': jnp.ones((D_MODEL,), jnp.float32), 'norm1_b': jnp.zeros((D_MODEL,), jnp.float32), 'wq': s(ks[1], (D_MODEL, D_MODEL), D_MODEL), 'wk': s(ks[2], (D_MODEL, D_MODEL), D_MODEL), 'wv': s(ks[3], (D_MODEL, D_MODEL), D_MODEL), 'wg': s(ks[4], (D_MODEL, D_MODEL), D_MODEL), 'wo': s(ks[5], (D_MODEL, D_MODEL), D_MODEL), 'norm2_w': jnp.ones((D_MODEL,), jnp.float32), 'norm2_b': jnp.zeros((D_MODEL,), jnp.float32), 'w1': s(ks[6], (D_MODEL, HID), D_MODEL), 'w2': s(ks[7], (D_MODEL, HID), D_MODEL), 'w3': s(ks[8], (HID, D_MODEL), HID)}
    _L0_attn_a_in = _L0_attn_a_setup()

    def _L0_attn_b_setup():
        import jax, jax.numpy as jnp
        import numpy as np
        D_INNER, D_STATE, DT_RANK = (256, 16, 128)
        BATCH, SEQ = (2, 256)

        def _selective_scan(u, delta, A, B, C, D):
            dA = jnp.exp(delta[..., None] * A[None, None])
            dBu = (delta * u)[..., None] * B[:, :, None, :]

            def step(h, inp):
                dA_t, dBu_t, C_t = inp
                h = dA_t * h + dBu_t
                y_t = jnp.einsum('bdn,bn->bd', h, C_t)
                return (h, y_t)
            h0 = jnp.zeros((u.shape[0], u.shape[2], A.shape[1]), dtype=u.dtype)
            xs = (jnp.moveaxis(dA, 1, 0), jnp.moveaxis(dBu, 1, 0), jnp.moveaxis(C, 1, 0))
            _, ys = jax.lax.scan(step, h0, xs)
            y = jnp.moveaxis(ys, 0, 1)
            return y + u * D[None, None, :]
        key = jax.random.key(seed)
        ks = jax.random.split(key, 6)
        x = jax.random.normal(ks[0], (BATCH, SEQ, D_INNER), dtype=jnp.float32)
        A_log = jax.random.uniform(ks[1], (D_INNER, D_STATE), minval=-4.0, maxval=-1.0, dtype=jnp.float32)
        D = jnp.ones((D_INNER,), dtype=jnp.float32)
        x_proj_w = jax.random.normal(ks[2], (DT_RANK + 2 * D_STATE, D_INNER), dtype=jnp.float32) / np.sqrt(D_INNER)
        dt_proj_w = jax.random.normal(ks[3], (D_INNER, DT_RANK), dtype=jnp.float32) / np.sqrt(DT_RANK)
        dt_std = DT_RANK ** (-0.5)
        dt_proj_b = jax.random.uniform(ks[4], (D_INNER,), minval=-dt_std, maxval=dt_std, dtype=jnp.float32)
        return {'x': x, 'A_log': A_log, 'D': D, 'x_proj_w': x_proj_w, 'dt_proj_w': dt_proj_w, 'dt_proj_b': dt_proj_b}
    _L0_attn_b_in = _L0_attn_b_setup()

    def _L0_ffn_setup():
        import jax, jax.numpy as jnp
        import numpy as np
        DIM = 256
        HID = 704
        ZERO_POINT = 128.0

        def _qlinear(x, wq, scale):
            W = (wq.astype(jnp.float32) - ZERO_POINT) * scale[:, None]
            return jnp.einsum('bsd,hd->bsh', x, W)
        key = jax.random.key(seed)
        ks = jax.random.split(key, 7)
        B, S = (4, 256)
        sg = jax.random.uniform(ks[1], (HID,)) * (0.02 / np.sqrt(DIM)) + 0.0001
        su = jax.random.uniform(ks[3], (HID,)) * (0.02 / np.sqrt(DIM)) + 0.0001
        sd = jax.random.uniform(ks[5], (DIM,)) * (0.02 / np.sqrt(HID)) + 0.0001
        return {'x': jax.random.normal(ks[0], (B, S, DIM), dtype=jnp.float32), 'wq_gate': jax.random.randint(ks[2], (HID, DIM), 0, 32, dtype=jnp.int32), 's_gate': sg, 'wq_up': jax.random.randint(ks[4], (HID, DIM), 0, 32, dtype=jnp.int32), 's_up': su, 'wq_down': jax.random.randint(ks[6], (DIM, HID), 0, 32, dtype=jnp.int32), 's_down': sd}
    _L0_ffn_in = _L0_ffn_setup()
    _d = {'L0_attn_a_x': _L0_attn_a_in['x'], 'L0_attn_a_norm1_w': _L0_attn_a_in['norm1_w'], 'L0_attn_a_norm1_b': _L0_attn_a_in['norm1_b'], 'L0_attn_a_wq': _L0_attn_a_in['wq'], 'L0_attn_a_wk': _L0_attn_a_in['wk'], 'L0_attn_a_wv': _L0_attn_a_in['wv'], 'L0_attn_a_wg': _L0_attn_a_in['wg'], 'L0_attn_a_wo': _L0_attn_a_in['wo'], 'L0_attn_a_norm2_w': _L0_attn_a_in['norm2_w'], 'L0_attn_a_norm2_b': _L0_attn_a_in['norm2_b'], 'L0_attn_a_w1': _L0_attn_a_in['w1'], 'L0_attn_a_w2': _L0_attn_a_in['w2'], 'L0_attn_a_w3': _L0_attn_a_in['w3'], 'L0_attn_b_A_log': _L0_attn_b_in['A_log'], 'L0_attn_b_D': _L0_attn_b_in['D'], 'L0_attn_b_x_proj_w': _L0_attn_b_in['x_proj_w'], 'L0_attn_b_dt_proj_w': _L0_attn_b_in['dt_proj_w'], 'L0_attn_b_dt_proj_b': _L0_attn_b_in['dt_proj_b'], 'L0_ffn_wq_gate': _L0_ffn_in['wq_gate'], 'L0_ffn_s_gate': _L0_ffn_in['s_gate'], 'L0_ffn_wq_up': _L0_ffn_in['wq_up'], 'L0_ffn_s_up': _L0_ffn_in['s_up'], 'L0_ffn_wq_down': _L0_ffn_in['wq_down'], 'L0_ffn_s_down': _L0_ffn_in['s_down']}
    _x0 = _d['L0_attn_a_x']
    _d['L0_attn_a_x'] = jax.random.normal(jax.random.fold_in(jax.random.key(seed), 1), (1, 2048, 256), dtype=_x0.dtype)
    del _x0
    return _d

def reference(L0_attn_a_x, L0_attn_a_norm1_w, L0_attn_a_norm1_b, L0_attn_a_wq, L0_attn_a_wk, L0_attn_a_wv, L0_attn_a_wg, L0_attn_a_wo, L0_attn_a_norm2_w, L0_attn_a_norm2_b, L0_attn_a_w1, L0_attn_a_w2, L0_attn_a_w3, L0_attn_b_A_log, L0_attn_b_D, L0_attn_b_x_proj_w, L0_attn_b_dt_proj_w, L0_attn_b_dt_proj_b, L0_ffn_wq_gate, L0_ffn_s_gate, L0_ffn_wq_up, L0_ffn_s_up, L0_ffn_wq_down, L0_ffn_s_down):

    def _L0_attn_a_ref(x, norm1_w, norm1_b, wq, wk, wv, wg, wo, norm2_w, norm2_b, w1, w2, w3):
        import jax, jax.numpy as jnp
        import numpy as np
        D_MODEL = 256
        NHEAD = 16
        DH = D_MODEL // NHEAD
        HID = int(D_MODEL * 4.0 * (2.0 / 3.0))
        EPS = 1e-05

        def _layernorm(x, w, b):
            mu = jnp.mean(x, axis=-1, keepdims=True)
            var = jnp.var(x, axis=-1, keepdims=True)
            return (x - mu) * jax.lax.rsqrt(var + EPS) * w + b

        def _decay_mask(seq_len, nhead, dtype):
            gamma = 1.0 - jnp.exp2(-5.0 - jnp.arange(nhead, dtype=jnp.float32))
            n = jnp.arange(seq_len)
            diff = n[:, None] - n[None, :]
            mask = diff >= 0
            D = jnp.where(mask[None], gamma[:, None, None] ** jnp.maximum(diff, 0)[None].astype(jnp.float32), 0.0)
            return D.astype(dtype)
        B, S, D = x.shape
        h = _layernorm(x, norm1_w, norm1_b)

        def split(t):
            return t.reshape(B, S, NHEAD, DH).transpose(0, 2, 1, 3)
        q = split(h @ wq)
        k = split(h @ wk) * DH ** (-0.5)
        v = split(h @ wv)
        Dm = _decay_mask(S, NHEAD, x.dtype)
        scores = jnp.einsum('bhsd,bhtd->bhst', q, k) * Dm[None]
        ret = jnp.einsum('bhst,bhtd->bhsd', scores, v)
        mu = jnp.mean(ret, axis=-1, keepdims=True)
        var = jnp.var(ret, axis=-1, keepdims=True)
        ret = (ret - mu) * jax.lax.rsqrt(var + EPS)
        ret = ret.transpose(0, 2, 1, 3).reshape(B, S, D)
        y = jax.nn.silu(h @ wg) * ret @ wo
        x = x + y
        h2 = _layernorm(x, norm2_w, norm2_b)
        ffn = jax.nn.silu(h2 @ w1) * (h2 @ w2) @ w3
        return x + ffn

    def _L0_attn_b_ref(x, A_log, D, x_proj_w, dt_proj_w, dt_proj_b):
        import jax, jax.numpy as jnp
        import numpy as np
        D_INNER, D_STATE, DT_RANK = (256, 16, 128)
        BATCH, SEQ = (2, 256)

        def _selective_scan(u, delta, A, B, C, D):
            dA = jnp.exp(delta[..., None] * A[None, None])
            dBu = (delta * u)[..., None] * B[:, :, None, :]

            def step(h, inp):
                dA_t, dBu_t, C_t = inp
                h = dA_t * h + dBu_t
                y_t = jnp.einsum('bdn,bn->bd', h, C_t)
                return (h, y_t)
            h0 = jnp.zeros((u.shape[0], u.shape[2], A.shape[1]), dtype=u.dtype)
            xs = (jnp.moveaxis(dA, 1, 0), jnp.moveaxis(dBu, 1, 0), jnp.moveaxis(C, 1, 0))
            _, ys = jax.lax.scan(step, h0, xs)
            y = jnp.moveaxis(ys, 0, 1)
            return y + u * D[None, None, :]
        x_dbl = jnp.einsum('bld,ed->ble', x, x_proj_w)
        delta_r = x_dbl[..., :DT_RANK]
        B = x_dbl[..., DT_RANK:DT_RANK + D_STATE]
        C = x_dbl[..., DT_RANK + D_STATE:]
        delta = jnp.einsum('blr,dr->bld', delta_r, dt_proj_w) + dt_proj_b
        delta = jax.nn.softplus(delta)
        A = -jnp.exp(A_log)
        return _selective_scan(x, delta, A, B, C, D)

    def _L0_ffn_ref(x, wq_gate, s_gate, wq_up, s_up, wq_down, s_down):
        import jax, jax.numpy as jnp
        import numpy as np
        DIM = 256
        HID = 704
        ZERO_POINT = 128.0

        def _qlinear(x, wq, scale):
            W = (wq.astype(jnp.float32) - ZERO_POINT) * scale[:, None]
            return jnp.einsum('bsd,hd->bsh', x, W)
        gate = _qlinear(x, wq_gate, s_gate)
        gate = jax.nn.silu(gate)
        up = _qlinear(x, wq_up, s_up)
        return _qlinear(gate * up, wq_down, s_down)
    x = L0_attn_a_x
    x = x + _L0_attn_a_ref(_layernorm(x, axis=-1), L0_attn_a_norm1_w, L0_attn_a_norm1_b, L0_attn_a_wq, L0_attn_a_wk, L0_attn_a_wv, L0_attn_a_wg, L0_attn_a_wo, L0_attn_a_norm2_w, L0_attn_a_norm2_b, L0_attn_a_w1, L0_attn_a_w2, L0_attn_a_w3)
    x = x + _L0_ffn_ref(_layernorm(x, axis=-1), L0_ffn_wq_gate, L0_ffn_s_gate, L0_ffn_wq_up, L0_ffn_s_up, L0_ffn_wq_down, L0_ffn_s_down)
    x = x + _L0_attn_b_ref(_layernorm(x, axis=-1), L0_attn_b_A_log, L0_attn_b_D, L0_attn_b_x_proj_w, L0_attn_b_dt_proj_w, L0_attn_b_dt_proj_b)
    x = x + _L0_ffn_ref(_layernorm(x, axis=-1), L0_ffn_wq_gate, L0_ffn_s_gate, L0_ffn_wq_up, L0_ffn_s_up, L0_ffn_wq_down, L0_ffn_s_down)
    return x

_drawn_inputs = setup_inputs


def setup_inputs(seed=0):
    import zlib

    import numpy as np

    out = dict(_drawn_inputs(seed))
    spreads = {'L0_attn_a_norm1_w': (1.0, 0.2),
     'L0_attn_a_norm1_b': (0.0, 0.1),
     'L0_attn_a_norm2_w': (1.0, 0.2),
     'L0_attn_a_norm2_b': (0.0, 0.1),
     'L0_attn_b_D': (1.0, 0.6)}
    factors = {'L0_attn_b_dt_proj_b': 8.779,
     'L0_ffn_s_gate': 8.0,
     'L0_ffn_s_up': 8.0,
     'L0_ffn_s_down': 8.0}
    for name, (base, spread) in spreads.items():
        noise = np.random.default_rng([zlib.crc32(name.encode()), seed]).standard_normal(out[name].shape)
        drawn = base * np.exp(spread * noise) if base else spread * noise
        out[name] = jnp.asarray(drawn.astype(out[name].dtype))
    for name, factor in factors.items():
        out[name] = (out[name] * factor).astype(out[name].dtype)
    return out
```

```python
from contextlib import ExitStack

import numpy as np

from concourse import mybir

F32 = mybir.dt.float32
F32R = mybir.dt.float32r
BF16 = mybir.dt.bfloat16
I32 = mybir.dt.int32
ALU = mybir.AluOpType
ACT = mybir.ActivationFunctionType
AX_X = mybir.AxisListType.X

P = 128
S = 2048
D = 256
FT = D // P
T = 512
TT = T // P
CHUNKS = S // T
HEADS = 16
DH = D // HEADS
HID_A = 682
HID_Q = 704
HT = 6
HP = HT * P
NS = 16
DTR = 128
EPS = 1e-5
ZERO_POINT = 128.0

COLS = dict(n1w=(0, 2), n1b=(2, 4), n2w=(4, 6), n2b=(6, 8), dskip=(8, 10), dtb=(10, 12),
            sgate=(12, 18), sup=(18, 24), alog=(24, 56))
NCOLS = 56
CONSTS = dict(decay=(0, 2048), ident=(2048, 2176), qdecay=(2176, 2432), kdecay=(2432, 2688),
              headmask=(2688, 2816), even=(2816, 2817), odd=(2817, 2818), chunkdecay=(2818, 2820),
              select=(2820, 2852), half=(2852, 2856))
NCONST = 2856


def shape_constants():
    c = np.zeros((P, NCONST), np.float64)
    gamma = (np.float32(1.0) - np.exp2(np.float32(-5.0) - np.arange(HEADS, dtype=np.float32))).astype(np.float64)
    t = np.arange(P)[:, None]
    s = np.arange(P)[None, :]
    for h in range(HEADS):
        c[:, h * P:(h + 1) * P] = np.where(s >= t, gamma[h] ** np.maximum(s - t, 0), 0.0)

    def put(name, a):
        lo, hi = CONSTS[name]
        c[:, lo:hi] = a

    row_head = np.arange(P) // DH
    put("ident", np.eye(P))
    put("qdecay", np.concatenate([gamma[row_head + 8 * f][:, None] ** (s + 1) for f in range(FT)], axis=1))
    put("kdecay", DH ** -0.5 * gamma[np.arange(D) // DH][None, :] ** (P - 1 - t))
    put("headmask", (row_head[:, None] == row_head[None, :]))
    put("even", (DH ** -0.5 * (row_head % 2 == 0))[:, None])
    put("odd", (DH ** -0.5 * (row_head % 2 == 1))[:, None])
    put("chunkdecay", np.stack([gamma[row_head + 8 * f] ** P for f in range(FT)], axis=1))
    put("select", (np.arange(P)[:, None] % 32 == np.arange(32)[None, :]) * (np.arange(P)[:, None] < 96))
    put("half", -0.5)
    return c.astype(np.float32)


class Norm:

    def __init__(self, name, sem, src, src_ready, nrm, banks, full, hi, lo, small, gains=None, twice=None):
        self.src, self.src_ready, self.nrm, self.banks = src, src_ready, nrm, banks
        self.full, self.hi, self.lo, self.gains, self.twice = full, hi, lo, gains, twice
        self.stats, self.mv, self.var, self.rstd, self.r2 = small
        self.done = {what: sem(f"{name}_{what}") for what in (
            "stats", "aggr", "var", "rstd", "step", "normed", "plain", "turned", "full", "hi", "lo")}


class Ffn:

    def __init__(self, name, sem, norm, gu, down, pairs, ybanks, gate_scale, hid_scale):
        self.norm, self.gu, self.down, self.pairs, self.ybanks = norm, gu, down, pairs, ybanks
        self.gate_scale, self.hid_scale = gate_scale, hid_scale
        self.done = {what: sem(f"{name}_{what}") for what in (
            "gu", "tanh", "gated", "hid", "hi", "lo", "down", "scaled", "added")}


def program(nc, x, w_qkvg, w_o, w_12, w_3, w_gu, w_dn, w_xp, w_dt, cols, s_down, consts, out):
    x_view = x.rearrange("(n t p) d -> n p t d", p=P, t=TT)
    out_view = out.rearrange("(n t p) d -> n p t d", p=P, t=TT)

    with ExitStack() as ctx:
        sems = []

        def sb(name, shape, dt, c=ctx):
            return c.enter_context(nc.sbuf_tensor(name, shape, dt))

        def sem(name):
            s = ctx.enter_context(nc.semaphore(name))
            sems.append(s)
            return s

        banks = [ctx.enter_context(nc.psum_tensor(f"bank{i}", [P, 512], F32)) for i in range(8)]

        def pair(name, shape):
            return sb(name + "_hi", shape, F32R), sb(name + "_lo", shape, F32R)

        qkvg = pair("qkvg", [P, FT, 4 * D])
        wo = pair("wo", [P, FT, D])
        w12 = pair("w12", [P, FT, 2 * HP])
        w3 = pair("w3", [P, HT, D])
        gu = pair("gu", [P, FT, 2 * HP])
        dn = pair("dn", [P, HT, D])
        xp = pair("xp", [P, FT, DTR + 2 * NS])
        dtw = pair("dtw", [P, D])
        cst = sb("cst", [P, NCONST], F32)
        col = sb("col", [P, NCOLS], F32)
        sdrow = sb("sdrow", [P, D], F32)
        select = sb("select", [96, 32], BF16)
        a_neg = sb("a_neg", [P, FT * NS], F32)
        gate_half = sb("gate_half", [P, HT], F32)
        hid_scale = sb("hid_scale", [P, HT], F32)
        retain = sb("retain", [P, TT, FT, P], F32)
        hstate = sb("hstate", [P, FT, NS], F32)

        def const(name):
            lo, hi = CONSTS[name]
            return cst[:, lo:hi]

        def column(name, j=None):
            lo, hi = COLS[name]
            return col[:, lo:hi] if j is None else col[:, lo + j:lo + j + 1]

        ident = const("ident")

        with ExitStack() as stage:
            def st(name, shape, dt=F32):
                return sb("raw_" + name, shape, dt, stage)

            loads = [
                ("qkvg", st("qkvg", [P, FT, 4 * D]), w_qkvg.rearrange("(k p) m -> p k m", p=P), qkvg),
                ("wo", st("wo", [P, FT, D]), w_o.rearrange("(k p) m -> p k m", p=P), wo),
                ("w12", st("w12", [P, FT, 2 * HP]), w_12.rearrange("(k p) m -> p k m", p=P), w12),
                ("w3", st("w3", [P, HT, D]), w_3.rearrange("(k p) m -> p k m", p=P), w3),
                ("gu", st("gu", [P, FT, 2 * HP], I32), w_gu.rearrange("(k p) m -> p k m", p=P), gu),
                ("dn", st("dn", [P, HT, D], I32), w_dn.rearrange("(k p) m -> p k m", p=P), dn),
                ("xp", st("xp", [P, FT, DTR + 2 * NS]), w_xp.rearrange("(k p) m -> p k m", p=P), xp),
                ("dtw", st("dtw", [P, D]), w_dt, dtw),
            ]
            shifted = {"gu": st("gu_f", [P, FT, 2 * HP]), "dn": st("dn_f", [P, HT, D])}
            small_loaded = sem("small_loaded")
            loaded = {name: sem(f"{name}_loaded") for name, *_ in loads}
            part_hi = sem("part_hi")
            int_shifted = sem("int_shifted")
            halved = sem("halved")
            decay_exp = sem("decay_exp")

            with nc.Block() as block:
                @block.sync
                def _(sp):
                    sp.dma_start(cst[:], consts).then_inc(small_loaded, 16)
                    sp.dma_start(col[:], cols).then_inc(small_loaded, 16)
                    sp.dma_start(sdrow[:], s_down.partition_broadcast(P)).then_inc(small_loaded, 16)
                    for name, raw, src, _parts in loads:
                        sp.dma_start(raw[:], src).then_inc(loaded[name], 16)

                @block.scalar
                def _(act):
                    act.wait_ge(small_loaded, 48)
                    nc.scalar.activation(a_neg[:], column("alog"), ACT.Exp).then_inc(decay_exp, 1)

                @block.vector
                def _(dve):
                    nc.vector.memset(retain[:], 0.0)
                    nc.vector.memset(hstate[:], 0.0)
                    dve.wait_ge(small_loaded, 48)
                    nc.vector.tensor_copy(select[:], const("select")[0:96, :])
                    nc.vector.tensor_scalar(gate_half[:], column("sgate"), 0.5, None, ALU.mult).then_inc(halved, 1)
                    dve.wait_ge(halved, 1)
                    nc.vector.tensor_tensor(hid_scale[:], gate_half[:], column("sup"), ALU.mult)
                    dve.wait_ge(decay_exp, 1)
                    nc.vector.tensor_scalar(a_neg[:], a_neg[:], -1.0, None, ALU.mult)
                    ints = 0
                    for n, (name, raw, _src, (hi, lo)) in enumerate(loads):
                        dve.wait_ge(loaded[name], 16)
                        if name in shifted:
                            nc.vector.tensor_scalar(shifted[name][:], raw[:], -ZERO_POINT, None,
                                                    ALU.add).then_inc(int_shifted, 1)
                            ints += 1
                            dve.wait_ge(int_shifted, ints)
                            raw = shifted[name]
                        nc.vector.tensor_copy(hi[:], raw[:]).then_inc(part_hi, 1)
                        dve.wait_ge(part_hi, n + 1)
                        nc.vector.tensor_tensor(lo[:], raw[:], hi[:].bitcast(F32), ALU.subtract)

        xres = sb("xres", [P, TT, D], F32)
        nrm = sb("nrm", [P, TT, D], F32)
        xn = sb("xn", [P, TT, D], F32)
        hT = sb("hT", [P, FT, T], F32)
        hT_hi = sb("hT_hi", [P, FT, T], F32R)
        hT_lo = sb("hT_lo", [P, FT, T], F32R)
        act_ring = sb("act_ring", [P, 3, T], F32)
        hid_hi = sb("hid_hi", [P, 3, T], F32R)
        hid_lo = sb("hid_lo", [P, 3, T], F32R)

        def small(name):
            return (sb(name + "_stats", [P, TT, 6], F32), sb(name + "_mv", [P, TT, 2], F32),
                    sb(name + "_var", [P, TT], F32), sb(name + "_rstd", [P, TT], F32), sb(name + "_r2", [P, TT], F32))

        with ExitStack() as only_attn:
            qT = sb("qT", [P, FT, T], F32, only_attn)
            qTd = sb("qTd", [P, FT, T], F32, only_attn)
            kT = [sb("kT_even", [P, FT, T], F32, only_attn), sb("kT_odd", [P, FT, T], F32, only_attn)]
            kdec = sb("kdec", [P, TT, D], F32, only_attn)
            vtok = sb("vtok", [P, TT, D], F32, only_attn)
            probs = sb("probs", [P, 2, 512], F32, only_attn)
            gated = sb("gated", [P, TT, D], F32, only_attn)
            centred = sb("centred", [P, TT, D], F32, only_attn)
            squares = sb("squares", [P, TT, D], F32, only_attn)
            kvmask = sb("kvmask", [P, TT, FT, P], F32, only_attn)
            rmean = sb("rmean", [P, TT, HEADS], F32, only_attn)
            rvar = sb("rvar", [P, TT, HEADS], F32, only_attn)
            rstd = sb("ret_rstd", [P, TT, HEADS], F32, only_attn)
        yT_hi = hT_hi
        yT_lo = hT_lo

        delta = sb("delta", [P, FT, T], F32)
        dr_hi = sb("dr_hi", [P, T], F32R)
        dr_lo = sb("dr_lo", [P, T], F32R)
        sp_pos = sb("sp_pos", [P, FT, T], F32)
        du = sp_pos
        bc_full = sb("bc_full", [32, 2, T], F32)
        bc_parts = sb("bc_parts", [96, T], BF16)
        b_rep = sb("b_rep", [P, 2, T], F32)
        c_rep = sb("c_rep", [P, 2, T], F32)
        dA = sb("dA", [P, 2, FT, T], F32)
        hbuf = sb("hbuf", [P, 3, FT, T], F32)
        yscan = sb("yscan", [P, FT, T], F32)

        sems.clear()
        x_in = sem("x_in")
        x_out = sem("x_out")

        z_added = sem("z_added")
        xz_added = sem("xz_added")
        x3_added = sem("x3_added")

        n1 = Norm("n1", sem, xres, (x_in, 16), nrm, (0, 1), hT, hT_hi, hT_lo, small("n1"),
                  gains=("n1w", "n1b"), twice=xn)
        n2 = Norm("n2", sem, xn, (z_added, 2), nrm, (4, 5), hT, hT_hi, hT_lo, small("n2"), gains=("n2w", "n2b"))
        f1 = Ffn("f1", sem, n2, w12, w3, ((0, 1), (2, 3)), (4, 5), None, None)
        n3 = Norm("n3", sem, xres, (f1.done["added"], 2), nrm, (4, 5), hT, hT_hi, hT_lo, small("n3"))
        f2 = Ffn("f2", sem, n3, gu, dn, ((0, 1), (2, 3)), (4, 5), gate_half, hid_scale)
        n4 = Norm("n4", sem, xres, (f2.done["added"], 2), nrm, (6, 7), hT, hT_hi, hT_lo, small("n4"))
        n5 = Norm("n5", sem, xres, (x3_added, 2), nrm, (4, 5), hT, hT_hi, hT_lo, small("n5"))
        f3 = Ffn("f3", sem, n5, gu, dn, ((0, 1), (2, 3)), (4, 5), gate_half, hid_scale)

        q_turned, q_copied, q_decayed = sem("q_turned"), sem("q_copied"), sem("q_decayed")
        k_turned, k_masked = sem("k_turned"), sem("k_masked")
        kv_made, k_decayed, v_copied = sem("kv_made"), sem("k_decayed"), sem("v_copied")
        g_made, g_tanh, g_gated = sem("g_made"), sem("g_tanh"), sem("g_gated")
        outer_made, outer_masked, state_ready = sem("outer_made"), sem("outer_masked"), sem("state_ready")
        scores_made, probs_made, probs_used = sem("scores_made"), sem("probs_made"), sem("probs_used")
        ret_made, ret_mean, ret_centred = sem("ret_made"), sem("ret_mean"), sem("ret_centred")
        ret_squared, ret_var, ret_rstd = sem("ret_squared"), sem("ret_var"), sem("ret_rstd")
        g_scaled, ret_gated = sem("g_scaled"), sem("ret_gated")
        yt_turned, yt_hi, yt_lo, y_projected = sem("yt_turned"), sem("yt_hi"), sem("yt_lo"), sem("y_projected")

        dr_made, drh_made, drl_made = sem("dr_made"), sem("drh_made"), sem("drl_made")
        bc_made, bc_copied, bc_part = sem("bc_made"), sem("bc_copied"), sem("bc_part")
        dt_made, dt_abs, dt_exp, dt_ln, dt_pos = sem("dt_made"), sem("dt_abs"), sem("dt_exp"), sem("dt_ln"), sem("dt_pos")
        delta_made, du_made = sem("delta_made"), sem("du_made")
        rep_made, rep_copied = sem("rep_made"), sem("rep_copied")
        decay_made, dbu_made, scanned, saved, outs_made, y_added = (
            sem("decay_made"), sem("dbu_made"), sem("scanned"), sem("saved"), sem("outs_made"), sem("y_added"))
        y_skipped, y_back = sem("y_skipped"), sem("y_back")

        def products(acc, sta, mov, start, stop, skip=False):
            terms = []
            for (sh, sl), (mh, ml) in zip(sta, mov):
                terms += [(sh, mh), (sh, ml), (sl, mh)]
            for n, (a, b) in enumerate(terms):
                last = nc.tensor.matmul(acc, a, b, start=start and n == 0, stop=stop and n == len(terms) - 1,
                                        skip_group_check=skip)
            return last

        def pe_norm(pe, n):
            for ft in range(FT):
                for tt in range(TT):
                    if ft == 0:
                        pe.wait_ge(n.done["normed"], tt + 1)
                    last = nc.tensor.transpose(banks[n.banks[ft]][:, tt * P:(tt + 1) * P],
                                               n.nrm[:, tt, ft * P:(ft + 1) * P], ident)
                last.then_inc(n.done["turned"], 1)

        def pe_gate_up(pe, f, j):
            if j == 0:
                pe.wait_ge(f.norm.done["lo"], FT)
            if j >= len(f.pairs):
                pe.wait_ge(f.done["hid"], j - len(f.pairs) + 1)
            for half, bank in enumerate(f.pairs[j % len(f.pairs)]):
                m = slice(half * HP + j * P, half * HP + (j + 1) * P)
                sta = [(f.gu[0][:, k, m], f.gu[1][:, k, m]) for k in range(FT)]
                mov = [(f.norm.hi[:, k, :], f.norm.lo[:, k, :]) for k in range(FT)]
                last = products(banks[bank][:], sta, mov, True, True)
            last.then_inc(f.done["gu"], 1)

        def pe_down(pe, f, j):
            pe.wait_ge(f.done["lo"], j + 1)
            for tt in range(TT):
                t = slice(tt * P, (tt + 1) * P)
                acc = banks[f.ybanks[tt // 2]][:, (tt % 2) * D:(tt % 2 + 1) * D]
                last = products(acc, [(hid_hi[:, j % 3, t], hid_lo[:, j % 3, t])],
                                [(f.down[0][:, j, :], f.down[1][:, j, :])],
                                j == 0 and tt % 2 == 0, j == HT - 1, skip=True)
            last.then_inc(f.done["down"], 1)

        def pe_ffn(pe, f):
            for j in range(HT + 2):
                if j < HT:
                    pe_gate_up(pe, f, j)
                if j >= 2:
                    pe_down(pe, f, j - 2)

        def pe_attention(pe):
            hT_parts = [(n1.hi[:, k, :], n1.lo[:, k, :]) for k in range(FT)]
            pe.wait_ge(n1.done["lo"], FT)
            for ft in range(FT):
                m = slice(ft * P, (ft + 1) * P)
                sta = [(qkvg[0][:, k, m], qkvg[1][:, k, m]) for k in range(FT)]
                products(banks[2 + ft][:], sta, hT_parts, True, True).then_inc(q_turned, 1)
            for ft in range(FT):
                m = slice(D + ft * P, D + (ft + 1) * P)
                sta = [(qkvg[0][:, k, m], qkvg[1][:, k, m]) for k in range(FT)]
                products(banks[ft][:], sta, hT_parts, True, True).then_inc(k_turned, 1)
            for tt in range(TT):
                if tt < 2:
                    pe.wait_ge(q_copied, tt + 1)
                    pe.wait_ge(q_decayed, tt + 1)
                else:
                    pe.wait_ge(k_decayed, tt - 1)
                    pe.wait_ge(v_copied, tt - 1)
                sta = [(n1.hi[:, k, tt * P:(tt + 1) * P], n1.lo[:, k, tt * P:(tt + 1) * P]) for k in range(FT)]
                mov = [(qkvg[0][:, k, D:3 * D], qkvg[1][:, k, D:3 * D]) for k in range(FT)]
                products(banks[2 + tt % 2][:], sta, mov, True, True).then_inc(kv_made, 1)
            for tt in range(TT):
                if tt % 2 == 0:
                    pe.wait_ge(k_masked, tt + 2)
                sta = [(n1.hi[:, k, tt * P:(tt + 1) * P], n1.lo[:, k, tt * P:(tt + 1) * P]) for k in range(FT)]
                mov = [(qkvg[0][:, k, 3 * D:4 * D], qkvg[1][:, k, 3 * D:4 * D]) for k in range(FT)]
                last = products(banks[tt // 2][:, (tt % 2) * D:(tt % 2 + 1) * D], sta, mov, True, True)
                if tt % 2:
                    last.then_inc(g_made, 1)
            for tt in range(TT):
                if tt % 2 == 0:
                    pe.wait_ge(k_decayed, tt // 2 + 3)
                    pe.wait_ge(v_copied, tt // 2 + 3)
                for f in range(FT):
                    c = ((tt % 2) * FT + f) * P
                    last = nc.tensor.matmul(banks[2 + tt // 2][:, c:c + P], kdec[:, tt, f * P:(f + 1) * P],
                                            vtok[:, tt, f * P:(f + 1) * P], start=True, stop=True)
                if tt % 2:
                    last.then_inc(outer_made, 1)
            uses = [(cp, f, rg) for cp in range(2) for f in range(FT) for rg in range(4)]

            def score(u):
                cp, f, rg = uses[u]
                bank = banks[u % 2]
                if u < 2:
                    pe.wait_ge(g_gated, u + 1)
                    pe.wait_ge(k_masked, 4)
                    pe.wait_ge(q_copied, 2)
                else:
                    pe.wait_ge(probs_made, u - 1)
                rows = slice(32 * rg, 32 * rg + 32)
                for c in range(2):
                    tok = slice((2 * cp + c) * P, (2 * cp + c + 1) * P)
                    for par in range(2):
                        o = (c * 2 + par) * P
                        last = nc.tensor.matmul(bank[:, o:o + P], kT[par][rows, f, tok], qT[rows, f, tok],
                                                start=True, stop=True)
                last.then_inc(scores_made, 1)

            def values(u):
                cp, f, rg = uses[u]
                if f == 0 and rg == 0:
                    pe.wait_ge(outer_masked, cp + 1)
                    pe.wait_ge(q_decayed, 2)
                    for c in range(2):
                        if 2 * cp + c:
                            pe.wait_ge(state_ready, 2 * cp + c)
                        tok = slice((2 * cp + c) * P, (2 * cp + c + 1) * P)
                        for g in range(FT):
                            last = nc.tensor.matmul(banks[2 + cp][:, c * D + g * P:c * D + (g + 1) * P], qTd[:, g, tok],
                                                    retain[:, 2 * cp + c, g, :], start=(c == 0 and g == 0), stop=False,
                                                    skip_group_check=True)
                pe.wait_ge(probs_made, u + 1)
                for c in range(2):
                    for par in range(2):
                        h = f * 8 + rg * 2 + par
                        o = (c * 2 + par) * P
                        last = nc.tensor.matmul(banks[2 + cp][:, c * D + h * DH:c * D + (h + 1) * DH],
                                                probs[:, u % 2, o:o + P], vtok[:, 2 * cp + c, h * DH:(h + 1) * DH],
                                                start=False, stop=True, skip_group_check=True)
                last.then_inc(probs_used, 1)

            for u in range(len(uses) + 1):
                if u < len(uses):
                    score(u)
                if u >= 1:
                    values(u - 1)
            for ft in range(FT):
                pe.wait_ge(probs_made, 16)
                for tt in range(TT):
                    if ft == 0 and tt % 2 == 0:
                        pe.wait_ge(ret_gated, tt // 2 + 1)
                    last = nc.tensor.transpose(banks[ft][:, tt * P:(tt + 1) * P], gated[:, tt, ft * P:(ft + 1) * P], ident)
                last.then_inc(yt_turned, 1)
            pe.wait_ge(yt_lo, FT)
            pe.wait_ge(ret_centred, 2)
            for tt in range(TT):
                t = slice(tt * P, (tt + 1) * P)
                last = products(banks[2 + tt // 2][:, (tt % 2) * D:(tt % 2 + 1) * D],
                                [(yT_hi[:, k, t], yT_lo[:, k, t]) for k in range(FT)],
                                [(wo[0][:, k, :], wo[1][:, k, :]) for k in range(FT)], True, True)
                if tt % 2:
                    last.then_inc(y_projected, 1)

        def pe_scan(pe):
            pe.wait_ge(n4.done["lo"], FT)
            hT_parts = [(n4.hi[:, k, :], n4.lo[:, k, :]) for k in range(FT)]
            products(banks[6][:], [(xp[0][:, k, 0:DTR], xp[1][:, k, 0:DTR]) for k in range(FT)],
                     hT_parts, True, True).then_inc(dr_made, 1)
            bc = slice(DTR, DTR + 2 * NS)
            products(banks[7][0:32, :], [(xp[0][:, k, bc].bitcast(F32), xp[1][:, k, bc].bitcast(F32)) for k in range(FT)],
                     [(a.bitcast(F32), b.bitcast(F32)) for a, b in hT_parts], True, True).then_inc(bc_made, 1)
            pe.wait_ge(drl_made, 1)
            for ft in range(FT):
                if ft == 1:
                    pe.wait_ge(bc_copied, 1)
                m = slice(ft * P, (ft + 1) * P)
                products(banks[6 + ft][:], [(dtw[0][:, m], dtw[1][:, m])], [(dr_hi[:], dr_lo[:])],
                         True, True).then_inc(dt_made, 1)
            pe.wait_ge(bc_part, 3)
            for n in range(NS):
                for which in range(2):
                    if n == 0:
                        pe.wait_ge(dt_abs, which + 1)
                        pe.wait_ge(dt_pos, which + 1)
                    else:
                        pe.wait_ge(rep_copied, 2 * n - 1 + which)
                    row = which * NS + n
                    nc.tensor.matmul(banks[6 + which][:], select[:, row:row + 1].to_broadcast([96, P]), bc_parts[:],
                                     start=True, stop=True).then_inc(rep_made, 1)
            for tt in range(TT):
                if tt % 2 == 0:
                    pe.wait_ge(y_skipped, 2)
                    pe.wait_ge(rep_copied, 2 * NS)
                for ft in range(FT):
                    c = (tt % 2) * D + ft * P
                    last = nc.tensor.transpose(banks[6 + tt // 2][:, c:c + P], yscan[:, ft, tt * P:(tt + 1) * P], ident)
                if tt % 2:
                    last.then_inc(y_back, 1)

        def act_norm(act, n):
            for ft in range(FT):
                act.wait_ge(n.done["turned"], ft + 1)
                bank = banks[n.banks[ft]]
                if n.gains:
                    nc.scalar.activation(n.full[:, ft, :], bank[:], ACT.Identity, bias=column(n.gains[1], ft),
                                         scale=column(n.gains[0], ft)).then_inc(n.done["full"], 1)
                else:
                    nc.scalar.activation(n.full[:, ft, :], bank[:], ACT.Copy).then_inc(n.done["full"], 1)

        def act_tanh(act, f, j):
            act.wait_ge(f.done["gu"], j + 1)
            if j >= 3:
                act.wait_ge(f.done["lo"], j - 2)
            scale = 0.5 if f.gate_scale is None else f.gate_scale[:, j:j + 1]
            nc.scalar.activation(act_ring[:, j % 3, :], banks[f.pairs[j % len(f.pairs)][0]][:], ACT.Tanh,
                                 scale=scale).then_inc(f.done["tanh"], 1)

        def act_hidden(act, f, j):
            act.wait_ge(f.done["hid"], j + 1)
            if j >= 3:
                act.wait_ge(f.done["down"], j - 2)
            nc.scalar.activation(hid_hi[:, j % 3, :], act_ring[:, j % 3, :], ACT.Copy).then_inc(f.done["hi"], 1)

        def act_ffn(act, f):
            for j in range(HT + 1):
                if j < HT:
                    act_tanh(act, f, j)
                if j >= 1:
                    act_hidden(act, f, j - 1)

        def act_attention(act):
            for ft in range(FT):
                act.wait_ge(q_turned, ft + 1)
                nc.scalar.activation(qT[:, ft, :], banks[2 + ft][:], ACT.Copy).then_inc(q_copied, 1)
            for ft in range(FT):
                act.wait_ge(k_turned, ft + 1)
                for par, name in enumerate(("even", "odd")):
                    nc.scalar.activation(kT[par][:, ft, :], banks[ft][:], ACT.Copy,
                                         scale=const(name)).then_inc(k_masked, 1)
            for tt in range(TT):
                act.wait_ge(kv_made, tt + 1)
                nc.scalar.activation(vtok[:, tt, :], banks[2 + tt % 2][:, D:2 * D], ACT.Copy).then_inc(v_copied, 1)
            for half in range(2):
                act.wait_ge(g_made, half + 1)
                nc.scalar.activation(gated[:, 2 * half:2 * half + 2, :], banks[half][:], ACT.Tanh,
                                     scale=0.5).then_inc(g_tanh, 1)
            for half in range(2):
                act.wait_ge(ret_centred, half + 1)
                t2 = slice(2 * half, 2 * half + 2)
                nc.scalar.activation(squares[:, t2, :], centred[:, t2, :], ACT.Square).then_inc(ret_squared, 1)
            for ft in range(FT):
                act.wait_ge(yt_turned, ft + 1)
                nc.scalar.activation(yT_hi[:, ft, :], banks[ft][:], ACT.Copy).then_inc(yt_hi, 1)

        def act_scan(act):
            act.wait_ge(dr_made, 1)
            nc.scalar.activation(dr_hi[:], banks[6][:], ACT.Copy).then_inc(drh_made, 1)
            act.wait_ge(bc_made, 1)
            nc.scalar.activation(bc_full[:, 0, :], banks[7][0:32, :], ACT.Copy).then_inc(bc_copied, 1)
            for ft in range(FT):
                act.wait_ge(dt_made, ft + 1)
                nc.scalar.activation(delta[:, ft, :], banks[6 + ft][:], ACT.Abs, bias=column("dtb", ft)).then_inc(dt_abs, 1)
            for ft in range(FT):
                act.wait_ge(dt_abs, ft + 1)
                nc.scalar.activation(delta[:, ft, :], delta[:, ft, :], ACT.Exp, scale=-1.0).then_inc(dt_exp, 1)
            for ft in range(FT):
                act.wait_ge(dt_exp, ft + 1)
                nc.scalar.activation(delta[:, ft, :], delta[:, ft, :], ACT.Ln, bias=1.0).then_inc(dt_ln, 1)
            for n in range(NS):
                for which, rep in enumerate((b_rep, c_rep)):
                    act.wait_ge(rep_made, 2 * n + which + 1)
                    if n >= 2:
                        act.wait_ge((dbu_made, outs_made)[which], n - 1)
                    nc.scalar.activation(rep[:, n % 2, :], banks[6 + which][:], ACT.Copy).then_inc(rep_copied, 1)
                if n == 0:
                    act.wait_ge(delta_made, FT)
                if n >= 2:
                    act.wait_ge(scanned, FT * (n - 1))
                for ft in range(FT):
                    c = ft * NS + n
                    nc.scalar.activation(dA[:, n % 2, ft, :], delta[:, ft, :], ACT.Exp,
                                         scale=a_neg[:, c:c + 1]).then_inc(decay_made, 1)

        def dve_norm_stats(dve, n):
            dve.wait_ge(*n.src_ready)
            for tt in range(TT):
                nc.vector.bn_stats(n.stats[:, tt, :], n.src[:, tt, :]).then_inc(n.done["stats"], 1)
            for tt in range(TT):
                dve.wait_ge(n.done["stats"], tt + 1)
                nc.vector.bn_aggr(n.mv[:, tt, :], n.stats[:, tt, :]).then_inc(n.done["aggr"], 1)
            dve.wait_ge(n.done["aggr"], TT)
            nc.vector.tensor_scalar(n.var[:], n.mv[:, :, 1], EPS, None, ALU.add).then_inc(n.done["var"], 1)

        def dve_norm_apply(dve, n):
            dve.wait_ge(n.done["rstd"], 1)
            r = n.r2 if n.twice is not None else n.rstd
            for tt in range(TT):
                nc.vector.tensor_scalar(n.nrm[:, tt, :], n.src[:, tt, :], n.mv[:, tt, 0:1], r[:, tt:tt + 1],
                                        ALU.subtract, ALU.mult).then_inc(n.done["normed"], 1)
            if n.twice is not None:
                for tt in range(TT):
                    nc.vector.tensor_scalar(n.twice[:, tt, :], n.src[:, tt, :], n.mv[:, tt, 0:1], n.rstd[:, tt:tt + 1],
                                            ALU.subtract, ALU.mult).then_inc(n.done["plain"], 1)

        def dve_norm_split(dve, n):
            for ft in range(FT):
                dve.wait_ge(n.done["full"], ft + 1)
                nc.vector.tensor_copy(n.hi[:, ft, :], n.full[:, ft, :]).then_inc(n.done["hi"], 1)

        def dve_norm(dve, n):
            dve_norm_stats(dve, n)
            dve_norm_apply(dve, n)
            dve_norm_split(dve, n)

        def dve_hidden(dve, f, j):
            g, u = f.pairs[j % len(f.pairs)]
            a = act_ring[:, j % 3, :]
            dve.wait_ge(f.done["tanh"], j + 1)
            nc.vector.scalar_tensor_tensor(a, a, 1.0, banks[g][:], ALU.add, ALU.mult).then_inc(f.done["gated"], 1)
            dve.wait_ge(f.done["gated"], j + 1)
            scale = 0.5 if f.hid_scale is None else f.hid_scale[:, j:j + 1]
            nc.vector.scalar_tensor_tensor(a, a, scale, banks[u][:], ALU.mult, ALU.mult).then_inc(f.done["hid"], 1)

        def dve_ffn_end(dve, f):
            dve.wait_ge(f.done["down"], HT)
            for half in range(2):
                t2 = slice(2 * half, 2 * half + 2)
                y = banks[f.ybanks[half]][:].rearrange("p (t d) -> p t d", t=2)
                if f.hid_scale is None:
                    dve.wait_ge(xz_added, 1)
                    nc.vector.tensor_tensor(xres[:, t2, :], xres[:, t2, :], y, ALU.add).then_inc(f.done["added"], 1)
                else:
                    nc.vector.tensor_tensor(f.norm.nrm[:, t2, :], y, sdrow[:].unsqueeze(1).to_broadcast([P, 2, D]),
                                            ALU.mult).then_inc(f.done["scaled"], 1)
            if f.hid_scale is not None:
                for half in range(2):
                    t2 = slice(2 * half, 2 * half + 2)
                    dve.wait_ge(f.done["scaled"], half + 1)
                    nc.vector.tensor_tensor(xres[:, t2, :], xres[:, t2, :], f.norm.nrm[:, t2, :],
                                            ALU.add).then_inc(f.done["added"], 1)

        def dve_ffn(dve, f):
            for j in range(HT):
                dve_hidden(dve, f, j)
            dve_ffn_end(dve, f)

        def dve_attention(dve):
            for ft in range(FT):
                dve.wait_ge(q_turned, ft + 1)
                dve.wait_ge(q_copied, ft + 1)
                lo, _ = CONSTS["qdecay"]
                table = cst[:, lo + ft * P:lo + (ft + 1) * P].unsqueeze(1).to_broadcast([P, TT, P])
                nc.vector.tensor_tensor(qTd[:, ft, :].rearrange("p (t s) -> p t s", t=TT),
                                        banks[2 + ft][:].rearrange("p (t s) -> p t s", t=TT), table,
                                        ALU.mult).then_inc(q_decayed, 1)
            for tt in range(TT):
                dve.wait_ge(kv_made, tt + 1)
                dve.wait_ge(v_copied, tt + 1)
                nc.vector.tensor_tensor(kdec[:, tt, :], banks[2 + tt % 2][:, 0:D], const("kdecay"),
                                        ALU.mult).then_inc(k_decayed, 1)
            for half in range(2):
                dve.wait_ge(g_tanh, half + 1)
                t2 = slice(2 * half, 2 * half + 2)
                nc.vector.scalar_tensor_tensor(gated[:, t2, :], gated[:, t2, :], 1.0,
                                               banks[half][:].rearrange("p (t d) -> p t d", t=2),
                                               ALU.add, ALU.mult).then_inc(g_gated, 1)
            mask = const("headmask").unsqueeze(1).to_broadcast([P, 2 * FT, P])
            for half in range(2):
                dve.wait_ge(outer_made, half + 1)
                nc.vector.tensor_tensor(kvmask[:, 2 * half:2 * half + 2, :, :].rearrange("p t f e -> p (t f) e"),
                                        banks[2 + half][:].rearrange("p (g e) -> p g e", e=P), mask,
                                        ALU.mult).then_inc(outer_masked, 1)
            dve.wait_ge(outer_masked, 2)

            def carry(c):
                if c == TT - 1:
                    dve.wait_ge(probs_used, 1)
                if c >= 1:
                    dve.wait_ge(state_ready, c)
                for f in range(FT):
                    dst = retain[:, (c + 1) % TT, f, :]
                    last = nc.vector.scalar_tensor_tensor(dst, retain[:, c, f, :], const("chunkdecay")[:, f:f + 1],
                                                          kvmask[:, c, f, :], ALU.mult, ALU.add)
                last.then_inc(state_ready, 1)

            for c in range(TT - 1):
                carry(c)
            for u in range(16):
                f, rg = (u // 4) % 2, u % 4
                dve.wait_ge(scores_made, u + 1)
                if u >= 2:
                    dve.wait_ge(probs_used, u - 1)
                h = f * 8 + rg * 2
                table = cst[:, h * P:(h + 2) * P].rearrange("p (h s) -> p h s", h=2)
                src = banks[u % 2][:].rearrange("p (c h s) -> p c h s", c=2, h=2)
                dst = probs[:, u % 2, :].rearrange("p (c h s) -> p c h s", c=2, h=2)
                nc.vector.tensor_tensor(dst, src, table.unsqueeze(1).to_broadcast([P, 2, 2, P]),
                                        ALU.mult).then_inc(probs_made, 1)
                if u == 5:
                    carry(TT - 1)
            for half in range(2):
                t2 = slice(2 * half, 2 * half + 2)
                dve.wait_ge(probs_used, 8 * (half + 1))
                ret = banks[2 + half][:].rearrange("p (g e) -> p g e", e=DH)
                mean = rmean[:, t2, :].rearrange("p t h -> p (t h)")
                nc.vector.tensor_reduce(mean, ret, AX_X, ALU.add).then_inc(ret_mean, 1)
                dve.wait_ge(ret_mean, 2 * half + 1)
                nc.vector.tensor_scalar(mean, mean, 1.0 / DH, None, ALU.mult).then_inc(ret_mean, 1)
                dve.wait_ge(ret_mean, 2 * half + 2)
                cen = centred[:, t2, :].rearrange("p t (h e) -> p (t h) e", e=DH)
                nc.vector.tensor_tensor(cen, ret, mean.unsqueeze(2).to_broadcast([P, 2 * HEADS, DH]),
                                        ALU.subtract).then_inc(ret_centred, 1)
                dve.wait_ge(ret_squared, half + 1)
                var = rvar[:, t2, :].rearrange("p t h -> p (t h)")
                nc.vector.tensor_reduce(var, squares[:, t2, :].rearrange("p t (h e) -> p (t h) e", e=DH),
                                        AX_X, ALU.add).then_inc(ret_var, 1)
                dve.wait_ge(ret_var, 2 * half + 1)
                nc.vector.tensor_scalar(var, var, 1.0 / DH, EPS, ALU.mult, ALU.add).then_inc(ret_var, 1)
                nc.vector.scalar_tensor_tensor(gated[:, t2, :], gated[:, t2, :], 0.5, centred[:, t2, :],
                                               ALU.mult, ALU.mult).then_inc(g_scaled, 1)
                dve.wait_ge(g_scaled, half + 1)
                dve.wait_ge(ret_rstd, half + 1)
                gat = gated[:, t2, :].rearrange("p t (h e) -> p (t h) e", e=DH)
                r = rstd[:, t2, :].rearrange("p t h -> p (t h)").unsqueeze(2).to_broadcast([P, 2 * HEADS, DH])
                nc.vector.tensor_tensor(gat, gat, r, ALU.mult).then_inc(ret_gated, 1)
            for ft in range(FT):
                dve.wait_ge(yt_hi, ft + 1)
                nc.vector.tensor_tensor(yT_lo[:, ft, :], banks[ft][:], yT_hi[:, ft, :].bitcast(F32),
                                        ALU.subtract).then_inc(yt_lo, 1)
            dve.wait_ge(n1.done["plain"], TT)
            for half in range(2):
                t2 = slice(2 * half, 2 * half + 2)
                dve.wait_ge(y_projected, half + 1)
                nc.vector.tensor_tensor(xn[:, t2, :], xn[:, t2, :], banks[2 + half][:].rearrange("p (t d) -> p t d", t=2),
                                        ALU.add).then_inc(z_added, 1)

        def dve_scan(dve):
            dve.wait_ge(drh_made, 1)
            nc.vector.tensor_tensor(dr_lo[:], banks[6][:], dr_hi[:].bitcast(F32), ALU.subtract).then_inc(drl_made, 1)
            dve.wait_ge(bc_copied, 1)
            for part in range(3):
                here = bc_parts[32 * part:32 * part + 32, :]
                nc.vector.tensor_copy(here, bc_full[:, part % 2, :]).then_inc(bc_part, 1)
                if part < 2:
                    dve.wait_ge(bc_part, 2 * part + 1)
                    nc.vector.tensor_tensor(bc_full[:, (part + 1) % 2, :], bc_full[:, part, :], here,
                                            ALU.subtract).then_inc(bc_part, 1)
                    dve.wait_ge(bc_part, 2 * part + 2)
            for ft in range(FT):
                dve.wait_ge(dt_made, ft + 1)
                dve.wait_ge(dt_abs, ft + 1)
                nc.vector.tensor_scalar(sp_pos[:, ft, :], banks[6 + ft][:], column("dtb", ft), 0.0,
                                        ALU.add, ALU.max).then_inc(dt_pos, 1)
            for ft in range(FT):
                dve.wait_ge(dt_ln, ft + 1)
                dve.wait_ge(dt_pos, ft + 1)
                nc.vector.tensor_tensor(delta[:, ft, :], delta[:, ft, :], sp_pos[:, ft, :],
                                        ALU.add).then_inc(delta_made, 1)
            dve.wait_ge(delta_made, FT)
            nc.vector.tensor_tensor(du[:], delta[:], hT[:], ALU.mult).then_inc(du_made, 1)
            dve.wait_ge(du_made, 1)

            def add_outputs(n):
                dve.wait_ge(outs_made, n + 1)
                if n == 0:
                    nc.vector.tensor_copy(yscan[:], hbuf[:, 0, :, :]).then_inc(y_added, 1)
                else:
                    dve.wait_ge(y_added, n)
                    nc.vector.tensor_tensor(yscan[:], yscan[:], hbuf[:, n % 3, :, :], ALU.add).then_inc(y_added, 1)

            for n in range(NS):
                dve.wait_ge(rep_copied, 2 * n + 1)
                if n >= 3:
                    dve.wait_ge(y_added, n - 2)
                nc.vector.tensor_tensor(hbuf[:, n % 3, :, :], du[:], b_rep[:, n % 2, :].unsqueeze(1).to_broadcast([P, FT, T]),
                                        ALU.mult).then_inc(dbu_made, 1)
                dve.wait_ge(dbu_made, n + 1)
                for ft in range(FT):
                    dve.wait_ge(decay_made, FT * n + ft + 1)
                    nc.vector.tensor_tensor_scan(hbuf[:, n % 3, ft, :], dA[:, n % 2, ft, :], hbuf[:, n % 3, ft, :],
                                                 hstate[:, ft, n:n + 1], ALU.mult, ALU.add).then_inc(scanned, 1)
                if n >= 1:
                    add_outputs(n - 1)
            add_outputs(NS - 1)
            dve.wait_ge(y_added, NS)
            for ft in range(FT):
                nc.vector.scalar_tensor_tensor(yscan[:, ft, :], hT[:, ft, :], column("dskip", ft), yscan[:, ft, :],
                                               ALU.mult, ALU.add).then_inc(y_skipped, 1)
            for half in range(2):
                t2 = slice(2 * half, 2 * half + 2)
                dve.wait_ge(y_back, half + 1)
                nc.vector.tensor_tensor(xres[:, t2, :], xres[:, t2, :], banks[6 + half][:].rearrange("p (t d) -> p t d", t=2),
                                        ALU.add).then_inc(x3_added, 1)

        def pool_norm(pool, n):
            half = const("half")
            pool.wait_ge(n.done["var"], 1)
            if n.twice is None:
                nc.gpsimd.tensor_tensor(n.rstd[:], n.var[:], half, ALU.pow).then_inc(n.done["rstd"], 1)
            else:
                nc.gpsimd.tensor_tensor(n.rstd[:], n.var[:], half, ALU.pow).then_inc(n.done["step"], 1)
                pool.wait_ge(n.done["step"], 1)
                nc.gpsimd.tensor_tensor(n.var[:], n.mv[:, :, 1], n.rstd[:], ALU.mult).then_inc(n.done["step"], 1)
                pool.wait_ge(n.done["step"], 2)
                nc.gpsimd.tensor_tensor(n.var[:], n.var[:], n.rstd[:], ALU.mult).then_inc(n.done["step"], 1)
                pool.wait_ge(n.done["step"], 3)
                nc.gpsimd.tensor_scalar(n.var[:], n.var[:], EPS, None, ALU.add).then_inc(n.done["step"], 1)
                pool.wait_ge(n.done["step"], 4)
                nc.gpsimd.tensor_tensor(n.var[:], n.var[:], half, ALU.pow).then_inc(n.done["step"], 1)
                pool.wait_ge(n.done["step"], 5)
                nc.gpsimd.tensor_tensor(n.r2[:], n.var[:], n.rstd[:], ALU.mult).then_inc(n.done["rstd"], 1)
            for ft in range(FT):
                pool.wait_ge(n.done["hi"], ft + 1)
                nc.gpsimd.tensor_tensor(n.lo[:, ft, :], n.full[:, ft, :], n.hi[:, ft, :].bitcast(F32),
                                        ALU.subtract).then_inc(n.done["lo"], 1)

        def pool_ffn(pool, f):
            for j in range(HT):
                pool.wait_ge(f.done["hi"], j + 1)
                nc.gpsimd.tensor_tensor(hid_lo[:, j % 3, :], act_ring[:, j % 3, :], hid_hi[:, j % 3, :].bitcast(F32),
                                        ALU.subtract).then_inc(f.done["lo"], 1)

        def pool_attention(pool):
            for half in range(2):
                pool.wait_ge(ret_var, 2 * half + 2)
                t2 = slice(2 * half, 2 * half + 2)
                nc.gpsimd.tensor_tensor(rstd[:, t2, :], rvar[:, t2, :],
                                        const("half")[:, 0:1].unsqueeze(2).to_broadcast([P, 2, HEADS]),
                                        ALU.pow).then_inc(ret_rstd, 1)
            pool.wait_ge(z_added, 2)
            nc.gpsimd.tensor_tensor(xres[:], xres[:], xn[:], ALU.add).then_inc(xz_added, 1)

        def pool_scan(pool):
            for n in range(NS):
                pool.wait_ge(scanned, FT * (n + 1))
                nc.gpsimd.tensor_copy(hstate[:, :, n:n + 1], hbuf[:, n % 3, :, T - 1:T]).then_inc(saved, 1)
                pool.wait_ge(saved, n + 1)
                pool.wait_ge(rep_copied, 2 * n + 2)
                nc.gpsimd.tensor_tensor(hbuf[:, n % 3, :, :], hbuf[:, n % 3, :, :],
                                        c_rep[:, n % 2, :].unsqueeze(1).to_broadcast([P, FT, T]),
                                        ALU.mult).then_inc(outs_made, 1)

        with nc.Fori(0, CHUNKS) as chunk:
            with nc.Block() as block:
                @block.sync
                def _(sp):
                    sp.dma_start(xres[:], x_view[chunk]).then_inc(x_in, 16)
                    sp.wait_ge(f3.done["added"], 2)
                    sp.dma_start(out_view[chunk], xres[:]).then_inc(x_out, 16)
                    sp.wait_ge(x_out, 16)

                @block.tensor
                def _(pe):
                    pe_norm(pe, n1)
                    pe_attention(pe)
                    pe_norm(pe, n2)
                    pe_ffn(pe, f1)
                    pe_norm(pe, n3)
                    pe_ffn(pe, f2)
                    pe_norm(pe, n4)
                    pe_scan(pe)
                    pe_norm(pe, n5)
                    pe_ffn(pe, f3)

                @block.scalar
                def _(act):
                    act_norm(act, n1)
                    act_attention(act)
                    act_norm(act, n2)
                    act_ffn(act, f1)
                    act_norm(act, n3)
                    act_ffn(act, f2)
                    act_norm(act, n4)
                    act_scan(act)
                    act_norm(act, n5)
                    act_ffn(act, f3)

                @block.vector
                def _(dve):
                    dve_norm(dve, n1)
                    dve_attention(dve)
                    dve_norm(dve, n2)
                    dve_ffn(dve, f1)
                    dve_norm(dve, n3)
                    dve_ffn(dve, f2)
                    dve_norm(dve, n4)
                    dve_scan(dve)
                    dve_norm(dve, n5)
                    dve_ffn(dve, f3)

                @block.gpsimd
                def _(pool):
                    pool_norm(pool, n1)
                    pool_attention(pool)
                    pool_norm(pool, n2)
                    pool_ffn(pool, f1)
                    pool_norm(pool, n3)
                    pool_ffn(pool, f2)
                    pool_norm(pool, n4)
                    pool_scan(pool)
                    pool_norm(pool, n5)
                    pool_ffn(pool, f3)

            for s in sems:
                nc.sync.sem_clear(s)
            nc.all_engine_barrier()


def host_layout(i):
    def pad_cols(a, n):
        return np.concatenate([a, np.zeros((a.shape[0], n - a.shape[1]), a.dtype)], axis=1)

    def pad_rows(a, n):
        return np.concatenate([a, np.zeros((n - a.shape[0],) + a.shape[1:], a.dtype)], axis=0)

    def per_feature(v, tiles):
        return pad_rows(v, tiles * P).reshape(tiles, P).T

    a = {k: np.asarray(v) for k, v in i.items()}
    A, B, F = "L0_attn_a_", "L0_attn_b_", "L0_ffn_"
    cols = np.concatenate([
        per_feature(a[A + "norm1_w"], FT), per_feature(a[A + "norm1_b"], FT),
        per_feature(a[A + "norm2_w"], FT), per_feature(a[A + "norm2_b"], FT),
        per_feature(a[B + "D"], FT), per_feature(a[B + "dt_proj_b"], FT),
        per_feature(a[F + "s_gate"], HT), per_feature(a[F + "s_up"], HT),
        a[B + "A_log"].reshape(FT, P, NS).transpose(1, 0, 2).reshape(P, FT * NS)], axis=1)
    return {
        "x": a[A + "x"].reshape(S, D),
        "w_qkvg": np.concatenate([a[A + "wq"], a[A + "wk"], a[A + "wv"], a[A + "wg"]], axis=1),
        "w_o": a[A + "wo"],
        "w_12": np.concatenate([pad_cols(a[A + "w1"], HP), pad_cols(a[A + "w2"], HP)], axis=1),
        "w_3": pad_rows(a[A + "w3"], HP),
        "w_gu": np.concatenate([pad_cols(a[F + "wq_gate"].T, HP), pad_cols(a[F + "wq_up"].T, HP)], axis=1),
        "w_dn": pad_rows(a[F + "wq_down"].T, HP),
        "w_xp": a[B + "x_proj_w"].T,
        "w_dt": a[B + "dt_proj_w"].T,
        "cols": cols,
        "s_down": a[F + "s_down"].reshape(D),
        "consts": shape_constants(),
    }


def kernel(**inputs):
    import concourse.bacc as bacc
    from concourse.bass_utils import run_bass_kernel_spmd

    nc = bacc.Bacc("TRN2", target_bir_lowering=False, num_devices=1)
    arrays, args = {}, []
    for name, a in host_layout(inputs).items():
        a = np.ascontiguousarray(a)
        arrays[name + "_dram"] = a
        args.append(nc.dram_tensor(name + "_dram", a.shape, mybir.dt.from_np(a.dtype), kind="ExternalInput").ap())
    args.append(nc.dram_tensor("out_dram", (S, D), F32, kind="ExternalOutput").ap())
    program(nc, *args)
    r = run_bass_kernel_spmd(nc, [arrays], core_ids=[0])
    return r.results[0]["out_dram"].reshape(1, S, D)
```

```python
from contextlib import ExitStack

import numpy as np

import concourse.bass as bass
from concourse import mybir

F32 = mybir.dt.float32
F32R = mybir.dt.float32r
BF16 = mybir.dt.bfloat16
I32 = mybir.dt.int32
ALU = mybir.AluOpType
ACT = mybir.ActivationFunctionType
AX_X = mybir.AxisListType.X

P = 128
S = 2048
D = 256
FT = D // P
T = 256
TT = T // P
CHUNKS = S // T
HEADS = 16
DH = D // HEADS
HID_A = 682
HID_Q = 704
HT = 6
HP = HT * P
PAIRS = HT // 2
NEWTON = 3
XPW = 2 * P
NS = 16
SP = NS // 2
DTR = 128
EPS = 1e-5
ZERO_POINT = 128.0

COLS = dict(n1w=(0, 2), n1b=(2, 4), n2w=(4, 6), n2b=(6, 8), dskip=(8, 10), dtb=(10, 12),
            sgate=(12, 18), sup=(18, 24), alog=(24, 56))
NCOLS = 56
CONSTS = dict(decay=(0, 2048), ident=(2048, 2176), qdecay=(2176, 2432), kdecay=(2432, 2688),
              headmask=(2688, 2816), even=(2816, 2817), odd=(2817, 2818), chunkdecay=(2818, 2820),
              select=(2820, 2852), half=(2852, 2856))
NCONST = 2856


RMAX = bass.bass_isa.ReduceOp.max


def shape_constants():
    c = np.zeros((P, NCONST), np.float64)
    gamma = (np.float32(1.0) - np.exp2(np.float32(-5.0) - np.arange(HEADS, dtype=np.float32))).astype(np.float64)
    t = np.arange(P)[:, None]
    s = np.arange(P)[None, :]
    for h in range(HEADS):
        c[:, h * P:(h + 1) * P] = np.where(s >= t, gamma[h] ** np.maximum(s - t, 0), 0.0)

    def put(name, a):
        lo, hi = CONSTS[name]
        c[:, lo:hi] = a

    row_head = np.arange(P) // DH
    put("ident", np.eye(P))
    put("qdecay", np.concatenate([gamma[row_head + 8 * f][:, None] ** (s + 1) for f in range(FT)], axis=1))
    put("kdecay", DH ** -0.5 * gamma[np.arange(D) // DH][None, :] ** (P - 1 - t))
    put("headmask", (row_head[:, None] == row_head[None, :]))
    put("even", (DH ** -0.5 * (row_head % 2 == 0))[:, None])
    put("odd", (DH ** -0.5 * (row_head % 2 == 1))[:, None])
    put("chunkdecay", np.stack([gamma[row_head + 8 * f] ** P for f in range(FT)], axis=1))
    put("select", (np.arange(P)[:, None] % 32 == np.arange(32)[None, :]) * (np.arange(P)[:, None] < 96))
    put("half", -0.5)
    return c.astype(np.float32)


class Norm:

    def __init__(self, name, sem, src, src_ready, nrm, bank, parts, small, gains=None, twice=None, keep=False):
        self.keep = keep or gains is not None
        self.src, self.src_ready, self.nrm, self.bank = src, src_ready, nrm, bank
        self.full, self.hi, self.lo = parts
        self.stats, self.mv, self.var, self.rstd = small
        self.gains, self.twice = gains, twice
        steps = ["stats", "aggr", "var", "rstd", "normed", "turned", "hi", "lo"]
        steps += ["full"] if self.keep else []
        steps += ["plain"] if twice is not None else []
        self.done = {what: sem(f"{name}_{what}") for what in steps}


class Ffn:

    def __init__(self, name, sem, norm, gu, down, banks, ybank, ring, res, out, gate_scale=None, hid_scale=None,
                 pool_add=False):
        self.norm, self.gu, self.down, self.banks, self.ybank = norm, gu, down, banks, ybank
        self.act, self.hi, self.lo = ring
        self.res, self.out, self.gate_scale, self.hid_scale, self.pool_add = res, out, gate_scale, hid_scale, pool_add
        steps = ["gu", "tanh", "gated", "hid", "hi", "lo", "down", "added"] + (["scaled"] if hid_scale is not None else [])
        self.done = {what: sem(f"{name}_{what}") for what in steps}


def program(nc, x, w_qkvg, w_o, w_12, w_3, w_gu, w_dn, w_xp, w_dt, cols, s_down, consts, out):
    x_view = x.rearrange("(n t p) d -> n p t d", p=P, t=TT)
    out_view = out.rearrange("(n t p) d -> n p t d", p=P, t=TT)

    with ExitStack() as ctx:
        sems = []

        def sb(name, shape, dt=F32, c=ctx):
            return c.enter_context(nc.sbuf_tensor(name, shape, dt))

        def sem(name):
            s = ctx.enter_context(nc.semaphore(name))
            sems.append(s)
            return s

        banks = [ctx.enter_context(nc.psum_tensor(f"bank{i}", [P, 512], F32)) for i in range(8)]

        def pair(name, shape):
            return sb(name + "_hi", shape, F32R), sb(name + "_lo", shape, F32R)

        qkvg = pair("qkvg", [P, FT, 4 * D])
        wo = pair("wo", [P, FT, D])
        w12 = pair("w12", [P, FT, 2 * HP])
        w3 = pair("w3", [P, HT, D])
        gu = pair("gu", [P, FT, 2 * HP])
        dn = pair("dn", [P, HT, D])
        xp = pair("xp", [P, FT, XPW])
        dtw = pair("dtw", [P, D])
        cst = sb("cst", [P, NCONST])
        col = sb("col", [P, NCOLS])
        sdrow = sb("sdrow", [P, D])
        select = sb("select", [96, 32], BF16)
        a_neg = sb("a_neg", [P, FT * NS])
        gate_half = sb("gate_half", [P, HT])
        hid_scale = sb("hid_scale", [P, HT])
        wide_ints = sb("wide_ints", [P, 4])
        wide_flag = sb("wide_flag", [P, 1], I32)
        retain = sb("retain", [P, TT, FT, P])
        hstate = sb("hstate", [P, NS, FT])

        def const(name):
            lo, hi = CONSTS[name]
            return cst[:, lo:hi]

        def column(name, j=None):
            lo, hi = COLS[name]
            return col[:, lo:hi] if j is None else col[:, lo + j:lo + j + 1]

        ident = const("ident")

        with ExitStack() as stage:
            def st(name, shape, dt=F32):
                return sb("raw_" + name, shape, dt, stage)

            loads = [
                ("qkvg", st("qkvg", [P, FT, 4 * D]), w_qkvg.rearrange("(k p) m -> p k m", p=P), qkvg),
                ("wo", st("wo", [P, FT, D]), w_o.rearrange("(k p) m -> p k m", p=P), wo),
                ("w12", st("w12", [P, FT, 2 * HP]), w_12.rearrange("(k p) m -> p k m", p=P), w12),
                ("w3", st("w3", [P, HT, D]), w_3.rearrange("(k p) m -> p k m", p=P), w3),
                ("gu", st("gu", [P, FT, 2 * HP], I32), w_gu.rearrange("(k p) m -> p k m", p=P), gu),
                ("dn", st("dn", [P, HT, D], I32), w_dn.rearrange("(k p) m -> p k m", p=P), dn),
                ("xp", st("xp", [P, FT, XPW]), w_xp.rearrange("(k p) m -> p k m", p=P), xp),
                ("dtw", st("dtw", [P, D]), w_dt, dtw),
            ]
            shifted = {"gu": st("gu_f", [P, FT, 2 * HP]), "dn": st("dn_f", [P, HT, D])}
            small_loaded = sem("small_loaded")
            loaded = {name: sem(f"{name}_loaded") for name, *_ in loads}
            part_hi = sem("part_hi")
            int_shifted = sem("int_shifted")
            halved = sem("halved")
            decay_exp = sem("decay_exp")
            part_lo, wide_seen, wide_spread = sem("part_lo"), sem("wide_seen"), sem("wide_spread")
            wide_any, wide_all = st("wide_any", [P, 1]), st("wide_all", [P, 1])

            with nc.Block() as block:
                @block.sync
                def _(sp):
                    sp.dma_start(cst[:], consts).then_inc(small_loaded, 16)
                    sp.dma_start(col[:], cols).then_inc(small_loaded, 16)
                    sp.dma_start(sdrow[:], s_down.partition_broadcast(P)).then_inc(small_loaded, 16)
                    for name, raw, src, _parts in loads:
                        sp.dma_start(raw[:], src).then_inc(loaded[name], 16)

                @block.scalar
                def _(act):
                    act.wait_ge(small_loaded, 48)
                    nc.scalar.activation(a_neg[:], column("alog"), ACT.Exp).then_inc(decay_exp, 1)

                @block.vector
                def _(dve):
                    nc.vector.memset(retain[:], 0.0)
                    nc.vector.memset(hstate[:], 0.0)
                    dve.wait_ge(small_loaded, 48)
                    nc.vector.tensor_copy(select[:], const("select")[0:96, :])
                    nc.vector.tensor_scalar(gate_half[:], column("sgate"), 0.5, None, ALU.mult).then_inc(halved, 1)
                    dve.wait_ge(halved, 1)
                    nc.vector.tensor_tensor(hid_scale[:], gate_half[:], column("sup"), ALU.mult)
                    dve.wait_ge(decay_exp, 1)
                    nc.vector.tensor_scalar(a_neg[:], a_neg[:], -1.0, None, ALU.mult)
                    ints = 0
                    for n, (name, raw, _src, (hi, lo)) in enumerate(loads):
                        dve.wait_ge(loaded[name], 16)
                        if name in shifted:
                            nc.vector.tensor_scalar(shifted[name][:], raw[:], -ZERO_POINT, None,
                                                    ALU.add).then_inc(int_shifted, 1)
                            ints += 1
                            dve.wait_ge(int_shifted, ints)
                            raw = shifted[name]
                        nc.vector.tensor_copy(hi[:], raw[:]).then_inc(part_hi, 1)
                        dve.wait_ge(part_hi, n + 1)
                        nc.vector.tensor_tensor(lo[:], raw[:], hi[:].bitcast(F32), ALU.subtract).then_inc(part_lo, 1)
                        if name in shifted:
                            dve.wait_ge(part_lo, n + 1)
                            flat = lo[:].bitcast(F32).rearrange("p a b -> p (a b)")
                            nc.vector.tensor_reduce(wide_ints[:, 2 * ints - 2:2 * ints - 1], flat, AX_X, ALU.max)
                            nc.vector.tensor_reduce(wide_ints[:, 2 * ints - 1:2 * ints], flat, AX_X,
                                                    ALU.min).then_inc(wide_seen, 1)
                    dve.wait_ge(wide_seen, 2)
                    nc.vector.tensor_scalar(wide_ints[:], wide_ints[:], 0.0, None, ALU.not_equal).then_inc(wide_seen, 1)
                    dve.wait_ge(wide_seen, 3)
                    nc.vector.tensor_reduce(wide_any[:], wide_ints[:], AX_X, ALU.max).then_inc(wide_seen, 1)
                    dve.wait_ge(wide_spread, 1)
                    nc.vector.tensor_copy(wide_flag[:], wide_all[:])

                @block.gpsimd
                def _(pool):
                    pool.wait_ge(wide_seen, 4)
                    nc.gpsimd.partition_all_reduce(wide_all[:], wide_any[:], P, RMAX).then_inc(wide_spread, 1)

        def small(name, kinds=1):
            return (sb(name + "_stats", [P, TT, 6]), sb(name + "_mv", [P, TT, 2]),
                    sb(name + "_var", [P, kinds * TT]), sb(name + "_rstd", [P, kinds * TT]))

        def parts(name):
            return sb(name, [P, FT, T]), sb(name + "_hi", [P, FT, T], F32R), sb(name + "_lo", [P, FT, T], F32R)

        def ring(name, c):
            return (sb(name + "_act", [P, 2, 2, T], F32, c), sb(name + "_hi", [P, 2, 2, T], F32R, c),
                    sb(name + "_lo", [P, 2, 2, T], F32R, c))

        xin = sb("xin", [P, TT, D])
        xres = sb("xres", [P, TT, D])
        nrm = sb("nrm", [P, TT, D])
        xn = sb("xn", [P, TT, D])
        hT = parts("hT")
        small_front = small("front")
        small_twice = small("twice", 2)
        with ExitStack() as only_attn:
            q_hi = sb("q_hi", [P, FT, TT, 2, P], F32R, only_attn)
            q_lo = sb("q_lo", [P, FT, TT, 2, P], F32R, only_attn)
            qTd = sb("qTd", [P, FT, T], F32, only_attn)
            k_hi = sb("k_hi", [P, FT, T], F32R, only_attn)
            k_lo = sb("k_lo", [P, FT, T], F32R, only_attn)
            kdec = sb("kdec", [P, TT, D], F32, only_attn)
            vtok = sb("vtok", [P, TT, D], F32, only_attn)
            kvmask = sb("kvmask", [P, TT, FT, P], F32, only_attn)
            probs = sb("probs", [P, 3, 512], F32, only_attn)
            gated = sb("gated", [P, TT, D], F32, only_attn)
            squares = sb("squares", [P, TT, D], F32, only_attn)
            rmean = sb("rmean", [P, TT * HEADS], F32, only_attn)
            rvar = sb("rvar", [P, TT * HEADS], F32, only_attn)
            rstd = sb("ret_rstd", [P, TT * HEADS], F32, only_attn)
        centred = kdec
        with ExitStack() as only_ffn:
            front_ring = ring("front_ring", only_ffn)
        sb("front_shared", [P, 15 * 512 + 3 * TT * HEADS])

        xback = sb("xback", [P, TT, D])
        nrm_b = sb("nrm_b", [P, TT, D])
        uT = parts("uT")
        small_back = small("back")
        yscan = sb("yscan", [P, FT, T])
        with ExitStack() as only_ffn:
            back_ring = ring("back_ring", only_ffn)
        delta = sb("delta", [P, FT, T])
        du = sb("du", [P, FT, T])
        dr_hi = sb("dr_hi", [P, T], F32R)
        dr_lo = sb("dr_lo", [P, T], F32R)
        bc_full = sb("bc_full", [32, 2, T])
        bc_parts = sb("bc_parts", [96, T], BF16)
        rep = sb("rep", [P, 2, 2, 2, T])
        dA = sb("dA", [P, 2, 2, FT, T])
        hbuf = sb("hbuf", [P, 3, 2, FT, T])

        sems.clear()
        x_in, x_next, x_out, x_taken = sem("x_in"), sem("x_next"), sem("x_out"), sem("x_taken")
        z_added, xz_added, x3_added = sem("z_added"), sem("xz_added"), sem("x3_added")

        n1 = Norm("n1", sem, xin, None, nrm, 0, hT, small_twice, gains=("n1w", "n1b"), twice=xn)
        n2 = Norm("n2", sem, xn, (z_added, 1), nrm, 4, hT, small_front, gains=("n2w", "n2b"))
        f1 = Ffn("f1", sem, n2, w12, w3, ((0, 1), (2, 3)), 4, front_ring, xres, xres)
        n3 = Norm("n3", sem, xres, (f1.done["added"], 1), nrm, 4, hT, small_front)
        f2 = Ffn("f2", sem, n3, gu, dn, ((0, 1), (2, 3)), 4, front_ring, xres, xres, gate_half, hid_scale)
        n4 = Norm("n4", sem, xres, None, nrm_b, 5, uT, small_back, keep=True)
        n5 = Norm("n5", sem, xback, (x3_added, 1), nrm_b, 6, uT, small_back)
        f3 = Ffn("f3", sem, n5, gu, dn, ((5, 6),), 7, back_ring, xback, xback, gate_half, hid_scale)

        q_turned, q_rounded, q_parted, q_decayed = sem("q_turned"), sem("q_rounded"), sem("q_parted"), sem("q_decayed")
        k_turned, k_rounded, k_parted = sem("k_turned"), sem("k_rounded"), sem("k_parted")
        kv_made, k_decayed, v_copied = sem("kv_made"), sem("k_decayed"), sem("v_copied")
        g_made, g_tanh, g_gated = sem("g_made"), sem("g_tanh"), sem("g_gated")
        outer_made, outer_masked, state_ready = sem("outer_made"), sem("outer_masked"), sem("state_ready")
        scores_made, probs_made, probs_used = sem("scores_made"), sem("probs_made"), sem("probs_used")
        ret_mean, ret_centred = sem("ret_mean"), sem("ret_centred")
        ret_squared, ret_var, ret_root = sem("ret_squared"), sem("ret_var"), sem("ret_root")
        g_scaled, ret_gated = sem("g_scaled"), sem("ret_gated")
        yt_turned, yt_hi, yt_lo, y_projected = sem("yt_turned"), sem("yt_hi"), sem("yt_lo"), sem("y_projected")

        drbc_made, drh_made, drl_made = sem("drbc_made"), sem("drh_made"), sem("drl_made")
        bc_copied, bc_part = sem("bc_copied"), sem("bc_part")
        dt_made, dt_abs, dt_exp, dt_ln, dt_pos = sem("dt_made"), sem("dt_abs"), sem("dt_exp"), sem("dt_ln"), sem("dt_pos")
        delta_made, du_made = sem("delta_made"), sem("du_made")
        rep_made, rep_copied = sem("rep_made"), sem("rep_copied")
        decay_made, dbu_made, scanned, saved, outs_made, y_added = (
            sem("decay_made"), sem("dbu_made"), sem("scanned"), sem("saved"), sem("outs_made"), sem("y_added"))
        y_skipped, pair_summed, y_back = sem("y_skipped"), sem("pair_summed"), sem("y_back")

        def products(acc, sta, mov, start, stop, skip=False):
            terms = []
            for (sh, sl), (mh, ml) in zip(sta, mov):
                terms += [(sh, mh), (sh, ml), (sl, mh)]
            terms = [(a, b) for a, b in terms if a is not None and b is not None]
            for n, (a, b) in enumerate(terms):
                last = nc.tensor.matmul(acc, a, b, start=start and n == 0, stop=stop and n == len(terms) - 1,
                                        skip_group_check=skip)
            return last

        def cut(pair_, *at, low=True):
            return pair_[0][at], pair_[1][at] if low else None

        ALL = slice(None)

        def pe_norm_turn(pe, n):
            for ft in range(FT):
                for tt in range(TT):
                    if ft == 0:
                        pe.wait_ge(n.done["normed"], tt + 1)
                    last = nc.tensor.transpose(banks[n.bank][:, ft * T + tt * P:ft * T + (tt + 1) * P],
                                               n.nrm[:, tt, ft * P:(ft + 1) * P], ident)
            last.then_inc(n.done["turned"], 1)

        def pe_gate_up(pe, f, p, low):
            if p == 0:
                pe.wait_ge(f.norm.done["lo"], 1)
            if p >= len(f.banks):
                pe.wait_ge(f.done["hid"], p - len(f.banks) + 1)
            for half, bank in enumerate(f.banks[p % len(f.banks)]):
                for i in range(2):
                    c = half * HP + (2 * p + i) * P
                    sta = [cut(f.gu, ALL, k, slice(c, c + P), low=low) for k in range(FT)]
                    mov = [(f.norm.hi[:, k, :], f.norm.lo[:, k, :]) for k in range(FT)]
                    last = products(banks[bank][:, i * T:(i + 1) * T], sta, mov, True, True)
            last.then_inc(f.done["gu"], 1)

        def pe_down(pe, f, p, low):
            pe.wait_ge(f.done["lo"], p + 1)
            for tt in range(TT):
                t = slice(tt * P, (tt + 1) * P)
                acc = banks[f.ybank][:, tt * D:(tt + 1) * D]
                last = products(acc, [(f.hi[:, p % 2, i, t], f.lo[:, p % 2, i, t]) for i in range(2)],
                                [cut(f.down, ALL, 2 * p + i, ALL, low=low) for i in range(2)],
                                p == 0 and tt == 0, p == PAIRS - 1, skip=True)
            last.then_inc(f.done["down"], 1)

        def pe_queries_keys(pe):
            pe.wait_ge(n1.done["lo"], 1)
            hp = [(n1.hi[:, k, :], n1.lo[:, k, :]) for k in range(FT)]
            for which, (bank, done) in enumerate(((1, q_turned), (2, k_turned))):
                for ft in range(FT):
                    m = slice(which * D + ft * P, which * D + (ft + 1) * P)
                    last = products(banks[bank][:, ft * T:(ft + 1) * T], [cut(qkvg, ALL, k, m) for k in range(FT)],
                                    hp, True, True)
                last.then_inc(done, 1)

        def pe_keys_values(pe, tt):
            sta = [(n1.hi[:, k, tt * P:(tt + 1) * P], n1.lo[:, k, tt * P:(tt + 1) * P]) for k in range(FT)]
            products(banks[3 + tt][:], sta, [cut(qkvg, ALL, k, slice(D, 3 * D)) for k in range(FT)],
                     True, True).then_inc(kv_made, 1)

        def pe_gates(pe):
            for tt in range(TT):
                sta = [(n1.hi[:, k, tt * P:(tt + 1) * P], n1.lo[:, k, tt * P:(tt + 1) * P]) for k in range(FT)]
                last = products(banks[0][:, tt * D:(tt + 1) * D], sta,
                                [cut(qkvg, ALL, k, slice(3 * D, 4 * D)) for k in range(FT)], True, True)
            last.then_inc(g_made, 1)

        def pe_outer(pe):
            pe.wait_ge(q_parted, 2)
            for tt in range(TT):
                pe.wait_ge(k_decayed, tt + 1)
                for f in range(FT):
                    c = (tt * FT + f) * P
                    last = nc.tensor.matmul(banks[1][:, c:c + P], kdec[:, tt, f * P:(f + 1) * P],
                                            vtok[:, tt, f * P:(f + 1) * P], start=True, stop=True)
            last.then_inc(outer_made, 1)

        def pe_score(pe, u):
            f, rg = u // 4, u % 4
            if u == 0:
                pe.wait_ge(q_parted, 2)
                pe.wait_ge(k_parted, 1)
                pe.wait_ge(k_decayed, 2)
                pe.wait_ge(g_gated, 1)
            if u >= 3:
                pe.wait_ge(probs_made, u - 2)
            bank = banks[(2, 4, 0)[u % 3]]
            rows = slice(32 * rg, 32 * rg + 32)
            for c in range(TT):
                tok = slice(c * P, (c + 1) * P)
                last = products(bank[:, c * 2 * P:(c + 1) * 2 * P], [(k_hi[rows, f, tok], k_lo[rows, f, tok])],
                                [(q_hi[rows, f, c], q_lo[rows, f, c])], True, True)
            last.then_inc(scores_made, 1)

        def pe_value(pe, u):
            f, rg = u // 4, u % 4
            if u == 0:
                pe.wait_ge(outer_masked, 1)
                for c in range(TT):
                    if c:
                        pe.wait_ge(state_ready, c)
                    tok = slice(c * P, (c + 1) * P)
                    for g in range(FT):
                        last = nc.tensor.matmul(banks[3][:, c * D + g * P:c * D + (g + 1) * P], qTd[:, g, tok],
                                                retain[:, c, g, :], start=(c == 0 and g == 0), stop=False,
                                                skip_group_check=True)
            pe.wait_ge(probs_made, u + 1)
            for c in range(TT):
                for par in range(2):
                    h = f * 8 + rg * 2 + par
                    o = (c * 2 + par) * P
                    last = nc.tensor.matmul(banks[3][:, c * D + h * DH:c * D + (h + 1) * DH],
                                            probs[:, u % 3, o:o + P], vtok[:, c, h * DH:(h + 1) * DH],
                                            start=False, stop=True, skip_group_check=True)
            last.then_inc(probs_used, 1)

        def pe_ret_turn(pe):
            pe.wait_ge(ret_gated, 1)
            for ft in range(FT):
                for tt in range(TT):
                    c = ft * T + tt * P
                    last = nc.tensor.transpose(banks[1][:, c:c + P], gated[:, tt, ft * P:(ft + 1) * P], ident)
            last.then_inc(yt_turned, 1)

        def pe_project(pe):
            pe.wait_ge(yt_lo, 1)
            for tt in range(TT):
                t = slice(tt * P, (tt + 1) * P)
                last = products(banks[3][:, tt * D:(tt + 1) * D], [(hT[1][:, k, t], hT[2][:, k, t]) for k in range(FT)],
                                [cut(wo, ALL, k, ALL) for k in range(FT)], True, True)
            last.then_inc(y_projected, 1)

        def pe_state_inputs(pe):
            pe.wait_ge(n4.done["lo"], 1)
            for i in range(2):
                last = products(banks[6][:, i * T:(i + 1) * T], [cut(xp, ALL, k, slice(i * P, (i + 1) * P)) for k in range(FT)],
                                [(n4.hi[:, k, :], n4.lo[:, k, :]) for k in range(FT)], True, True)
            last.then_inc(drbc_made, 1)

        def pe_steps_size(pe):
            pe.wait_ge(drl_made, 1)
            for ft in range(FT):
                last = products(banks[7][:, ft * T:(ft + 1) * T], [cut(dtw, ALL, slice(ft * P, (ft + 1) * P))],
                                [(dr_hi[:], dr_lo[:])], True, True)
            last.then_inc(dt_made, 1)

        def pe_spread(pe, sp):
            if sp == 0:
                pe.wait_ge(bc_part, 5)
            for i in range(2):
                if sp:
                    pe.wait_ge(rep_copied, 2 * sp - 1 + i)
                for which in range(2):
                    row = which * NS + 2 * sp + i
                    last = nc.tensor.matmul(banks[5 + i][:, which * T:(which + 1) * T],
                                            select[:, row:row + 1].to_broadcast([96, P]), bc_parts[:],
                                            start=True, stop=True)
                last.then_inc(rep_made, 1)

        def pe_scan_back(pe):
            pe.wait_ge(rep_copied, NS)
            pe.wait_ge(y_added, SP)
            for tt in range(TT):
                for ft in range(FT):
                    c = tt * D + ft * P
                    last = nc.tensor.transpose(banks[5][:, c:c + P], yscan[:, ft, tt * P:(tt + 1) * P], ident)
            last.then_inc(y_back, 1)

        def act_take(act):
            nc.scalar.activation(xback[:], xres[:], ACT.Copy).then_inc(x_taken, 1)

        def act_norm_turn(act, n):
            act.wait_ge(n.done["turned"], 1)
            bank = banks[n.bank]
            if n.gains:
                for ft in range(FT):
                    last = nc.scalar.activation(n.full[:, ft, :], bank[:, ft * T:(ft + 1) * T], ACT.Identity,
                                                bias=column(n.gains[1], ft), scale=column(n.gains[0], ft))
                last.then_inc(n.done["full"], 1)
            elif n.keep:
                nc.scalar.activation(n.full[:].rearrange("p f t -> p (f t)"), bank[:], ACT.Copy).then_inc(n.done["full"], 1)
            else:
                nc.scalar.activation(n.hi[:].rearrange("p f t -> p (f t)"), bank[:], ACT.Copy).then_inc(n.done["hi"], 1)

        def act_gate_up(act, f, p):
            act.wait_ge(f.done["gu"], p + 1)
            if p >= 2:
                act.wait_ge(f.done["lo"], p - 1)
            bank = banks[f.banks[p % len(f.banks)][0]]
            if f.gate_scale is None:
                nc.scalar.activation(f.act[:, p % 2, :, :].rearrange("p i t -> p (i t)"), bank[:], ACT.Tanh,
                                     scale=0.5).then_inc(f.done["tanh"], 1)
            else:
                for i in range(2):
                    j = 2 * p + i
                    last = nc.scalar.activation(f.act[:, p % 2, i, :], bank[:, i * T:(i + 1) * T], ACT.Tanh,
                                                scale=f.gate_scale[:, j:j + 1])
                last.then_inc(f.done["tanh"], 1)

        def act_split(act, f, p):
            act.wait_ge(f.done["hid"], p + 1)
            if p >= 2:
                act.wait_ge(f.done["down"], p - 1)
            nc.scalar.activation(f.hi[:, p % 2], f.act[:, p % 2], ACT.Copy).then_inc(f.done["hi"], 1)

        def act_queries_keys(act):
            act.wait_ge(q_turned, 1)
            for par, name in enumerate(("even", "odd")):
                nc.scalar.activation(q_hi[:, :, :, par, :], banks[1][:].rearrange("p (f t s) -> p f t s", f=FT, t=TT),
                                     ACT.Copy, scale=const(name)).then_inc(q_rounded, 1)
            act.wait_ge(k_turned, 1)
            nc.scalar.activation(k_hi[:].rearrange("p f t -> p (f t)"), banks[2][:], ACT.Copy).then_inc(k_rounded, 1)

        def act_keys_values(act, tt):
            act.wait_ge(kv_made, tt + 1)
            nc.scalar.activation(vtok[:, tt, :], banks[3 + tt][:, D:2 * D], ACT.Copy).then_inc(v_copied, 1)

        def act_gates(act):
            act.wait_ge(g_made, 1)
            nc.scalar.activation(gated[:].rearrange("p t d -> p (t d)"), banks[0][:], ACT.Tanh,
                                 scale=0.5).then_inc(g_tanh, 1)

        def act_group_norm(act):
            act.wait_ge(ret_centred, 1)
            nc.scalar.activation(squares[:], centred[:], ACT.Square).then_inc(ret_squared, 1)

        def act_ret_turn(act):
            act.wait_ge(yt_turned, 1)
            nc.scalar.activation(hT[1][:].rearrange("p f t -> p (f t)"), banks[1][:], ACT.Copy).then_inc(yt_hi, 1)

        def act_state_inputs(act):
            act.wait_ge(drbc_made, 1)
            nc.scalar.activation(dr_hi[:], banks[6][:, 0:T], ACT.Copy).then_inc(drh_made, 1)
            nc.scalar.activation(bc_full[:, 0, :], banks[6][0:32, T:2 * T], ACT.Copy).then_inc(bc_copied, 1)

        def act_steps_size(act):
            act.wait_ge(dt_made, 1)
            for ft in range(FT):
                nc.scalar.activation(delta[:, ft, :], banks[7][:, ft * T:(ft + 1) * T], ACT.Abs,
                                     bias=column("dtb", ft)).then_inc(dt_abs, 1)
            act.wait_ge(dt_abs, FT)
            nc.scalar.activation(delta[:], delta[:], ACT.Exp, scale=-1.0).then_inc(dt_exp, 1)
            act.wait_ge(dt_exp, 1)
            nc.scalar.activation(delta[:], delta[:], ACT.Ln, bias=1.0).then_inc(dt_ln, 1)

        def act_spread(act, sp):
            for i in range(2):
                act.wait_ge(rep_made, 2 * sp + i + 1)
                if sp >= 2 and i == 0:
                    act.wait_ge(dbu_made, sp - 1)
                    act.wait_ge(outs_made, sp - 1)
                nc.scalar.activation(rep[:, sp % 2, i].rearrange("p w t -> p (w t)"), banks[5 + i][:],
                                     ACT.Copy).then_inc(rep_copied, 1)
            if sp == 0:
                act.wait_ge(delta_made, 1)
            if sp >= 2:
                act.wait_ge(scanned, 4 * (sp - 1))
            for i in range(2):
                for ft in range(FT):
                    c = ft * NS + 2 * sp + i
                    nc.scalar.activation(dA[:, sp % 2, i, ft, :], delta[:, ft, :], ACT.Exp,
                                         scale=a_neg[:, c:c + 1]).then_inc(decay_made, 1)

        def dve_norm_stats(dve, n):
            if n.src_ready:
                dve.wait_ge(*n.src_ready)
            for tt in range(TT):
                nc.vector.bn_stats(n.stats[:, tt, :], n.src[:, tt, :]).then_inc(n.done["stats"], 1)
            for tt in range(TT):
                dve.wait_ge(n.done["stats"], tt + 1)
                nc.vector.bn_aggr(n.mv[:, tt, :], n.stats[:, tt, :]).then_inc(n.done["aggr"], 1)
            dve.wait_ge(n.done["aggr"], TT)
            nc.vector.tensor_scalar(n.var[:, 0:TT], n.mv[:, :, 1], EPS, None, ALU.add).then_inc(n.done["var"], 1)
            if n.twice is not None:
                nc.vector.tensor_scalar(n.var[:, TT:2 * TT], n.mv[:, :, 1], 1.0 + EPS, EPS * EPS, ALU.mult,
                                        ALU.add).then_inc(n.done["var"], 1)

        def dve_norm_apply(dve, n):
            dve.wait_ge(n.done["rstd"], 1)
            first = TT if n.twice is not None else 0
            for tt in range(TT):
                nc.vector.tensor_scalar(n.nrm[:, tt, :], n.src[:, tt, :], n.mv[:, tt, 0:1],
                                        n.rstd[:, first + tt:first + tt + 1],
                                        ALU.subtract, ALU.mult).then_inc(n.done["normed"], 1)
            if n.twice is not None:
                for tt in range(TT):
                    nc.vector.tensor_scalar(n.twice[:, tt, :], n.src[:, tt, :], n.mv[:, tt, 0:1], n.rstd[:, tt:tt + 1],
                                            ALU.subtract, ALU.mult).then_inc(n.done["plain"], 1)

        def dve_norm_split(dve, n):
            if n.keep:
                dve.wait_ge(n.done["full"], 1)
                nc.vector.tensor_copy(n.hi[:], n.full[:]).then_inc(n.done["hi"], 1)
            else:
                dve.wait_ge(n.done["hi"], 1)
                nc.vector.tensor_tensor(n.lo[:].rearrange("p f t -> p (f t)"), banks[n.bank][:],
                                        n.hi[:].bitcast(F32).rearrange("p f t -> p (f t)"),
                                        ALU.subtract).then_inc(n.done["lo"], 1)

        def dve_gate_up(dve, f, p):
            g, u = f.banks[p % len(f.banks)]
            a = f.act[:, p % 2].rearrange("p i t -> p (i t)")
            dve.wait_ge(f.done["tanh"], p + 1)
            nc.vector.scalar_tensor_tensor(a, a, 1.0, banks[g][:], ALU.add, ALU.mult).then_inc(f.done["gated"], 1)
            dve.wait_ge(f.done["gated"], p + 1)
            if f.hid_scale is None:
                nc.vector.scalar_tensor_tensor(a, a, 0.5, banks[u][:], ALU.mult, ALU.mult).then_inc(f.done["hid"], 1)
            else:
                for i in range(2):
                    j = 2 * p + i
                    last = nc.vector.scalar_tensor_tensor(f.act[:, p % 2, i, :], f.act[:, p % 2, i, :],
                                                          f.hid_scale[:, j:j + 1], banks[u][:, i * T:(i + 1) * T],
                                                          ALU.mult, ALU.mult)
                last.then_inc(f.done["hid"], 1)

        def dve_ffn_end(dve, f):
            dve.wait_ge(f.done["down"], PAIRS)
            y = banks[f.ybank][:].rearrange("p (t d) -> p t d", t=TT)
            if f.hid_scale is None:
                dve.wait_ge(xz_added, 1)
                nc.vector.tensor_tensor(f.out[:], f.res[:], y, ALU.add).then_inc(f.done["added"], 1)
            else:
                tmp = f.norm.nrm
                nc.vector.tensor_tensor(tmp[:], y, sdrow[:].unsqueeze(1).to_broadcast([P, TT, D]),
                                        ALU.mult).then_inc(f.done["scaled"], 1)
                if not f.pool_add:
                    dve.wait_ge(f.done["scaled"], 1)
                    nc.vector.tensor_tensor(f.out[:], f.res[:], tmp[:], ALU.add).then_inc(f.done["added"], 1)

        def dve_queries_keys(dve):
            dve.wait_ge(q_rounded, 2)
            table = const("qdecay").rearrange("p (f s) -> p f s", f=FT).unsqueeze(2).to_broadcast([P, FT, TT, P])
            nc.vector.tensor_tensor(qTd[:].rearrange("p f (t s) -> p f t s", t=TT),
                                    banks[1][:].rearrange("p (f t s) -> p f t s", f=FT, t=TT), table,
                                    ALU.mult).then_inc(q_decayed, 1)
            for par, name in enumerate(("even", "odd")):
                nc.vector.scalar_tensor_tensor(q_lo[:, :, :, par, :],
                                               banks[1][:].rearrange("p (f t s) -> p f t s", f=FT, t=TT), const(name),
                                               q_hi[:, :, :, par, :].bitcast(F32), ALU.mult,
                                               ALU.subtract).then_inc(q_parted, 1)
            dve.wait_ge(k_rounded, 1)
            nc.vector.tensor_tensor(k_lo[:].rearrange("p f t -> p (f t)"), banks[2][:],
                                    k_hi[:].bitcast(F32).rearrange("p f t -> p (f t)"), ALU.subtract).then_inc(k_parted, 1)

        def dve_keys_values(dve, tt):
            dve.wait_ge(v_copied, tt + 1)
            nc.vector.tensor_tensor(kdec[:, tt, :], banks[3 + tt][:, 0:D], const("kdecay"),
                                    ALU.mult).then_inc(k_decayed, 1)

        def dve_gates(dve):
            dve.wait_ge(g_tanh, 1)
            nc.vector.scalar_tensor_tensor(gated[:].rearrange("p t d -> p (t d)"), gated[:].rearrange("p t d -> p (t d)"),
                                           1.0, banks[0][:], ALU.add, ALU.mult).then_inc(g_gated, 1)

        def dve_outer(dve):
            mask = const("headmask").unsqueeze(1).to_broadcast([P, TT * FT, P])
            dve.wait_ge(outer_made, 1)
            nc.vector.tensor_tensor(kvmask[:].rearrange("p t f e -> p (t f) e"),
                                    banks[1][:].rearrange("p (g e) -> p g e", e=P), mask,
                                    ALU.mult).then_inc(outer_masked, 1)
            dve.wait_ge(outer_masked, 1)
            dve_carry(dve, 0)

        def dve_carry(dve, c):
            if c == TT - 1:
                dve.wait_ge(probs_used, 1)
                dve.wait_ge(state_ready, c)
            for f in range(FT):
                last = nc.vector.scalar_tensor_tensor(retain[:, (c + 1) % TT, f, :], retain[:, c, f, :],
                                                      const("chunkdecay")[:, f:f + 1], kvmask[:, c, f, :],
                                                      ALU.mult, ALU.add)
            last.then_inc(state_ready, 1)

        def dve_score(dve, u):
            f, rg = u // 4, u % 4
            dve.wait_ge(scores_made, u + 1)
            if u >= 3:
                dve.wait_ge(probs_used, u - 2)
            h = f * 8 + rg * 2
            table = cst[:, h * P:(h + 2) * P].rearrange("p (h s) -> p h s", h=2)
            src = banks[(2, 4, 0)[u % 3]][:].rearrange("p (c h s) -> p c h s", c=TT, h=2)
            dst = probs[:, u % 3, :].rearrange("p (c h s) -> p c h s", c=TT, h=2)
            nc.vector.tensor_tensor(dst, src, table.unsqueeze(1).to_broadcast([P, TT, 2, P]),
                                    ALU.mult).then_inc(probs_made, 1)
            if u == 4:
                dve_carry(dve, TT - 1)

        def dve_group_norm(dve):
            dve.wait_ge(probs_used, 8)
            ret = banks[3][:].rearrange("p (g e) -> p g e", e=DH)
            nc.vector.tensor_reduce(rmean[:], ret, AX_X, ALU.add).then_inc(ret_mean, 1)
            dve.wait_ge(ret_mean, 1)
            nc.vector.tensor_scalar(rmean[:], rmean[:], 1.0 / DH, None, ALU.mult).then_inc(ret_mean, 1)
            dve.wait_ge(ret_mean, 2)
            cen = centred[:].rearrange("p t (h e) -> p (t h) e", e=DH)
            nc.vector.tensor_tensor(cen, ret, rmean[:].unsqueeze(2).to_broadcast([P, TT * HEADS, DH]),
                                    ALU.subtract).then_inc(ret_centred, 1)

        def dve_group_gate(dve):
            dve.wait_ge(ret_centred, 1)
            nc.vector.scalar_tensor_tensor(gated[:], gated[:], 0.5, centred[:], ALU.mult,
                                           ALU.mult).then_inc(g_scaled, 1)
            dve.wait_ge(ret_squared, 1)
            nc.vector.tensor_reduce(rvar[:], squares[:].rearrange("p t (h e) -> p (t h) e", e=DH),
                                    AX_X, ALU.add).then_inc(ret_var, 1)
            dve.wait_ge(ret_var, 1)
            nc.vector.tensor_scalar(rvar[:], rvar[:], 1.0 / DH, EPS, ALU.mult, ALU.add).then_inc(ret_var, 1)
            dve.wait_ge(ret_var, 2)
            nc.vector.tensor_scalar(rstd[:].bitcast(I32), rvar[:].bitcast(I32), 1, None,
                                    ALU.logical_shift_right).then_inc(ret_root, 1)
            dve.wait_ge(ret_root, 1)
            nc.vector.tensor_scalar(rstd[:].bitcast(I32), rstd[:].bitcast(I32), -1.0, float(0x5F3759DF), ALU.mult,
                                    ALU.add).then_inc(ret_root, 1)
            for step in range(NEWTON):
                dve.wait_ge(ret_root, 3 * step + 2)
                nc.vector.tensor_tensor(rmean[:], rstd[:], rstd[:], ALU.mult).then_inc(ret_root, 1)
                dve.wait_ge(ret_root, 3 * step + 3)
                nc.vector.scalar_tensor_tensor(rmean[:], rmean[:], -0.5, rvar[:], ALU.mult,
                                               ALU.mult).then_inc(ret_root, 1)
                dve.wait_ge(ret_root, 3 * step + 4)
                nc.vector.scalar_tensor_tensor(rstd[:], rmean[:], 1.5, rstd[:], ALU.add,
                                               ALU.mult).then_inc(ret_root, 1)

        def dve_group_scale(dve):
            dve.wait_ge(g_scaled, 1)
            dve.wait_ge(ret_root, 3 * NEWTON + 2)
            gat = gated[:].rearrange("p t (h e) -> p (t h) e", e=DH)
            nc.vector.tensor_tensor(gat, gat, rstd[:].unsqueeze(2).to_broadcast([P, TT * HEADS, DH]),
                                    ALU.mult).then_inc(ret_gated, 1)

        def dve_ret_split(dve):
            dve.wait_ge(yt_hi, 1)
            nc.vector.tensor_tensor(hT[2][:].rearrange("p f t -> p (f t)"), banks[1][:],
                                    hT[1][:].bitcast(F32).rearrange("p f t -> p (f t)"), ALU.subtract).then_inc(yt_lo, 1)

        def dve_project(dve):
            dve.wait_ge(n1.done["plain"], TT)
            dve.wait_ge(y_projected, 1)
            nc.vector.tensor_tensor(xn[:], xn[:], banks[3][:].rearrange("p (t d) -> p t d", t=TT),
                                    ALU.add).then_inc(z_added, 1)

        def dve_state_inputs(dve):
            dve.wait_ge(drh_made, 1)
            dve.wait_ge(bc_copied, 1)
            nc.vector.tensor_tensor(dr_lo[:], banks[6][:, 0:T], dr_hi[:].bitcast(F32), ALU.subtract).then_inc(drl_made, 1)
            for part in range(3):
                here = bc_parts[32 * part:32 * part + 32, :]
                nc.vector.tensor_copy(here, bc_full[:, part % 2, :]).then_inc(bc_part, 1)
                if part < 2:
                    dve.wait_ge(bc_part, 2 * part + 1)
                    nc.vector.tensor_tensor(bc_full[:, (part + 1) % 2, :], bc_full[:, part, :], here,
                                            ALU.subtract).then_inc(bc_part, 1)
                    dve.wait_ge(bc_part, 2 * part + 2)

        def dve_steps_size(dve):
            dve.wait_ge(dt_abs, FT)
            for ft in range(FT):
                last = nc.vector.tensor_scalar(du[:, ft, :], banks[7][:, ft * T:(ft + 1) * T], column("dtb", ft), 0.0,
                                               ALU.add, ALU.max)
            last.then_inc(dt_pos, 1)

        def dve_steps_end(dve):
            dve.wait_ge(dt_pos, 1)
            dve.wait_ge(dt_ln, 1)
            nc.vector.tensor_tensor(delta[:], delta[:], du[:], ALU.add).then_inc(delta_made, 1)
            dve.wait_ge(delta_made, 1)
            nc.vector.tensor_tensor(du[:], delta[:], n4.full[:], ALU.mult).then_inc(du_made, 1)

        def dve_spread(dve, sp):
            if sp == 0:
                dve.wait_ge(du_made, 1)
            dve.wait_ge(rep_copied, 2 * sp + 2)
            if sp >= 3:
                dve.wait_ge(y_added, sp - 2)
            nc.vector.tensor_tensor(hbuf[:, sp % 3], du[:].unsqueeze(1).to_broadcast([P, 2, FT, T]),
                                    rep[:, sp % 2, :, 0, :].unsqueeze(2).to_broadcast([P, 2, FT, T]),
                                    ALU.mult).then_inc(dbu_made, 1)

        def dve_scan(dve, sp):
            dve.wait_ge(dbu_made, sp + 1)
            for i in range(2):
                for ft in range(FT):
                    n = 2 * sp + i
                    dve.wait_ge(decay_made, 4 * sp + 2 * i + ft + 1)
                    h = hbuf[:, sp % 3, i, ft, :]
                    nc.vector.tensor_tensor_scan(h, dA[:, sp % 2, i, ft, :], h, hstate[:, n, ft:ft + 1],
                                                 ALU.mult, ALU.add).then_inc(scanned, 1)

        def dve_scan_skip(dve):
            for ft in range(FT):
                last = nc.vector.tensor_scalar(yscan[:, ft, :], n4.full[:, ft, :], column("dskip", ft), None, ALU.mult)
            last.then_inc(y_skipped, 1)

        def dve_collect(dve, sp):
            dve.wait_ge(pair_summed, sp + 1)
            if sp == 0:
                dve.wait_ge(y_skipped, 1)
            else:
                dve.wait_ge(y_added, sp)
            nc.vector.tensor_tensor(yscan[:], yscan[:], hbuf[:, sp % 3, 0], ALU.add).then_inc(y_added, 1)

        def dve_scan_back(dve):
            dve.wait_ge(y_back, 1)
            dve.wait_ge(x_taken, 1)
            nc.vector.tensor_tensor(xback[:], xback[:], banks[5][:].rearrange("p (t d) -> p t d", t=TT),
                                    ALU.add).then_inc(x3_added, 1)

        def pool_norm_stats(pool, n):
            pool.wait_ge(n.done["var"], 2 if n.twice is not None else 1)
            nc.gpsimd.tensor_tensor(n.rstd[:], n.var[:], const("half")[:, 0:n.var.shape[1]],
                                    ALU.pow).then_inc(n.done["rstd"], 1)

        def pool_norm_split(pool, n):
            if not n.keep:
                return
            pool.wait_ge(n.done["hi"], 1)
            nc.gpsimd.tensor_tensor(n.lo[:], n.full[:], n.hi[:].bitcast(F32), ALU.subtract).then_inc(n.done["lo"], 1)

        def pool_split(pool, f, p):
            pool.wait_ge(f.done["hi"], p + 1)
            nc.gpsimd.tensor_tensor(f.lo[:, p % 2], f.act[:, p % 2], f.hi[:, p % 2].bitcast(F32),
                                    ALU.subtract).then_inc(f.done["lo"], 1)

        def pool_ffn_end(pool, f):
            if f.pool_add:
                pool.wait_ge(f.done["scaled"], 1)
                nc.gpsimd.tensor_tensor(f.out[:], f.res[:], f.norm.nrm[:], ALU.add).then_inc(f.done["added"], 1)

        def pool_project(pool):
            pool.wait_ge(z_added, 1)
            pool.wait_ge(n1.done["plain"], TT)
            if with_back:
                pool.wait_ge(x_taken, 1)
                pool.wait_ge(n4.done["normed"], TT)
            nc.gpsimd.tensor_tensor(xres[:], xin[:], xn[:], ALU.add).then_inc(xz_added, 1)

        def pool_collect(pool, sp):
            pool.wait_ge(scanned, 4 * (sp + 1))
            h = hbuf[:, sp % 3]
            nc.gpsimd.tensor_copy(hstate[:, 2 * sp:2 * sp + 2, :], h[:, :, :, T - 1]).then_inc(saved, 1)
            pool.wait_ge(saved, sp + 1)
            pool.wait_ge(rep_copied, 2 * sp + 2)
            nc.gpsimd.tensor_tensor(h, h, rep[:, sp % 2, :, 1, :].unsqueeze(2).to_broadcast([P, 2, FT, T]),
                                    ALU.mult).then_inc(outs_made, 1)
            pool.wait_ge(outs_made, sp + 1)
            nc.gpsimd.tensor_tensor(h[:, 0], h[:, 0], h[:, 1], ALU.add).then_inc(pair_summed, 1)


        def finish():
            numbers = [s.num for s in sems]
            assert numbers == list(range(numbers[0], numbers[0] + len(numbers)))
            nc.sync.sem_clear(range(numbers[0], numbers[0] + len(numbers)))
            nc.all_engine_barrier()

        with_back = False
        with nc.Block() as block:
            @block.sync
            def _(sp):
                sp.dma_start(xin[:], x_view[0]).then_inc(x_in, 16)
                sp.wait_ge(xz_added, 1)
                sp.dma_start(xin[:], x_view[1]).then_inc(x_next, 16)
                sp.wait_ge(x_next, 16)

            @block.tensor
            def _(pe):
                def steps(low):
                    pe_norm_turn(pe, n1)
                    pe_queries_keys(pe)
                    pe_keys_values(pe, 0)
                    pe_keys_values(pe, 1)
                    pe_gates(pe)
                    pe_outer(pe)
                    pe_score(pe, 0)
                    pe_score(pe, 1)
                    pe_value(pe, 0)
                    pe_score(pe, 2)
                    pe_value(pe, 1)
                    pe_score(pe, 3)
                    pe_value(pe, 2)
                    pe_score(pe, 4)
                    pe_value(pe, 3)
                    pe_score(pe, 5)
                    pe_value(pe, 4)
                    pe_score(pe, 6)
                    pe_value(pe, 5)
                    pe_score(pe, 7)
                    pe_value(pe, 6)
                    pe_value(pe, 7)
                    pe_ret_turn(pe)
                    pe_project(pe)
                    pe_norm_turn(pe, n2)
                    pe_gate_up(pe, f1, 0, True)
                    pe_gate_up(pe, f1, 1, True)
                    pe_down(pe, f1, 0, True)
                    pe_gate_up(pe, f1, 2, True)
                    pe_down(pe, f1, 1, True)
                    pe_down(pe, f1, 2, True)
                    pe_norm_turn(pe, n3)
                    pe_gate_up(pe, f2, 0, low)
                    pe_gate_up(pe, f2, 1, low)
                    pe_down(pe, f2, 0, low)
                    pe_gate_up(pe, f2, 2, low)
                    pe_down(pe, f2, 1, low)
                    pe_down(pe, f2, 2, low)

                wide = pe.value_load(wide_flag[0:1, 0:1], min_val=0, max_val=1)
                with pe.If(wide > 0):
                    steps(True)
                with pe.Else():
                    steps(False)

            @block.scalar
            def _(act):
                act_norm_turn(act, n1)
                act_queries_keys(act)
                act_keys_values(act, 0)
                act_keys_values(act, 1)
                act_gates(act)
                act_group_norm(act)
                act_ret_turn(act)
                act_norm_turn(act, n2)
                act_gate_up(act, f1, 0)
                act_gate_up(act, f1, 1)
                act_split(act, f1, 0)
                act_split(act, f1, 1)
                act_gate_up(act, f1, 2)
                act_split(act, f1, 2)
                act_norm_turn(act, n3)
                act_gate_up(act, f2, 0)
                act_gate_up(act, f2, 1)
                act_split(act, f2, 0)
                act_split(act, f2, 1)
                act_gate_up(act, f2, 2)
                act_split(act, f2, 2)

            @block.vector
            def _(dve):
                dve.wait_ge(x_in, 16)
                dve_norm_stats(dve, n1)
                dve_norm_apply(dve, n1)
                dve_norm_split(dve, n1)
                dve_queries_keys(dve)
                dve_keys_values(dve, 0)
                dve_keys_values(dve, 1)
                dve_gates(dve)
                dve_outer(dve)
                for i in range(8):
                    dve_score(dve, i)
                dve_group_norm(dve)
                dve_group_gate(dve)
                dve_group_scale(dve)
                dve_ret_split(dve)
                dve_project(dve)
                dve_norm_stats(dve, n2)
                dve_norm_apply(dve, n2)
                dve_norm_split(dve, n2)
                for i in range(3):
                    dve_gate_up(dve, f1, i)
                dve_ffn_end(dve, f1)
                dve_norm_stats(dve, n3)
                dve_norm_apply(dve, n3)
                dve_norm_split(dve, n3)
                for i in range(3):
                    dve_gate_up(dve, f2, i)
                dve_ffn_end(dve, f2)

            @block.gpsimd
            def _(pool):
                pool_norm_stats(pool, n1)
                pool_norm_split(pool, n1)
                pool_project(pool)
                pool_norm_stats(pool, n2)
                pool_norm_split(pool, n2)
                for i in range(3):
                    pool_split(pool, f1, i)
                pool_ffn_end(pool, f1)
                pool_norm_stats(pool, n3)
                pool_norm_split(pool, n3)
                for i in range(3):
                    pool_split(pool, f2, i)
                pool_ffn_end(pool, f2)

        finish()

        with_back = True
        with nc.Fori(0, CHUNKS - 1) as chunk:
            with nc.Block() as block:
                @block.sync
                def _(sp):
                    sp.wait_ge(xz_added, 1)
                    sp.dma_start(xin[:], x_view[chunk + 2]).then_inc(x_next, 16)
                    sp.wait_ge(f3.done["added"], 1)
                    sp.dma_start(out_view[chunk], xback[:]).then_inc(x_out, 16)
                    sp.wait_ge(x_out, 16)
                    sp.wait_ge(x_next, 16)

                @block.tensor
                def _(pe):
                    def steps(low):
                        pe_norm_turn(pe, n1)
                        pe_norm_turn(pe, n4)
                        pe_queries_keys(pe)
                        pe_keys_values(pe, 0)
                        pe_state_inputs(pe)
                        pe_keys_values(pe, 1)
                        pe_gates(pe)
                        pe_steps_size(pe)
                        pe_outer(pe)
                        pe_score(pe, 0)
                        pe_score(pe, 1)
                        pe_spread(pe, 0)
                        pe_value(pe, 0)
                        pe_score(pe, 2)
                        pe_value(pe, 1)
                        pe_spread(pe, 1)
                        pe_score(pe, 3)
                        pe_value(pe, 2)
                        pe_score(pe, 4)
                        pe_spread(pe, 2)
                        pe_value(pe, 3)
                        pe_score(pe, 5)
                        pe_value(pe, 4)
                        pe_score(pe, 6)
                        pe_value(pe, 5)
                        pe_score(pe, 7)
                        pe_value(pe, 6)
                        pe_spread(pe, 3)
                        pe_value(pe, 7)
                        for i in range(4, 7):
                            pe_spread(pe, i)
                        pe_ret_turn(pe)
                        pe_project(pe)
                        pe_spread(pe, 7)
                        pe_norm_turn(pe, n2)
                        pe_gate_up(pe, f1, 0, True)
                        pe_gate_up(pe, f1, 1, True)
                        pe_scan_back(pe)
                        pe_down(pe, f1, 0, True)
                        pe_gate_up(pe, f1, 2, True)
                        pe_norm_turn(pe, n5)
                        pe_down(pe, f1, 1, True)
                        pe_gate_up(pe, f3, 0, low)
                        pe_down(pe, f1, 2, True)
                        pe_gate_up(pe, f3, 1, low)
                        pe_norm_turn(pe, n3)
                        pe_down(pe, f3, 0, low)
                        pe_gate_up(pe, f2, 0, low)
                        pe_gate_up(pe, f2, 1, low)
                        pe_gate_up(pe, f3, 2, low)
                        pe_down(pe, f3, 1, low)
                        pe_down(pe, f2, 0, low)
                        pe_gate_up(pe, f2, 2, low)
                        pe_down(pe, f2, 1, low)
                        pe_down(pe, f3, 2, low)
                        pe_down(pe, f2, 2, low)

                    wide = pe.value_load(wide_flag[0:1, 0:1], min_val=0, max_val=1)
                    with pe.If(wide > 0):
                        steps(True)
                    with pe.Else():
                        steps(False)

                @block.scalar
                def _(act):
                    act_take(act)
                    act_norm_turn(act, n1)
                    act_norm_turn(act, n4)
                    act_queries_keys(act)
                    act_keys_values(act, 0)
                    act_state_inputs(act)
                    act_keys_values(act, 1)
                    act_gates(act)
                    act_steps_size(act)
                    for i in range(4):
                        act_spread(act, i)
                    act_group_norm(act)
                    act_spread(act, 4)
                    act_spread(act, 5)
                    act_ret_turn(act)
                    act_spread(act, 6)
                    act_norm_turn(act, n2)
                    act_spread(act, 7)
                    act_gate_up(act, f1, 0)
                    act_gate_up(act, f1, 1)
                    act_split(act, f1, 0)
                    act_split(act, f1, 1)
                    act_gate_up(act, f1, 2)
                    act_norm_turn(act, n5)
                    act_split(act, f1, 2)
                    act_gate_up(act, f3, 0)
                    act_gate_up(act, f3, 1)
                    act_split(act, f3, 0)
                    act_norm_turn(act, n3)
                    act_split(act, f3, 1)
                    act_gate_up(act, f2, 0)
                    act_gate_up(act, f2, 1)
                    act_split(act, f2, 0)
                    act_gate_up(act, f3, 2)
                    act_split(act, f2, 1)
                    act_split(act, f3, 2)
                    act_gate_up(act, f2, 2)
                    act_split(act, f2, 2)

                @block.vector
                def _(dve):
                    dve_norm_stats(dve, n1)
                    dve_norm_stats(dve, n4)
                    dve_norm_apply(dve, n1)
                    dve_norm_apply(dve, n4)
                    dve_norm_split(dve, n1)
                    dve_norm_split(dve, n4)
                    dve_queries_keys(dve)
                    dve_keys_values(dve, 0)
                    dve_state_inputs(dve)
                    dve_keys_values(dve, 1)
                    dve_gates(dve)
                    dve_outer(dve)
                    dve_steps_size(dve)
                    dve_score(dve, 0)
                    dve_score(dve, 1)
                    dve_steps_end(dve)
                    dve_scan_skip(dve)
                    dve_score(dve, 2)
                    dve_spread(dve, 0)
                    dve_scan(dve, 0)
                    dve_score(dve, 3)
                    dve_score(dve, 4)
                    dve_spread(dve, 1)
                    dve_score(dve, 5)
                    dve_scan(dve, 1)
                    dve_score(dve, 6)
                    dve_score(dve, 7)
                    dve_collect(dve, 0)
                    dve_spread(dve, 2)
                    dve_group_norm(dve)
                    dve_scan(dve, 2)
                    dve_collect(dve, 1)
                    dve_spread(dve, 3)
                    dve_scan(dve, 3)
                    dve_group_gate(dve)
                    dve_group_scale(dve)
                    dve_collect(dve, 2)
                    dve_spread(dve, 4)
                    dve_ret_split(dve)
                    dve_scan(dve, 4)
                    dve_collect(dve, 3)
                    dve_spread(dve, 5)
                    dve_project(dve)
                    dve_scan(dve, 5)
                    dve_norm_stats(dve, n2)
                    dve_collect(dve, 4)
                    dve_spread(dve, 6)
                    dve_norm_apply(dve, n2)
                    dve_scan(dve, 6)
                    dve_norm_split(dve, n2)
                    dve_collect(dve, 5)
                    dve_spread(dve, 7)
                    dve_scan(dve, 7)
                    dve_collect(dve, 6)
                    dve_gate_up(dve, f1, 0)
                    dve_collect(dve, 7)
                    dve_gate_up(dve, f1, 1)
                    dve_scan_back(dve)
                    dve_norm_stats(dve, n5)
                    dve_norm_apply(dve, n5)
                    dve_gate_up(dve, f1, 2)
                    dve_norm_split(dve, n5)
                    dve_gate_up(dve, f3, 0)
                    dve_ffn_end(dve, f1)
                    dve_norm_stats(dve, n3)
                    dve_norm_apply(dve, n3)
                    dve_gate_up(dve, f3, 1)
                    dve_norm_split(dve, n3)
                    dve_gate_up(dve, f2, 0)
                    dve_gate_up(dve, f2, 1)
                    dve_gate_up(dve, f3, 2)
                    dve_gate_up(dve, f2, 2)
                    dve_ffn_end(dve, f3)
                    dve_ffn_end(dve, f2)

                @block.gpsimd
                def _(pool):
                    pool_norm_stats(pool, n1)
                    pool_norm_stats(pool, n4)
                    pool_norm_split(pool, n1)
                    pool_norm_split(pool, n4)
                    for i in range(5):
                        pool_collect(pool, i)
                    pool_project(pool)
                    pool_norm_stats(pool, n2)
                    pool_collect(pool, 5)
                    pool_norm_split(pool, n2)
                    pool_collect(pool, 6)
                    pool_collect(pool, 7)
                    pool_split(pool, f1, 0)
                    pool_split(pool, f1, 1)
                    pool_norm_stats(pool, n5)
                    pool_norm_split(pool, n5)
                    pool_split(pool, f1, 2)
                    pool_ffn_end(pool, f1)
                    pool_norm_stats(pool, n3)
                    pool_norm_split(pool, n3)
                    pool_split(pool, f3, 0)
                    pool_split(pool, f3, 1)
                    pool_split(pool, f2, 0)
                    pool_split(pool, f2, 1)
                    pool_split(pool, f3, 2)
                    pool_ffn_end(pool, f3)
                    pool_split(pool, f2, 2)
                    pool_ffn_end(pool, f2)

            finish()

        with nc.Block() as block:
            @block.sync
            def _(sp):
                sp.wait_ge(f3.done["added"], 1)
                sp.dma_start(out_view[CHUNKS - 1], xback[:]).then_inc(x_out, 16)
                sp.wait_ge(x_out, 16)

            @block.tensor
            def _(pe):
                def steps(low):
                    pe_norm_turn(pe, n4)
                    pe_state_inputs(pe)
                    pe_steps_size(pe)
                    for i in range(8):
                        pe_spread(pe, i)
                    pe_scan_back(pe)
                    pe_norm_turn(pe, n5)
                    pe_gate_up(pe, f3, 0, low)
                    pe_gate_up(pe, f3, 1, low)
                    pe_down(pe, f3, 0, low)
                    pe_gate_up(pe, f3, 2, low)
                    pe_down(pe, f3, 1, low)
                    pe_down(pe, f3, 2, low)

                wide = pe.value_load(wide_flag[0:1, 0:1], min_val=0, max_val=1)
                with pe.If(wide > 0):
                    steps(True)
                with pe.Else():
                    steps(False)

            @block.scalar
            def _(act):
                act_take(act)
                act_norm_turn(act, n4)
                act_state_inputs(act)
                act_steps_size(act)
                for i in range(8):
                    act_spread(act, i)
                act_norm_turn(act, n5)
                act_gate_up(act, f3, 0)
                act_gate_up(act, f3, 1)
                act_split(act, f3, 0)
                act_split(act, f3, 1)
                act_gate_up(act, f3, 2)
                act_split(act, f3, 2)

            @block.vector
            def _(dve):
                dve_norm_stats(dve, n4)
                dve_norm_apply(dve, n4)
                dve_norm_split(dve, n4)
                dve_state_inputs(dve)
                dve_steps_size(dve)
                dve_steps_end(dve)
                dve_scan_skip(dve)
                dve_spread(dve, 0)
                dve_scan(dve, 0)
                dve_spread(dve, 1)
                dve_scan(dve, 1)
                dve_collect(dve, 0)
                dve_spread(dve, 2)
                dve_scan(dve, 2)
                dve_collect(dve, 1)
                dve_spread(dve, 3)
                dve_scan(dve, 3)
                dve_collect(dve, 2)
                dve_spread(dve, 4)
                dve_scan(dve, 4)
                dve_collect(dve, 3)
                dve_spread(dve, 5)
                dve_scan(dve, 5)
                dve_collect(dve, 4)
                dve_spread(dve, 6)
                dve_scan(dve, 6)
                dve_collect(dve, 5)
                dve_spread(dve, 7)
                dve_scan(dve, 7)
                dve_collect(dve, 6)
                dve_collect(dve, 7)
                dve_scan_back(dve)
                dve_norm_stats(dve, n5)
                dve_norm_apply(dve, n5)
                dve_norm_split(dve, n5)
                for i in range(3):
                    dve_gate_up(dve, f3, i)
                dve_ffn_end(dve, f3)

            @block.gpsimd
            def _(pool):
                pool_norm_stats(pool, n4)
                pool_norm_split(pool, n4)
                for i in range(8):
                    pool_collect(pool, i)
                pool_norm_stats(pool, n5)
                pool_norm_split(pool, n5)
                for i in range(3):
                    pool_split(pool, f3, i)
                pool_ffn_end(pool, f3)


def host_layout(i):
    def pad_cols(a, n):
        return np.concatenate([a, np.zeros((a.shape[0], n - a.shape[1]), a.dtype)], axis=1)

    def pad_rows(a, n):
        return np.concatenate([a, np.zeros((n - a.shape[0],) + a.shape[1:], a.dtype)], axis=0)

    def per_feature(v, tiles):
        return pad_rows(v, tiles * P).reshape(tiles, P).T

    a = {k: np.asarray(v) for k, v in i.items()}
    A, B, F = "L0_attn_a_", "L0_attn_b_", "L0_ffn_"
    cols = np.concatenate([
        per_feature(a[A + "norm1_w"], FT), per_feature(a[A + "norm1_b"], FT),
        per_feature(a[A + "norm2_w"], FT), per_feature(a[A + "norm2_b"], FT),
        per_feature(a[B + "D"], FT), per_feature(a[B + "dt_proj_b"], FT),
        per_feature(a[F + "s_gate"], HT), per_feature(a[F + "s_up"], HT),
        a[B + "A_log"].reshape(FT, P, NS).transpose(1, 0, 2).reshape(P, FT * NS)], axis=1)
    return {
        "x": pad_rows(a[A + "x"].reshape(S, D), S + T),
        "w_qkvg": np.concatenate([a[A + "wq"], a[A + "wk"], a[A + "wv"], a[A + "wg"]], axis=1),
        "w_o": a[A + "wo"],
        "w_12": np.concatenate([pad_cols(a[A + "w1"], HP), pad_cols(a[A + "w2"], HP)], axis=1),
        "w_3": pad_rows(a[A + "w3"], HP),
        "w_gu": np.concatenate([pad_cols(a[F + "wq_gate"].T, HP), pad_cols(a[F + "wq_up"].T, HP)], axis=1),
        "w_dn": pad_rows(a[F + "wq_down"].T, HP),
        "w_xp": pad_cols(a[B + "x_proj_w"].T, XPW),
        "w_dt": a[B + "dt_proj_w"].T,
        "cols": cols,
        "s_down": a[F + "s_down"].reshape(D),
        "consts": shape_constants(),
    }


def kernel(**inputs):
    import concourse.bacc as bacc
    from concourse.bass_utils import run_bass_kernel_spmd

    nc = bacc.Bacc("TRN2", target_bir_lowering=False, num_devices=1)
    arrays, args = {}, []
    for name, a in host_layout(inputs).items():
        a = np.ascontiguousarray(a)
        arrays[name + "_dram"] = a
        args.append(nc.dram_tensor(name + "_dram", a.shape, mybir.dt.from_np(a.dtype), kind="ExternalInput").ap())
    args.append(nc.dram_tensor("out_dram", (S, D), F32, kind="ExternalOutput").ap())
    program(nc, *args)
    r = run_bass_kernel_spmd(nc, [arrays], core_ids=[0])
    return r.results[0]["out_dram"].reshape(1, S, D)
```

```python
from contextlib import ExitStack

import numpy as np

import concourse.bass as bass
from concourse import mybir

F32 = mybir.dt.float32
F32R = mybir.dt.float32r
BF16 = mybir.dt.bfloat16
I32 = mybir.dt.int32
ALU = mybir.AluOpType
ACT = mybir.ActivationFunctionType
AX_X = mybir.AxisListType.X

P = 128
S = 2048
D = 256
FT = D // P
T = 256
TT = T // P
CHUNKS = S // T
HEADS = 16
DH = D // HEADS
HID_A = 682
HID_Q = 704
HT = 6
HP = HT * P
PAIRS = HT // 2
NEWTON = 3
XPW = 2 * P
NS = 16
SP = NS // 2
DTR = 128
EPS = 1e-5
ZERO_POINT = 128.0

COLS = dict(n1w=(0, 2), n1b=(2, 4), n2w=(4, 6), n2b=(6, 8), dskip=(8, 10), dtb=(10, 12),
            sgate=(12, 18), sup=(18, 24), alog=(24, 56))
NCOLS = 56
CONSTS = dict(decay=(0, 2048), ident=(2048, 2176), qdecay=(2176, 2432), kdecay=(2432, 2688),
              headmask=(2688, 2816), even=(2816, 2817), odd=(2817, 2818), chunkdecay=(2818, 2820),
              select=(2820, 2852), half=(2852, 2856))
NCONST = 2856


RMAX = bass.bass_isa.ReduceOp.max


def shape_constants():
    c = np.zeros((P, NCONST), np.float64)
    gamma = (np.float32(1.0) - np.exp2(np.float32(-5.0) - np.arange(HEADS, dtype=np.float32))).astype(np.float64)
    t = np.arange(P)[:, None]
    s = np.arange(P)[None, :]
    for h in range(HEADS):
        c[:, h * P:(h + 1) * P] = np.where(s >= t, gamma[h] ** np.maximum(s - t, 0), 0.0)

    def put(name, a):
        lo, hi = CONSTS[name]
        c[:, lo:hi] = a

    row_head = np.arange(P) // DH
    put("ident", np.eye(P))
    put("qdecay", np.concatenate([gamma[row_head + 8 * f][:, None] ** (s + 1) for f in range(FT)], axis=1))
    put("kdecay", DH ** -0.5 * gamma[np.arange(D) // DH][None, :] ** (P - 1 - t))
    put("headmask", (row_head[:, None] == row_head[None, :]))
    put("even", (DH ** -0.5 * (row_head % 2 == 0))[:, None])
    put("odd", (DH ** -0.5 * (row_head % 2 == 1))[:, None])
    put("chunkdecay", np.stack([gamma[row_head + 8 * f] ** P for f in range(FT)], axis=1))
    put("select", (np.arange(P)[:, None] % 32 == np.arange(32)[None, :]) * (np.arange(P)[:, None] < 96))
    put("half", -0.5)
    return c.astype(np.float32)


class Norm:

    def __init__(self, name, sem, src, src_ready, nrm, bank, parts, small, gains=None, twice=None, keep=False):
        self.keep = keep or gains is not None
        self.src, self.src_ready, self.nrm, self.bank = src, src_ready, nrm, bank
        self.full, self.hi, self.lo = parts
        self.stats, self.mv, self.var, self.rstd = small
        self.gains, self.twice = gains, twice
        steps = ["stats", "aggr", "var", "rstd", "normed", "turned", "hi", "lo"]
        steps += ["full"] if self.keep else []
        steps += ["plain"] if twice is not None else []
        self.done = {what: sem(f"{name}_{what}") for what in steps}


class Ffn:

    def __init__(self, name, sem, norm, gu, down, banks, ybank, ring, res, out, gate_scale=None, hid_scale=None):
        self.norm, self.gu, self.down, self.banks, self.ybank = norm, gu, down, banks, ybank
        self.act, self.hi, self.lo = ring
        self.res, self.out, self.gate_scale, self.hid_scale = res, out, gate_scale, hid_scale
        steps = ["gu", "tanh", "gated", "hid", "hi", "lo", "down", "added"] + (["scaled"] if hid_scale is not None else [])
        self.done = {what: sem(f"{name}_{what}") for what in steps}


def program(nc, x, w_qkvg, w_o, w_12, w_3, w_gu, w_dn, w_xp, w_dt, cols, s_down, consts, out):
    x_view = x.rearrange("(n t p) d -> n p t d", p=P, t=TT)
    out_view = out.rearrange("(n t p) d -> n p t d", p=P, t=TT)

    with ExitStack() as ctx:
        sems = []

        def sb(name, shape, dt=F32, c=ctx):
            return c.enter_context(nc.sbuf_tensor(name, shape, dt))

        def sem(name):
            s = ctx.enter_context(nc.semaphore(name))
            sems.append(s)
            return s

        banks = [ctx.enter_context(nc.psum_tensor(f"bank{i}", [P, 512], F32)) for i in range(8)]

        shapes = dict(qkvg=[P, FT, 4 * D], wo=[P, FT, D], w12=[P, FT, 2 * HP], w3=[P, HT, D], gu=[P, FT, 2 * HP],
                      dn=[P, HT, D], xp=[P, FT, XPW], dtw=[P, D])
        with ExitStack() as until_split:
            raw = {name: sb("raw_" + name, shape, I32 if name in ("gu", "dn") else F32, until_split)
                   for name, shape in shapes.items()}
        low_part = {name: sb(name + "_lo", shape, F32R) for name, shape in shapes.items()}
        high_part = {name: sb(name + "_hi", shape, F32R) for name, shape in shapes.items()}
        qkvg, wo, w12, w3, gu, dn, xp, dtw = ((high_part[name], low_part[name]) for name in shapes)
        cst = sb("cst", [P, NCONST])
        col = sb("col", [P, NCOLS])
        sdrow = sb("sdrow", [P, D])
        select = sb("select", [96, 32], BF16)
        a_neg = sb("a_neg", [P, FT * NS])
        gate_half = sb("gate_half", [P, HT])
        hid_scale = sb("hid_scale", [P, HT])
        wide_ints = sb("wide_ints", [P, 6])
        wide_flag = sb("wide_flag", [P, 1], I32)
        retain = sb("retain", [P, TT, FT, P])
        hstate = sb("hstate", [P, NS, FT])

        def const(name):
            lo, hi = CONSTS[name]
            return cst[:, lo:hi]

        def column(name, j=None):
            lo, hi = COLS[name]
            return col[:, lo:hi] if j is None else col[:, lo + j:lo + j + 1]

        ident = const("ident")

        def piece(name, source, *at):
            return dict(source=source, raw=raw[name][(slice(None), *at)], hi=high_part[name][(slice(None), *at)],
                        lo=low_part[name][(slice(None), *at)], shift=name in ("gu", "dn"),
                        loaded=sem("_".join([name, *map(str, at), "loaded"])))

        def tiled(w):
            return w.rearrange("(k p) m -> p k m", p=P)

        pieces = [piece("qkvg", tiled(w_qkvg)[:, k], k) for k in range(FT)] + [piece("wo", tiled(w_o))]
        pieces += [piece("w12", tiled(w_12)[:, k], k) for k in range(FT)] + [piece("w3", tiled(w_3))]
        pieces += [piece("gu", tiled(w_gu)[:, k], k) for k in range(FT)] + [piece("dn", tiled(w_dn))]
        pieces += [piece("xp", tiled(w_xp)), piece("dtw", w_dt)]

        def prepared(i):
            return i < FT or pieces[i]["shift"]

        small_loaded, decay_loaded = sem("small_loaded"), sem("decay_loaded")
        weight_ready, weight_hi, weight_lo = sem("weight_ready"), sem("weight_hi"), sem("weight_lo")
        centre_made, neg_exp, halved = sem("centre_made"), sem("neg_exp"), sem("halved")
        wide_seen, wide_everywhere = sem("wide_seen"), sem("wide_everywhere")
        head_mean = sb("head_mean", [P, FT, HEADS])
        wide_any, wide_all = sb("wide_any", [P, 1]), sb("wide_all", [P, 1])

        def small(name, kinds=1):
            return (sb(name + "_stats", [P, TT, 6]), sb(name + "_mv", [P, TT, 2]),
                    sb(name + "_var", [P, kinds * TT]), sb(name + "_rstd", [P, kinds * TT]))

        def parts(name):
            return sb(name, [P, FT, T]), sb(name + "_hi", [P, FT, T], F32R), sb(name + "_lo", [P, FT, T], F32R)

        def ring(name, c):
            return (sb(name + "_act", [P, 2, 2, T], F32, c), sb(name + "_hi", [P, 2, 2, T], F32R, c),
                    sb(name + "_lo", [P, 2, 2, T], F32R, c))

        xin = sb("xin", [P, TT, D])
        xres = sb("xres", [P, TT, D])
        nrm = sb("nrm", [P, TT, D])
        xn = sb("xn", [P, TT, D])
        hT = parts("hT")
        small_front = small("front")
        small_twice = small("twice", 2)
        with ExitStack() as only_attn:
            q_hi = sb("q_hi", [P, FT, TT, 2, P], F32R, only_attn)
            q_lo = sb("q_lo", [P, FT, TT, 2, P], F32R, only_attn)
            qTd = sb("qTd", [P, FT, T], F32, only_attn)
            k_hi = sb("k_hi", [P, FT, T], F32R, only_attn)
            k_lo = sb("k_lo", [P, FT, T], F32R, only_attn)
            kdec = sb("kdec", [P, TT, D], F32, only_attn)
            vtok = sb("vtok", [P, TT, D], F32, only_attn)
            kvmask = sb("kvmask", [P, TT, FT, P], F32, only_attn)
            probs = sb("probs", [P, 3, 512], F32, only_attn)
            gated = sb("gated", [P, TT, D], F32, only_attn)
            squares = sb("squares", [P, TT, D], F32, only_attn)
            rscr = sb("rscr", [P, TT * HEADS], F32, only_attn)
            rvar = sb("rvar", [P, TT * HEADS], F32, only_attn)
            rstd = sb("ret_rstd", [P, TT * HEADS], F32, only_attn)
        with ExitStack() as only_ffn:
            front_ring = ring("front_ring", only_ffn)
        sb("front_shared", [P, 15 * 512 + 3 * TT * HEADS])

        xback = sb("xback", [P, TT, D])
        nrm_b = sb("nrm_b", [P, TT, D])
        uT = parts("uT")
        small_back = small("back")
        yscan = sb("yscan", [P, FT, T])
        with ExitStack() as only_ffn:
            back_ring = ring("back_ring", only_ffn)
        delta = sb("delta", [P, FT, T])
        du = sb("du", [P, FT, T])
        dr_hi = sb("dr_hi", [P, T], F32R)
        dr_lo = sb("dr_lo", [P, T], F32R)
        bc_full = sb("bc_full", [32, 2, T])
        bc_parts = sb("bc_parts", [96, T], BF16)
        rep = sb("rep", [P, 2, 2, 2, T])
        dA = sb("dA", [P, 2, 2, FT, T])
        hbuf = sb("hbuf", [P, 3, 2, FT, T])

        sems.clear()
        x_in, x_next, x_out, x_taken = sem("x_in"), sem("x_next"), sem("x_out"), sem("x_taken")
        z_added, xz_added, x3_added = sem("z_added"), sem("xz_added"), sem("x3_added")

        n1 = Norm("n1", sem, xin, None, nrm, 0, hT, small_twice, gains=("n1w", "n1b"), twice=xn)
        n2 = Norm("n2", sem, xn, (z_added, 1), nrm, 4, hT, small_front, gains=("n2w", "n2b"))
        f1 = Ffn("f1", sem, n2, w12, w3, ((0, 1), (2, 3)), 4, front_ring, xres, xres)
        n3 = Norm("n3", sem, xres, (f1.done["added"], 1), nrm, 4, hT, small_front)
        f2 = Ffn("f2", sem, n3, gu, dn, ((0, 1), (2, 3)), 4, front_ring, xres, xres, gate_half, hid_scale)
        n4 = Norm("n4", sem, xres, None, nrm_b, 5, uT, small_back, keep=True)
        n5 = Norm("n5", sem, xback, (x3_added, 1), nrm_b, 6, uT, small_back)
        f3 = Ffn("f3", sem, n5, gu, dn, ((5, 6),), 7, back_ring, xback, xback, gate_half, hid_scale)

        q_turned, q_rounded, q_parted, q_decayed = sem("q_turned"), sem("q_rounded"), sem("q_parted"), sem("q_decayed")
        k_turned, k_rounded, k_parted = sem("k_turned"), sem("k_rounded"), sem("k_parted")
        kv_made, k_decayed, v_copied = sem("kv_made"), sem("k_decayed"), sem("v_copied")
        g_made, g_tanh, g_gated = sem("g_made"), sem("g_tanh"), sem("g_gated")
        outer_made, outer_masked, state_ready = sem("outer_made"), sem("outer_masked"), sem("state_ready")
        scores_made, probs_made, probs_used = sem("scores_made"), sem("probs_made"), sem("probs_used")
        ret_squared, ret_var, ret_root = sem("ret_squared"), sem("ret_var"), sem("ret_root")
        g_scaled, ret_gated = sem("g_scaled"), sem("ret_gated")
        yt_turned, yt_hi, yt_lo, y_projected = sem("yt_turned"), sem("yt_hi"), sem("yt_lo"), sem("y_projected")

        drbc_made, drh_made, drl_made = sem("drbc_made"), sem("drh_made"), sem("drl_made")
        bc_copied, bc_part = sem("bc_copied"), sem("bc_part")
        dt_made, dt_abs, dt_exp, dt_ln, dt_pos = sem("dt_made"), sem("dt_abs"), sem("dt_exp"), sem("dt_ln"), sem("dt_pos")
        delta_made, du_made = sem("delta_made"), sem("du_made")
        rep_made, rep_copied = sem("rep_made"), sem("rep_copied")
        decay_made, dbu_made, scanned, saved, outs_made, y_added = (
            sem("decay_made"), sem("dbu_made"), sem("scanned"), sem("saved"), sem("outs_made"), sem("y_added"))
        y_skipped, pair_summed, y_back = sem("y_skipped"), sem("pair_summed"), sem("y_back")

        def products(acc, sta, mov, start, stop, skip=False):
            terms = []
            for (sh, sl), (mh, ml) in zip(sta, mov):
                terms += [(sh, mh), (sh, ml), (sl, mh)]
            terms = [(a, b) for a, b in terms if a is not None and b is not None]
            for n, (a, b) in enumerate(terms):
                last = nc.tensor.matmul(acc, a, b, start=start and n == 0, stop=stop and n == len(terms) - 1,
                                        skip_group_check=skip)
            return last

        def cut(pair_, *at, low=True):
            return pair_[0][at], pair_[1][at] if low else None

        ALL = slice(None)

        def pe_norm_turn(pe, n):
            for ft in range(FT):
                for tt in range(TT):
                    if ft == 0:
                        pe.wait_ge(n.done["normed"], tt + 1)
                    last = nc.tensor.transpose(banks[n.bank][:, ft * T + tt * P:ft * T + (tt + 1) * P],
                                               n.nrm[:, tt, ft * P:(ft + 1) * P], ident)
            last.then_inc(n.done["turned"], 1)

        def pe_gate_up(pe, f, p, low):
            if p == 0:
                pe.wait_ge(f.norm.done["lo"], 1)
            if p >= len(f.banks):
                pe.wait_ge(f.done["hid"], p - len(f.banks) + 1)
            for half, bank in enumerate(f.banks[p % len(f.banks)]):
                for i in range(2):
                    c = half * HP + (2 * p + i) * P
                    sta = [cut(f.gu, ALL, k, slice(c, c + P), low=low) for k in range(FT)]
                    mov = [(f.norm.hi[:, k, :], f.norm.lo[:, k, :]) for k in range(FT)]
                    last = products(banks[bank][:, i * T:(i + 1) * T], sta, mov, True, True)
            last.then_inc(f.done["gu"], 1)

        def pe_down(pe, f, p, low):
            pe.wait_ge(f.done["lo"], p + 1)
            for tt in range(TT):
                t = slice(tt * P, (tt + 1) * P)
                acc = banks[f.ybank][:, tt * D:(tt + 1) * D]
                last = products(acc, [(f.hi[:, p % 2, i, t], f.lo[:, p % 2, i, t]) for i in range(2)],
                                [cut(f.down, ALL, 2 * p + i, ALL, low=low) for i in range(2)],
                                p == 0 and tt == 0, p == PAIRS - 1, skip=True)
            last.then_inc(f.done["down"], 1)

        def pe_queries_keys(pe):
            pe.wait_ge(n1.done["lo"], 1)
            hp = [(n1.hi[:, k, :], n1.lo[:, k, :]) for k in range(FT)]
            for which, (bank, done) in enumerate(((1, q_turned), (2, k_turned))):
                for ft in range(FT):
                    m = slice(which * D + ft * P, which * D + (ft + 1) * P)
                    last = products(banks[bank][:, ft * T:(ft + 1) * T], [cut(qkvg, ALL, k, m) for k in range(FT)],
                                    hp, True, True)
                last.then_inc(done, 1)

        def pe_keys_values(pe, tt):
            sta = [(n1.hi[:, k, tt * P:(tt + 1) * P], n1.lo[:, k, tt * P:(tt + 1) * P]) for k in range(FT)]
            products(banks[3 + tt][:], sta, [cut(qkvg, ALL, k, slice(D, 3 * D)) for k in range(FT)],
                     True, True).then_inc(kv_made, 1)

        def pe_gates(pe):
            for tt in range(TT):
                sta = [(n1.hi[:, k, tt * P:(tt + 1) * P], n1.lo[:, k, tt * P:(tt + 1) * P]) for k in range(FT)]
                last = products(banks[0][:, tt * D:(tt + 1) * D], sta,
                                [cut(qkvg, ALL, k, slice(3 * D, 4 * D)) for k in range(FT)], True, True)
            last.then_inc(g_made, 1)

        def pe_outer(pe):
            pe.wait_ge(q_parted, 2)
            for tt in range(TT):
                pe.wait_ge(k_decayed, tt + 1)
                for f in range(FT):
                    c = (tt * FT + f) * P
                    last = nc.tensor.matmul(banks[1][:, c:c + P], kdec[:, tt, f * P:(f + 1) * P],
                                            vtok[:, tt, f * P:(f + 1) * P], start=True, stop=True)
            last.then_inc(outer_made, 1)

        def pe_score_products(pe, u):
            f, rg = u // 4, u % 4
            bank = banks[(2, 4, 0)[u % 3]]
            rows_ = slice(32 * rg, 32 * rg + 32)
            for c in range(TT):
                tok = slice(c * P, (c + 1) * P)
                acc = bank[:, c * 2 * P:(c + 1) * 2 * P]
                for n, (k, q) in enumerate(((k_hi, q_hi), (k_hi, q_lo), (k_lo, q_hi))):
                    last = nc.tensor.matmul(acc, k[rows_, f, tok], q[rows_, f, c], start=n == 0, stop=n == 2)
                    if c == TT - 1 and n == 2:
                        last.then_inc(scores_made, 1)
                    yield

        def pe_first_scores(pe, u):
            if u == 0:
                pe.wait_ge(q_parted, 2)
                pe.wait_ge(k_parted, 1)
                pe.wait_ge(k_decayed, 2)
                pe.wait_ge(g_gated, 1)
            for _ in pe_score_products(pe, u):
                pass

        def pe_value(pe, u):
            f, rg = u // 4, u % 4
            if u == 0:
                pe.wait_ge(outer_masked, 1)
                for c in range(TT):
                    if c:
                        pe.wait_ge(state_ready, c)
                    tok = slice(c * P, (c + 1) * P)
                    for g in range(FT):
                        last = nc.tensor.matmul(banks[3][:, c * D + g * P:c * D + (g + 1) * P], qTd[:, g, tok],
                                                retain[:, c, g, :], start=(c == 0 and g == 0), stop=False,
                                                skip_group_check=True)
            pe.wait_ge(probs_made, u + 1)
            ahead = pe_score_products(pe, u + 2) if u + 2 < 8 else iter(())
            next(ahead, None)
            for c in range(TT):
                for par in range(2):
                    h = f * 8 + rg * 2 + par
                    o = (c * 2 + par) * P
                    last = nc.tensor.matmul(banks[3][:, c * D + h * DH:c * D + (h + 1) * DH],
                                            probs[:, u % 3, o:o + P], vtok[:, c, h * DH:(h + 1) * DH],
                                            start=False, stop=True, skip_group_check=True)
                    if c == TT - 1 and par == 1:
                        last.then_inc(probs_used, 1)
                    next(ahead, None)
            for _ in ahead:
                pass

        def pe_need(pe, count):
            pe.wait_ge(weight_lo, count)

        def pe_ret_turn(pe):
            pe.wait_ge(ret_gated, 1)
            for ft in range(FT):
                for tt in range(TT):
                    c = ft * T + tt * P
                    last = nc.tensor.transpose(banks[1][:, c:c + P], gated[:, tt, ft * P:(ft + 1) * P], ident)
            last.then_inc(yt_turned, 1)

        def pe_project(pe):
            pe.wait_ge(yt_lo, 1)
            for tt in range(TT):
                t = slice(tt * P, (tt + 1) * P)
                last = products(banks[3][:, tt * D:(tt + 1) * D], [(hT[1][:, k, t], hT[2][:, k, t]) for k in range(FT)],
                                [cut(wo, ALL, k, ALL) for k in range(FT)], True, True)
            last.then_inc(y_projected, 1)

        def pe_state_inputs(pe):
            pe.wait_ge(n4.done["lo"], 1)
            for i in range(2):
                last = products(banks[6][:, i * T:(i + 1) * T], [cut(xp, ALL, k, slice(i * P, (i + 1) * P)) for k in range(FT)],
                                [(n4.hi[:, k, :], n4.lo[:, k, :]) for k in range(FT)], True, True)
            last.then_inc(drbc_made, 1)

        def pe_steps_size(pe):
            pe.wait_ge(drl_made, 1)
            for ft in range(FT):
                last = products(banks[7][:, ft * T:(ft + 1) * T], [cut(dtw, ALL, slice(ft * P, (ft + 1) * P))],
                                [(dr_hi[:], dr_lo[:])], True, True)
            last.then_inc(dt_made, 1)

        def pe_spread(pe, sp):
            if sp == 0:
                pe.wait_ge(bc_part, 5)
            for i in range(2):
                if sp:
                    pe.wait_ge(rep_copied, 2 * sp - 1 + i)
                for which in range(2):
                    row = which * NS + 2 * sp + i
                    last = nc.tensor.matmul(banks[5 + i][:, which * T:(which + 1) * T],
                                            select[:, row:row + 1].to_broadcast([96, P]), bc_parts[:],
                                            start=True, stop=True)
                last.then_inc(rep_made, 1)

        def pe_scan_back(pe):
            pe.wait_ge(rep_copied, NS)
            pe.wait_ge(y_added, SP)
            for tt in range(TT):
                for ft in range(FT):
                    c = tt * D + ft * P
                    last = nc.tensor.transpose(banks[5][:, c:c + P], yscan[:, ft, tt * P:(tt + 1) * P], ident)
            last.then_inc(y_back, 1)

        def act_weights(act, i):
            piece_ = pieces[i]
            if prepared(i):
                act.wait_ge(weight_ready, sum(prepared(n) for n in range(i + 1)))
            else:
                act.wait_ge(piece_["loaded"], 16)
            nc.scalar.activation(piece_["hi"], piece_["raw"].bitcast(F32), ACT.Copy).then_inc(weight_hi, 1)

        def act_tables(act):
            nc.scalar.activation(a_neg[:], column("alog"), ACT.Exp).then_inc(neg_exp, 1)

        def act_take(act):
            nc.scalar.activation(xback[:], xres[:], ACT.Copy).then_inc(x_taken, 1)

        def act_norm_turn(act, n):
            act.wait_ge(n.done["turned"], 1)
            bank = banks[n.bank]
            if n.gains:
                for ft in range(FT):
                    last = nc.scalar.activation(n.full[:, ft, :], bank[:, ft * T:(ft + 1) * T], ACT.Identity,
                                                bias=column(n.gains[1], ft), scale=column(n.gains[0], ft))
                last.then_inc(n.done["full"], 1)
            elif n.keep:
                nc.scalar.activation(n.full[:].rearrange("p f t -> p (f t)"), bank[:], ACT.Copy).then_inc(n.done["full"], 1)
            else:
                nc.scalar.activation(n.hi[:].rearrange("p f t -> p (f t)"), bank[:], ACT.Copy).then_inc(n.done["hi"], 1)

        def act_gate_up(act, f, p):
            act.wait_ge(f.done["gu"], p + 1)
            if p >= 2:
                act.wait_ge(f.done["lo"], p - 1)
            bank = banks[f.banks[p % len(f.banks)][0]]
            if f.gate_scale is None:
                nc.scalar.activation(f.act[:, p % 2, :, :].rearrange("p i t -> p (i t)"), bank[:], ACT.Tanh,
                                     scale=0.5).then_inc(f.done["tanh"], 1)
            else:
                for i in range(2):
                    j = 2 * p + i
                    last = nc.scalar.activation(f.act[:, p % 2, i, :], bank[:, i * T:(i + 1) * T], ACT.Tanh,
                                                scale=f.gate_scale[:, j:j + 1])
                last.then_inc(f.done["tanh"], 1)

        def act_split(act, f, p):
            act.wait_ge(f.done["hid"], p + 1)
            if p >= 2:
                act.wait_ge(f.done["down"], p - 1)
            nc.scalar.activation(f.hi[:, p % 2], f.act[:, p % 2], ACT.Copy).then_inc(f.done["hi"], 1)

        def act_consts(act):
            act.wait_ge(decay_loaded, 16)

        def act_queries_keys(act):
            act.wait_ge(q_turned, 1)
            for par, name in enumerate(("even", "odd")):
                nc.scalar.activation(q_hi[:, :, :, par, :], banks[1][:].rearrange("p (f t s) -> p f t s", f=FT, t=TT),
                                     ACT.Copy, scale=const(name)).then_inc(q_rounded, 1)
            act.wait_ge(k_turned, 1)
            nc.scalar.activation(k_hi[:].rearrange("p f t -> p (f t)"), banks[2][:], ACT.Copy).then_inc(k_rounded, 1)

        def act_keys_values(act, tt):
            act.wait_ge(kv_made, tt + 1)
            nc.scalar.activation(vtok[:, tt, :], banks[3 + tt][:, D:2 * D], ACT.Copy).then_inc(v_copied, 1)

        def act_gates(act):
            act.wait_ge(g_made, 1)
            nc.scalar.activation(gated[:].rearrange("p t d -> p (t d)"), banks[0][:], ACT.Tanh,
                                 scale=0.5).then_inc(g_tanh, 1)

        def act_group_norm(act):
            act.wait_ge(probs_used, 8)
            nc.scalar.activation(squares[:].rearrange("p t d -> p (t d)"), banks[3][:], ACT.Square).then_inc(ret_squared, 1)

        def act_ret_turn(act):
            act.wait_ge(yt_turned, 1)
            nc.scalar.activation(hT[1][:].rearrange("p f t -> p (f t)"), banks[1][:], ACT.Copy).then_inc(yt_hi, 1)

        def act_state_inputs(act):
            act.wait_ge(drbc_made, 1)
            nc.scalar.activation(dr_hi[:], banks[6][:, 0:T], ACT.Copy).then_inc(drh_made, 1)
            nc.scalar.activation(bc_full[:, 0, :], banks[6][0:32, T:2 * T], ACT.Copy).then_inc(bc_copied, 1)

        def act_steps_size(act):
            act.wait_ge(dt_made, 1)
            for ft in range(FT):
                nc.scalar.activation(delta[:, ft, :], banks[7][:, ft * T:(ft + 1) * T], ACT.Abs,
                                     bias=column("dtb", ft)).then_inc(dt_abs, 1)
            act.wait_ge(dt_abs, FT)
            nc.scalar.activation(delta[:], delta[:], ACT.Exp, scale=-1.0).then_inc(dt_exp, 1)
            act.wait_ge(dt_exp, 1)
            nc.scalar.activation(delta[:], delta[:], ACT.Ln, bias=1.0).then_inc(dt_ln, 1)

        def act_spread(act, sp):
            for i in range(2):
                act.wait_ge(rep_made, 2 * sp + i + 1)
                if sp >= 2 and i == 0:
                    act.wait_ge(dbu_made, sp - 1)
                    act.wait_ge(outs_made, sp - 1)
                nc.scalar.activation(rep[:, sp % 2, i].rearrange("p w t -> p (w t)"), banks[5 + i][:],
                                     ACT.Copy).then_inc(rep_copied, 1)
            if sp == 0:
                act.wait_ge(delta_made, 1)
            if sp >= 2:
                act.wait_ge(scanned, 4 * (sp - 1))
            for i in range(2):
                for ft in range(FT):
                    c = ft * NS + 2 * sp + i
                    nc.scalar.activation(dA[:, sp % 2, i, ft, :], delta[:, ft, :], ACT.Exp,
                                         scale=a_neg[:, c:c + 1]).then_inc(decay_made, 1)

        def dve_prepare(dve, i):
            piece_ = pieces[i]
            dve.wait_ge(piece_["loaded"], 16)
            if i < FT:
                v = piece_["raw"][:, 2 * D:3 * D].rearrange("p (h e) -> p h e", e=DH)
                nc.vector.tensor_reduce(head_mean[:, i], v, AX_X, ALU.add).then_inc(centre_made, 1)
                dve.wait_ge(centre_made, 2 * i + 1)
                nc.vector.tensor_scalar(head_mean[:, i], head_mean[:, i], 1.0 / DH, None, ALU.mult).then_inc(centre_made, 1)
                dve.wait_ge(centre_made, 2 * i + 2)
                nc.vector.tensor_tensor(v, v, head_mean[:, i].unsqueeze(2).to_broadcast([P, HEADS, DH]),
                                        ALU.subtract).then_inc(weight_ready, 1)
            else:
                nc.vector.tensor_scalar(piece_["raw"].bitcast(F32), piece_["raw"], -ZERO_POINT, None,
                                        ALU.add).then_inc(weight_ready, 1)

        def dve_weights(dve, i):
            piece_ = pieces[i]
            dve.wait_ge(weight_hi, i + 1)
            nc.vector.tensor_tensor(piece_["lo"], piece_["raw"].bitcast(F32), piece_["hi"].bitcast(F32),
                                    ALU.subtract).then_inc(weight_lo, 1)

        def dve_clear(dve):
            nc.vector.memset(retain[:], 0.0)
            nc.vector.memset(hstate[:], 0.0)

        def dve_tables(dve):
            nc.vector.tensor_copy(select[:], const("select")[0:96, :])
            nc.vector.tensor_scalar(gate_half[:], column("sgate"), 0.5, None, ALU.mult).then_inc(halved, 1)
            dve.wait_ge(halved, 1)
            nc.vector.tensor_tensor(hid_scale[:], gate_half[:], column("sup"), ALU.mult)
            dve.wait_ge(neg_exp, 1)
            nc.vector.tensor_scalar(a_neg[:], a_neg[:], -1.0, None, ALU.mult)

        def dve_wide(dve, n):
            dve.wait_ge(weight_lo, 7 + n)
            flat = pieces[6 + n]["lo"].bitcast(F32)
            flat = flat.rearrange("p a b -> p (a b)") if n == 2 else flat
            nc.vector.tensor_reduce(wide_ints[:, 2 * n:2 * n + 1], flat, AX_X, ALU.max).then_inc(wide_seen, 1)
            nc.vector.tensor_reduce(wide_ints[:, 2 * n + 1:2 * n + 2], flat, AX_X, ALU.min).then_inc(wide_seen, 1)

        def dve_wide_spread(dve):
            dve.wait_ge(wide_seen, 6)
            nc.vector.tensor_scalar(wide_ints[:], wide_ints[:], 0.0, None, ALU.not_equal).then_inc(wide_seen, 1)
            dve.wait_ge(wide_seen, 7)
            nc.vector.tensor_reduce(wide_any[:], wide_ints[:], AX_X, ALU.max).then_inc(wide_seen, 1)

        def dve_wide_end(dve):
            dve.wait_ge(wide_everywhere, 1)
            nc.vector.tensor_copy(wide_flag[:], wide_all[:])

        def dve_consts(dve):
            dve.wait_ge(small_loaded, 48)
            dve.wait_ge(decay_loaded, 16)

        def dve_norm_stats(dve, n):
            if n.src_ready:
                dve.wait_ge(*n.src_ready)
            for tt in range(TT):
                nc.vector.bn_stats(n.stats[:, tt, :], n.src[:, tt, :]).then_inc(n.done["stats"], 1)
            for tt in range(TT):
                dve.wait_ge(n.done["stats"], tt + 1)
                nc.vector.bn_aggr(n.mv[:, tt, :], n.stats[:, tt, :]).then_inc(n.done["aggr"], 1)
            dve.wait_ge(n.done["aggr"], TT)
            nc.vector.tensor_scalar(n.var[:, 0:TT], n.mv[:, :, 1], EPS, None, ALU.add).then_inc(n.done["var"], 1)
            if n.twice is not None:
                nc.vector.tensor_scalar(n.var[:, TT:2 * TT], n.mv[:, :, 1], 1.0 + EPS, EPS * EPS, ALU.mult,
                                        ALU.add).then_inc(n.done["var"], 1)

        def dve_norm_apply(dve, n):
            dve.wait_ge(n.done["rstd"], 1)
            first = TT if n.twice is not None else 0
            for tt in range(TT):
                nc.vector.tensor_scalar(n.nrm[:, tt, :], n.src[:, tt, :], n.mv[:, tt, 0:1],
                                        n.rstd[:, first + tt:first + tt + 1],
                                        ALU.subtract, ALU.mult).then_inc(n.done["normed"], 1)
            if n.twice is not None:
                for tt in range(TT):
                    nc.vector.tensor_scalar(n.twice[:, tt, :], n.src[:, tt, :], n.mv[:, tt, 0:1], n.rstd[:, tt:tt + 1],
                                            ALU.subtract, ALU.mult).then_inc(n.done["plain"], 1)

        def dve_norm_split(dve, n):
            if n.keep:
                dve.wait_ge(n.done["full"], 1)
                nc.vector.tensor_copy(n.hi[:], n.full[:]).then_inc(n.done["hi"], 1)
            else:
                dve.wait_ge(n.done["hi"], 1)
                nc.vector.tensor_tensor(n.lo[:].rearrange("p f t -> p (f t)"), banks[n.bank][:],
                                        n.hi[:].bitcast(F32).rearrange("p f t -> p (f t)"),
                                        ALU.subtract).then_inc(n.done["lo"], 1)

        def dve_gate_up(dve, f, p):
            g, u = f.banks[p % len(f.banks)]
            a = f.act[:, p % 2].rearrange("p i t -> p (i t)")
            dve.wait_ge(f.done["tanh"], p + 1)
            nc.vector.scalar_tensor_tensor(a, a, 1.0, banks[g][:], ALU.add, ALU.mult).then_inc(f.done["gated"], 1)
            dve.wait_ge(f.done["gated"], p + 1)
            if f.hid_scale is None:
                nc.vector.scalar_tensor_tensor(a, a, 0.5, banks[u][:], ALU.mult, ALU.mult).then_inc(f.done["hid"], 1)
            else:
                for i in range(2):
                    j = 2 * p + i
                    last = nc.vector.scalar_tensor_tensor(f.act[:, p % 2, i, :], f.act[:, p % 2, i, :],
                                                          f.hid_scale[:, j:j + 1], banks[u][:, i * T:(i + 1) * T],
                                                          ALU.mult, ALU.mult)
                last.then_inc(f.done["hid"], 1)

        def dve_ffn_end(dve, f):
            dve.wait_ge(f.done["down"], PAIRS)
            y = banks[f.ybank][:].rearrange("p (t d) -> p t d", t=TT)
            if f.hid_scale is None:
                dve.wait_ge(xz_added, 1)
                nc.vector.tensor_tensor(f.out[:], f.res[:], y, ALU.add).then_inc(f.done["added"], 1)
            else:
                tmp = f.norm.nrm
                nc.vector.tensor_tensor(tmp[:], y, sdrow[:].unsqueeze(1).to_broadcast([P, TT, D]),
                                        ALU.mult).then_inc(f.done["scaled"], 1)
                dve.wait_ge(f.done["scaled"], 1)
                nc.vector.tensor_tensor(f.out[:], f.res[:], tmp[:], ALU.add).then_inc(f.done["added"], 1)

        def dve_queries_keys(dve):
            dve.wait_ge(q_rounded, 2)
            table = const("qdecay").rearrange("p (f s) -> p f s", f=FT).unsqueeze(2).to_broadcast([P, FT, TT, P])
            nc.vector.tensor_tensor(qTd[:].rearrange("p f (t s) -> p f t s", t=TT),
                                    banks[1][:].rearrange("p (f t s) -> p f t s", f=FT, t=TT), table,
                                    ALU.mult).then_inc(q_decayed, 1)
            for par, name in enumerate(("even", "odd")):
                nc.vector.scalar_tensor_tensor(q_lo[:, :, :, par, :],
                                               banks[1][:].rearrange("p (f t s) -> p f t s", f=FT, t=TT), const(name),
                                               q_hi[:, :, :, par, :].bitcast(F32), ALU.mult,
                                               ALU.subtract).then_inc(q_parted, 1)
            dve.wait_ge(k_rounded, 1)
            nc.vector.tensor_tensor(k_lo[:].rearrange("p f t -> p (f t)"), banks[2][:],
                                    k_hi[:].bitcast(F32).rearrange("p f t -> p (f t)"), ALU.subtract).then_inc(k_parted, 1)

        def dve_keys_values(dve, tt):
            dve.wait_ge(v_copied, tt + 1)
            nc.vector.tensor_tensor(kdec[:, tt, :], banks[3 + tt][:, 0:D], const("kdecay"),
                                    ALU.mult).then_inc(k_decayed, 1)

        def dve_gates(dve):
            dve.wait_ge(g_tanh, 1)
            nc.vector.scalar_tensor_tensor(gated[:].rearrange("p t d -> p (t d)"), gated[:].rearrange("p t d -> p (t d)"),
                                           1.0, banks[0][:], ALU.add, ALU.mult).then_inc(g_gated, 1)

        def dve_outer(dve):
            mask = const("headmask").unsqueeze(1).to_broadcast([P, TT * FT, P])
            dve.wait_ge(outer_made, 1)
            nc.vector.tensor_tensor(kvmask[:].rearrange("p t f e -> p (t f) e"),
                                    banks[1][:].rearrange("p (g e) -> p g e", e=P), mask,
                                    ALU.mult).then_inc(outer_masked, 1)
            dve.wait_ge(outer_masked, 1)
            dve_carry(dve, 0)

        def dve_carry(dve, c):
            if c == TT - 1:
                dve.wait_ge(probs_used, 1)
                dve.wait_ge(state_ready, c)
            for f in range(FT):
                last = nc.vector.scalar_tensor_tensor(retain[:, (c + 1) % TT, f, :], retain[:, c, f, :],
                                                      const("chunkdecay")[:, f:f + 1], kvmask[:, c, f, :],
                                                      ALU.mult, ALU.add)
            last.then_inc(state_ready, 1)

        def dve_score(dve, u):
            f, rg = u // 4, u % 4
            dve.wait_ge(scores_made, u + 1)
            if u >= 3:
                dve.wait_ge(probs_used, u - 2)
            h = f * 8 + rg * 2
            table = cst[:, h * P:(h + 2) * P].rearrange("p (h s) -> p h s", h=2)
            src = banks[(2, 4, 0)[u % 3]][:].rearrange("p (c h s) -> p c h s", c=TT, h=2)
            dst = probs[:, u % 3, :].rearrange("p (c h s) -> p c h s", c=TT, h=2)
            nc.vector.tensor_tensor(dst, src, table.unsqueeze(1).to_broadcast([P, TT, 2, P]),
                                    ALU.mult).then_inc(probs_made, 1)
            if u == 4:
                dve_carry(dve, TT - 1)

        def dve_group_gate(dve):
            dve.wait_ge(ret_squared, 1)
            nc.vector.scalar_tensor_tensor(gated[:].rearrange("p t d -> p (t d)"), gated[:].rearrange("p t d -> p (t d)"),
                                           0.5, banks[3][:], ALU.mult, ALU.mult).then_inc(g_scaled, 1)
            nc.vector.tensor_reduce(rvar[:], squares[:].rearrange("p t (h e) -> p (t h) e", e=DH),
                                    AX_X, ALU.add).then_inc(ret_var, 1)
            dve.wait_ge(ret_var, 1)
            nc.vector.tensor_scalar(rvar[:], rvar[:], 1.0 / DH, EPS, ALU.mult, ALU.add).then_inc(ret_var, 1)
            dve.wait_ge(ret_var, 2)
            nc.vector.tensor_scalar(rstd[:].bitcast(I32), rvar[:].bitcast(I32), 1, None,
                                    ALU.logical_shift_right).then_inc(ret_root, 1)
            dve.wait_ge(ret_root, 1)
            nc.vector.tensor_scalar(rstd[:].bitcast(I32), rstd[:].bitcast(I32), -1.0, float(0x5F3759DF), ALU.mult,
                                    ALU.add).then_inc(ret_root, 1)
            for step in range(NEWTON):
                dve.wait_ge(ret_root, 3 * step + 2)
                nc.vector.tensor_tensor(rscr[:], rstd[:], rstd[:], ALU.mult).then_inc(ret_root, 1)
                dve.wait_ge(ret_root, 3 * step + 3)
                nc.vector.scalar_tensor_tensor(rscr[:], rscr[:], -0.5, rvar[:], ALU.mult,
                                               ALU.mult).then_inc(ret_root, 1)
                dve.wait_ge(ret_root, 3 * step + 4)
                nc.vector.scalar_tensor_tensor(rstd[:], rscr[:], 1.5, rstd[:], ALU.add,
                                               ALU.mult).then_inc(ret_root, 1)

        def dve_group_scale(dve):
            dve.wait_ge(g_scaled, 1)
            dve.wait_ge(ret_root, 3 * NEWTON + 2)
            gat = gated[:].rearrange("p t (h e) -> p (t h) e", e=DH)
            nc.vector.tensor_tensor(gat, gat, rstd[:].unsqueeze(2).to_broadcast([P, TT * HEADS, DH]),
                                    ALU.mult).then_inc(ret_gated, 1)

        def dve_ret_split(dve):
            dve.wait_ge(yt_hi, 1)
            nc.vector.tensor_tensor(hT[2][:].rearrange("p f t -> p (f t)"), banks[1][:],
                                    hT[1][:].bitcast(F32).rearrange("p f t -> p (f t)"), ALU.subtract).then_inc(yt_lo, 1)

        def dve_project(dve):
            dve.wait_ge(n1.done["plain"], TT)
            dve.wait_ge(y_projected, 1)
            nc.vector.tensor_tensor(xn[:], xn[:], banks[3][:].rearrange("p (t d) -> p t d", t=TT),
                                    ALU.add).then_inc(z_added, 1)

        def dve_state_inputs(dve):
            dve.wait_ge(drh_made, 1)
            dve.wait_ge(bc_copied, 1)
            nc.vector.tensor_tensor(dr_lo[:], banks[6][:, 0:T], dr_hi[:].bitcast(F32), ALU.subtract).then_inc(drl_made, 1)
            for part in range(3):
                here = bc_parts[32 * part:32 * part + 32, :]
                nc.vector.tensor_copy(here, bc_full[:, part % 2, :]).then_inc(bc_part, 1)
                if part < 2:
                    dve.wait_ge(bc_part, 2 * part + 1)
                    nc.vector.tensor_tensor(bc_full[:, (part + 1) % 2, :], bc_full[:, part, :], here,
                                            ALU.subtract).then_inc(bc_part, 1)
                    dve.wait_ge(bc_part, 2 * part + 2)

        def dve_steps_size(dve):
            dve.wait_ge(dt_abs, FT)
            for ft in range(FT):
                last = nc.vector.tensor_scalar(du[:, ft, :], banks[7][:, ft * T:(ft + 1) * T], column("dtb", ft), 0.0,
                                               ALU.add, ALU.max)
            last.then_inc(dt_pos, 1)

        def dve_steps_end(dve):
            dve.wait_ge(dt_pos, 1)
            dve.wait_ge(dt_ln, 1)
            nc.vector.tensor_tensor(delta[:], delta[:], du[:], ALU.add).then_inc(delta_made, 1)
            dve.wait_ge(delta_made, 1)
            nc.vector.tensor_tensor(du[:], delta[:], n4.full[:], ALU.mult).then_inc(du_made, 1)

        def dve_spread(dve, sp):
            if sp == 0:
                dve.wait_ge(du_made, 1)
            dve.wait_ge(rep_copied, 2 * sp + 2)
            if sp >= 3:
                dve.wait_ge(y_added, sp - 2)
            nc.vector.tensor_tensor(hbuf[:, sp % 3], du[:].unsqueeze(1).to_broadcast([P, 2, FT, T]),
                                    rep[:, sp % 2, :, 0, :].unsqueeze(2).to_broadcast([P, 2, FT, T]),
                                    ALU.mult).then_inc(dbu_made, 1)

        def dve_scan(dve, sp):
            dve.wait_ge(dbu_made, sp + 1)
            for i in range(2):
                for ft in range(FT):
                    n = 2 * sp + i
                    dve.wait_ge(decay_made, 4 * sp + 2 * i + ft + 1)
                    h = hbuf[:, sp % 3, i, ft, :]
                    nc.vector.tensor_tensor_scan(h, dA[:, sp % 2, i, ft, :], h, hstate[:, n, ft:ft + 1],
                                                 ALU.mult, ALU.add).then_inc(scanned, 1)

        def dve_scan_skip(dve):
            for ft in range(FT):
                last = nc.vector.tensor_scalar(yscan[:, ft, :], n4.full[:, ft, :], column("dskip", ft), None, ALU.mult)
            last.then_inc(y_skipped, 1)

        def dve_collect(dve, sp):
            dve.wait_ge(pair_summed, sp + 1)
            if sp == 0:
                dve.wait_ge(y_skipped, 1)
            else:
                dve.wait_ge(y_added, sp)
            nc.vector.tensor_tensor(yscan[:], yscan[:], hbuf[:, sp % 3, 0], ALU.add).then_inc(y_added, 1)

        def dve_scan_back(dve):
            dve.wait_ge(y_back, 1)
            dve.wait_ge(x_taken, 1)
            nc.vector.tensor_tensor(xback[:], xback[:], banks[5][:].rearrange("p (t d) -> p t d", t=TT),
                                    ALU.add).then_inc(x3_added, 1)

        def pool_wide_spread(pool):
            pool.wait_ge(wide_seen, 8)
            nc.gpsimd.partition_all_reduce(wide_all[:], wide_any[:], P, RMAX).then_inc(wide_everywhere, 1)

        def pool_norm_stats(pool, n):
            pool.wait_ge(n.done["var"], 2 if n.twice is not None else 1)
            nc.gpsimd.tensor_tensor(n.rstd[:], n.var[:], const("half")[:, 0:n.var.shape[1]],
                                    ALU.pow).then_inc(n.done["rstd"], 1)

        def pool_norm_split(pool, n):
            if not n.keep:
                return
            pool.wait_ge(n.done["hi"], 1)
            nc.gpsimd.tensor_tensor(n.lo[:], n.full[:], n.hi[:].bitcast(F32), ALU.subtract).then_inc(n.done["lo"], 1)

        def pool_split(pool, f, p):
            pool.wait_ge(f.done["hi"], p + 1)
            nc.gpsimd.tensor_tensor(f.lo[:, p % 2], f.act[:, p % 2], f.hi[:, p % 2].bitcast(F32),
                                    ALU.subtract).then_inc(f.done["lo"], 1)

        def pool_residual(pool):
            pool.wait_ge(z_added, 1)
            pool.wait_ge(n1.done["plain"], TT)
            if with_back:
                pool.wait_ge(x_taken, 1)
                pool.wait_ge(n4.done["normed"], TT)
            nc.gpsimd.tensor_tensor(xres[:], xin[:], xn[:], ALU.add).then_inc(xz_added, 1)

        def pool_collect(pool, sp):
            pool.wait_ge(scanned, 4 * (sp + 1))
            h = hbuf[:, sp % 3]
            nc.gpsimd.tensor_copy(hstate[:, 2 * sp:2 * sp + 2, :], h[:, :, :, T - 1]).then_inc(saved, 1)
            pool.wait_ge(saved, sp + 1)
            pool.wait_ge(rep_copied, 2 * sp + 2)
            nc.gpsimd.tensor_tensor(h, h, rep[:, sp % 2, :, 1, :].unsqueeze(2).to_broadcast([P, 2, FT, T]),
                                    ALU.mult).then_inc(outs_made, 1)
            pool.wait_ge(outs_made, sp + 1)
            nc.gpsimd.tensor_tensor(h[:, 0], h[:, 0], h[:, 1], ALU.add).then_inc(pair_summed, 1)


        def finish():
            numbers = [s.num for s in sems]
            assert numbers == list(range(numbers[0], numbers[0] + len(numbers)))
            nc.sync.sem_clear(range(numbers[0], numbers[0] + len(numbers)))
            nc.all_engine_barrier()

        with_back = False
        with nc.Block() as block:
            @block.sync
            def _(sp):
                sp.dma_start(xin[:], x_view[0]).then_inc(x_in, 16)
                small = slice(CONSTS["decay"][1], NCONST)
                sp.dma_start(cst[:, small], consts[:, small]).then_inc(small_loaded, 16)
                sp.dma_start(col[:], cols).then_inc(small_loaded, 16)
                sp.dma_start(sdrow[:], s_down.partition_broadcast(P)).then_inc(small_loaded, 16)
                for n, piece_ in enumerate(pieces):
                    if n == FT:
                        sp.dma_start(cst[:, :small.start], consts[:, :small.start]).then_inc(decay_loaded, 16)
                    sp.dma_start(piece_["raw"], piece_["source"]).then_inc(piece_["loaded"], 16)
                sp.wait_ge(xz_added, 1)
                sp.dma_start(xin[:], x_view[1]).then_inc(x_next, 16)
                sp.wait_ge(x_next, 16)

            @block.tensor
            def _(pe):
                pe.wait_ge(small_loaded, 48)
                pe_norm_turn(pe, n1)
                pe_need(pe, 2)
                pe_queries_keys(pe)
                pe_keys_values(pe, 0)
                pe_keys_values(pe, 1)
                pe_gates(pe)
                pe_outer(pe)
                pe_first_scores(pe, 0)
                pe_first_scores(pe, 1)
                for i in range(8):
                    pe_value(pe, i)
                pe_ret_turn(pe)
                pe_need(pe, 3)
                pe_project(pe)
                pe_norm_turn(pe, n2)
                pe_need(pe, 5)
                pe_gate_up(pe, f1, 0, True)
                pe_gate_up(pe, f1, 1, True)
                pe_need(pe, 6)
                pe_down(pe, f1, 0, True)
                pe_gate_up(pe, f1, 2, True)
                pe_down(pe, f1, 1, True)
                pe_down(pe, f1, 2, True)
                pe_norm_turn(pe, n3)
                pe_need(pe, 8)
                pe_gate_up(pe, f2, 0, True)
                pe_gate_up(pe, f2, 1, True)
                pe_need(pe, 9)
                pe_down(pe, f2, 0, True)
                pe_gate_up(pe, f2, 2, True)
                pe_down(pe, f2, 1, True)
                pe_down(pe, f2, 2, True)

            @block.scalar
            def _(act):
                act.wait_ge(small_loaded, 48)
                act_weights(act, 0)
                act_weights(act, 1)
                act_norm_turn(act, n1)
                act_consts(act)
                act_queries_keys(act)
                act_keys_values(act, 0)
                act_keys_values(act, 1)
                act_gates(act)
                for i in range(2, 6):
                    act_weights(act, i)
                act_group_norm(act)
                act_ret_turn(act)
                act_tables(act)
                act_norm_turn(act, n2)
                act_weights(act, 6)
                act_gate_up(act, f1, 0)
                act_weights(act, 7)
                act_gate_up(act, f1, 1)
                act_weights(act, 8)
                act_split(act, f1, 0)
                act_split(act, f1, 1)
                act_gate_up(act, f1, 2)
                act_weights(act, 9)
                act_split(act, f1, 2)
                act_norm_turn(act, n3)
                act_gate_up(act, f2, 0)
                act_weights(act, 10)
                act_gate_up(act, f2, 1)
                act_split(act, f2, 0)
                act_split(act, f2, 1)
                act_gate_up(act, f2, 2)
                act_split(act, f2, 2)

            @block.vector
            def _(dve):
                dve.wait_ge(x_in, 16)
                dve_norm_stats(dve, n1)
                dve_clear(dve)
                dve_prepare(dve, 0)
                dve_prepare(dve, 1)
                dve_norm_apply(dve, n1)
                dve_weights(dve, 0)
                dve_weights(dve, 1)
                dve_norm_split(dve, n1)
                dve_consts(dve)
                dve_queries_keys(dve)
                dve_keys_values(dve, 0)
                dve_keys_values(dve, 1)
                dve_gates(dve)
                dve_outer(dve)
                dve_score(dve, 0)
                dve_score(dve, 1)
                dve_weights(dve, 2)
                dve_score(dve, 2)
                dve_score(dve, 3)
                dve_weights(dve, 3)
                dve_score(dve, 4)
                dve_score(dve, 5)
                dve_weights(dve, 4)
                dve_score(dve, 6)
                dve_score(dve, 7)
                dve_weights(dve, 5)
                dve_prepare(dve, 6)
                dve_group_gate(dve)
                dve_group_scale(dve)
                dve_ret_split(dve)
                dve_project(dve)
                dve_tables(dve)
                dve_norm_stats(dve, n2)
                dve_prepare(dve, 7)
                dve_norm_apply(dve, n2)
                dve_norm_split(dve, n2)
                dve_weights(dve, 6)
                dve_prepare(dve, 8)
                dve_gate_up(dve, f1, 0)
                dve_weights(dve, 7)
                dve_wide(dve, 0)
                dve_gate_up(dve, f1, 1)
                dve_weights(dve, 8)
                dve_wide(dve, 1)
                dve_wide(dve, 2)
                dve_gate_up(dve, f1, 2)
                dve_weights(dve, 9)
                dve_wide_spread(dve)
                dve_ffn_end(dve, f1)
                dve_norm_stats(dve, n3)
                dve_norm_apply(dve, n3)
                dve_norm_split(dve, n3)
                dve_gate_up(dve, f2, 0)
                dve_weights(dve, 10)
                dve_gate_up(dve, f2, 1)
                dve_gate_up(dve, f2, 2)
                dve_ffn_end(dve, f2)
                dve_wide_end(dve)

            @block.gpsimd
            def _(pool):
                pool.wait_ge(small_loaded, 48)
                pool_norm_stats(pool, n1)
                pool_norm_split(pool, n1)
                pool_norm_stats(pool, n2)
                pool_residual(pool)
                pool_norm_split(pool, n2)
                pool_split(pool, f1, 0)
                pool_split(pool, f1, 1)
                pool_wide_spread(pool)
                pool_split(pool, f1, 2)
                pool_norm_stats(pool, n3)
                pool_norm_split(pool, n3)
                for i in range(3):
                    pool_split(pool, f2, i)

        finish()

        with_back = True
        with nc.Fori(0, CHUNKS - 1) as chunk:
            with nc.Block() as block:
                @block.sync
                def _(sp):
                    sp.wait_ge(xz_added, 1)
                    sp.dma_start(xin[:], x_view[chunk + 2]).then_inc(x_next, 16)
                    sp.wait_ge(f3.done["added"], 1)
                    sp.dma_start(out_view[chunk], xback[:]).then_inc(x_out, 16)
                    sp.wait_ge(x_out, 16)
                    sp.wait_ge(x_next, 16)

                @block.tensor
                def _(pe):
                    def steps(low):
                        pe_norm_turn(pe, n4)
                        pe_norm_turn(pe, n1)
                        pe_state_inputs(pe)
                        pe_queries_keys(pe)
                        pe_keys_values(pe, 0)
                        pe_keys_values(pe, 1)
                        pe_gates(pe)
                        pe_steps_size(pe)
                        pe_spread(pe, 0)
                        pe_outer(pe)
                        pe_first_scores(pe, 0)
                        pe_first_scores(pe, 1)
                        pe_value(pe, 0)
                        pe_spread(pe, 1)
                        pe_value(pe, 1)
                        pe_spread(pe, 2)
                        pe_value(pe, 2)
                        pe_value(pe, 3)
                        pe_spread(pe, 3)
                        pe_value(pe, 4)
                        pe_spread(pe, 4)
                        for i in range(5, 8):
                            pe_value(pe, i)
                        pe_spread(pe, 5)
                        pe_spread(pe, 6)
                        pe_ret_turn(pe)
                        pe_project(pe)
                        pe_spread(pe, 7)
                        pe_norm_turn(pe, n2)
                        pe_gate_up(pe, f1, 0, True)
                        pe_gate_up(pe, f1, 1, True)
                        pe_scan_back(pe)
                        pe_down(pe, f1, 0, True)
                        pe_norm_turn(pe, n5)
                        pe_gate_up(pe, f1, 2, True)
                        pe_down(pe, f1, 1, True)
                        pe_gate_up(pe, f3, 0, low)
                        pe_down(pe, f1, 2, True)
                        pe_gate_up(pe, f3, 1, low)
                        pe_norm_turn(pe, n3)
                        pe_down(pe, f3, 0, low)
                        pe_gate_up(pe, f2, 0, low)
                        pe_gate_up(pe, f2, 1, low)
                        pe_gate_up(pe, f3, 2, low)
                        pe_down(pe, f3, 1, low)
                        pe_down(pe, f2, 0, low)
                        pe_gate_up(pe, f2, 2, low)
                        pe_down(pe, f3, 2, low)
                        pe_down(pe, f2, 1, low)
                        pe_down(pe, f2, 2, low)

                    wide = pe.value_load(wide_flag[0:1, 0:1], min_val=0, max_val=1)
                    with pe.If(wide > 0):
                        steps(True)
                    with pe.Else():
                        steps(False)

                @block.scalar
                def _(act):
                    act_take(act)
                    act_norm_turn(act, n4)
                    act_norm_turn(act, n1)
                    act_queries_keys(act)
                    act_keys_values(act, 0)
                    act_state_inputs(act)
                    act_keys_values(act, 1)
                    act_gates(act)
                    act_steps_size(act)
                    for i in range(5):
                        act_spread(act, i)
                    act_group_norm(act)
                    act_spread(act, 5)
                    act_spread(act, 6)
                    act_ret_turn(act)
                    act_norm_turn(act, n2)
                    act_spread(act, 7)
                    act_gate_up(act, f1, 0)
                    act_gate_up(act, f1, 1)
                    act_split(act, f1, 0)
                    act_split(act, f1, 1)
                    act_norm_turn(act, n5)
                    act_gate_up(act, f1, 2)
                    act_split(act, f1, 2)
                    act_gate_up(act, f3, 0)
                    act_gate_up(act, f3, 1)
                    act_split(act, f3, 0)
                    act_norm_turn(act, n3)
                    act_gate_up(act, f2, 0)
                    act_split(act, f3, 1)
                    act_gate_up(act, f2, 1)
                    act_split(act, f2, 0)
                    act_gate_up(act, f3, 2)
                    act_split(act, f2, 1)
                    act_split(act, f3, 2)
                    act_gate_up(act, f2, 2)
                    act_split(act, f2, 2)

                @block.vector
                def _(dve):
                    dve_norm_stats(dve, n4)
                    dve_norm_apply(dve, n4)
                    dve_norm_stats(dve, n1)
                    dve_norm_split(dve, n4)
                    dve_norm_apply(dve, n1)
                    dve_norm_split(dve, n1)
                    dve_queries_keys(dve)
                    dve_keys_values(dve, 0)
                    dve_state_inputs(dve)
                    dve_keys_values(dve, 1)
                    dve_gates(dve)
                    dve_steps_size(dve)
                    dve_outer(dve)
                    dve_score(dve, 0)
                    dve_score(dve, 1)
                    dve_steps_end(dve)
                    dve_scan_skip(dve)
                    dve_spread(dve, 0)
                    dve_score(dve, 2)
                    dve_scan(dve, 0)
                    dve_score(dve, 3)
                    dve_spread(dve, 1)
                    dve_score(dve, 4)
                    dve_scan(dve, 1)
                    dve_collect(dve, 0)
                    dve_spread(dve, 2)
                    dve_scan(dve, 2)
                    dve_score(dve, 5)
                    dve_collect(dve, 1)
                    dve_spread(dve, 3)
                    dve_score(dve, 6)
                    dve_scan(dve, 3)
                    dve_collect(dve, 2)
                    dve_score(dve, 7)
                    dve_spread(dve, 4)
                    dve_scan(dve, 4)
                    dve_group_gate(dve)
                    dve_group_scale(dve)
                    dve_collect(dve, 3)
                    dve_spread(dve, 5)
                    dve_ret_split(dve)
                    dve_scan(dve, 5)
                    dve_collect(dve, 4)
                    dve_project(dve)
                    dve_norm_stats(dve, n2)
                    dve_spread(dve, 6)
                    dve_norm_apply(dve, n2)
                    dve_norm_split(dve, n2)
                    dve_scan(dve, 6)
                    dve_collect(dve, 5)
                    dve_spread(dve, 7)
                    dve_scan(dve, 7)
                    dve_collect(dve, 6)
                    dve_gate_up(dve, f1, 0)
                    dve_collect(dve, 7)
                    dve_scan_back(dve)
                    dve_norm_stats(dve, n5)
                    dve_norm_apply(dve, n5)
                    dve_gate_up(dve, f1, 1)
                    dve_norm_split(dve, n5)
                    dve_gate_up(dve, f1, 2)
                    dve_gate_up(dve, f3, 0)
                    dve_ffn_end(dve, f1)
                    dve_norm_stats(dve, n3)
                    dve_norm_apply(dve, n3)
                    dve_norm_split(dve, n3)
                    dve_gate_up(dve, f3, 1)
                    dve_gate_up(dve, f2, 0)
                    dve_gate_up(dve, f2, 1)
                    dve_gate_up(dve, f3, 2)
                    dve_gate_up(dve, f2, 2)
                    dve_ffn_end(dve, f3)
                    dve_ffn_end(dve, f2)

                @block.gpsimd
                def _(pool):
                    pool_norm_stats(pool, n4)
                    pool_norm_stats(pool, n1)
                    pool_norm_split(pool, n4)
                    pool_norm_split(pool, n1)
                    for i in range(6):
                        pool_collect(pool, i)
                    pool_norm_stats(pool, n2)
                    pool_residual(pool)
                    pool_norm_split(pool, n2)
                    pool_collect(pool, 6)
                    pool_collect(pool, 7)
                    pool_split(pool, f1, 0)
                    pool_norm_stats(pool, n5)
                    pool_norm_split(pool, n5)
                    pool_split(pool, f1, 1)
                    pool_split(pool, f1, 2)
                    pool_norm_stats(pool, n3)
                    pool_norm_split(pool, n3)
                    pool_split(pool, f3, 0)
                    pool_split(pool, f3, 1)
                    pool_split(pool, f2, 0)
                    pool_split(pool, f3, 2)
                    pool_split(pool, f2, 1)
                    pool_split(pool, f2, 2)

            finish()

        with nc.Block() as block:
            @block.sync
            def _(sp):
                sp.wait_ge(f3.done["added"], 1)
                sp.dma_start(out_view[CHUNKS - 1], xback[:]).then_inc(x_out, 16)
                sp.wait_ge(x_out, 16)

            @block.tensor
            def _(pe):
                def steps(low):
                    pe_norm_turn(pe, n4)
                    pe_state_inputs(pe)
                    pe_steps_size(pe)
                    for i in range(8):
                        pe_spread(pe, i)
                    pe_scan_back(pe)
                    pe_norm_turn(pe, n5)
                    pe_gate_up(pe, f3, 0, low)
                    pe_gate_up(pe, f3, 1, low)
                    pe_down(pe, f3, 0, low)
                    pe_gate_up(pe, f3, 2, low)
                    pe_down(pe, f3, 1, low)
                    pe_down(pe, f3, 2, low)

                wide = pe.value_load(wide_flag[0:1, 0:1], min_val=0, max_val=1)
                with pe.If(wide > 0):
                    steps(True)
                with pe.Else():
                    steps(False)

            @block.scalar
            def _(act):
                act_take(act)
                act_norm_turn(act, n4)
                act_state_inputs(act)
                act_steps_size(act)
                for i in range(8):
                    act_spread(act, i)
                act_norm_turn(act, n5)
                act_gate_up(act, f3, 0)
                act_gate_up(act, f3, 1)
                act_split(act, f3, 0)
                act_split(act, f3, 1)
                act_gate_up(act, f3, 2)
                act_split(act, f3, 2)

            @block.vector
            def _(dve):
                dve_norm_stats(dve, n4)
                dve_norm_apply(dve, n4)
                dve_norm_split(dve, n4)
                dve_state_inputs(dve)
                dve_steps_size(dve)
                dve_steps_end(dve)
                dve_scan_skip(dve)
                dve_spread(dve, 0)
                dve_scan(dve, 0)
                dve_spread(dve, 1)
                dve_scan(dve, 1)
                dve_collect(dve, 0)
                dve_spread(dve, 2)
                dve_scan(dve, 2)
                dve_collect(dve, 1)
                dve_spread(dve, 3)
                dve_scan(dve, 3)
                dve_collect(dve, 2)
                dve_spread(dve, 4)
                dve_scan(dve, 4)
                dve_collect(dve, 3)
                dve_spread(dve, 5)
                dve_scan(dve, 5)
                dve_collect(dve, 4)
                dve_spread(dve, 6)
                dve_scan(dve, 6)
                dve_collect(dve, 5)
                dve_spread(dve, 7)
                dve_scan(dve, 7)
                dve_collect(dve, 6)
                dve_collect(dve, 7)
                dve_scan_back(dve)
                dve_norm_stats(dve, n5)
                dve_norm_apply(dve, n5)
                dve_norm_split(dve, n5)
                for i in range(3):
                    dve_gate_up(dve, f3, i)
                dve_ffn_end(dve, f3)

            @block.gpsimd
            def _(pool):
                pool_norm_stats(pool, n4)
                pool_norm_split(pool, n4)
                for i in range(8):
                    pool_collect(pool, i)
                pool_norm_stats(pool, n5)
                pool_norm_split(pool, n5)
                for i in range(3):
                    pool_split(pool, f3, i)


def host_layout(i):
    def pad_cols(a, n):
        return np.concatenate([a, np.zeros((a.shape[0], n - a.shape[1]), a.dtype)], axis=1)

    def pad_rows(a, n):
        return np.concatenate([a, np.zeros((n - a.shape[0],) + a.shape[1:], a.dtype)], axis=0)

    def per_feature(v, tiles):
        return pad_rows(v, tiles * P).reshape(tiles, P).T

    a = {k: np.asarray(v) for k, v in i.items()}
    A, B, F = "L0_attn_a_", "L0_attn_b_", "L0_ffn_"
    cols = np.concatenate([
        per_feature(a[A + "norm1_w"], FT), per_feature(a[A + "norm1_b"], FT),
        per_feature(a[A + "norm2_w"], FT), per_feature(a[A + "norm2_b"], FT),
        per_feature(a[B + "D"], FT), per_feature(a[B + "dt_proj_b"], FT),
        per_feature(a[F + "s_gate"], HT), per_feature(a[F + "s_up"], HT),
        a[B + "A_log"].reshape(FT, P, NS).transpose(1, 0, 2).reshape(P, FT * NS)], axis=1)
    return {
        "x": pad_rows(a[A + "x"].reshape(S, D), S + T),
        "w_qkvg": np.concatenate([a[A + "wq"], a[A + "wk"], a[A + "wv"], a[A + "wg"]], axis=1),
        "w_o": a[A + "wo"],
        "w_12": np.concatenate([pad_cols(a[A + "w1"], HP), pad_cols(a[A + "w2"], HP)], axis=1),
        "w_3": pad_rows(a[A + "w3"], HP),
        "w_gu": np.concatenate([pad_cols(a[F + "wq_gate"].T, HP), pad_cols(a[F + "wq_up"].T, HP)], axis=1),
        "w_dn": pad_rows(a[F + "wq_down"].T, HP),
        "w_xp": pad_cols(a[B + "x_proj_w"].T, XPW),
        "w_dt": a[B + "dt_proj_w"].T,
        "cols": cols,
        "s_down": a[F + "s_down"].reshape(D),
        "consts": shape_constants(),
    }


def kernel(**inputs):
    import concourse.bacc as bacc
    from concourse.bass_utils import run_bass_kernel_spmd

    nc = bacc.Bacc("TRN2", target_bir_lowering=False, num_devices=1)
    arrays, args = {}, []
    for name, a in host_layout(inputs).items():
        a = np.ascontiguousarray(a)
        arrays[name + "_dram"] = a
        args.append(nc.dram_tensor(name + "_dram", a.shape, mybir.dt.from_np(a.dtype), kind="ExternalInput").ap())
    args.append(nc.dram_tensor("out_dram", (S, D), F32, kind="ExternalOutput").ap())
    program(nc, *args)
    r = run_bass_kernel_spmd(nc, [arrays], core_ids=[0])
    return r.results[0]["out_dram"].reshape(1, S, D)
```
